# Optimizing a Trainium2 kernel written in Bass

```python
import numpy as np
import jax
import jax.numpy as jnp

def _softmax(x, axis=-1):
    return jax.nn.softmax(x, axis=axis)

def _gelu(x):
    return jax.nn.gelu(x, approximate=True)

def _silu(x):
    return jax.nn.silu(x)

def _sigmoid(x):
    return jax.nn.sigmoid(x)

def _layernorm(x, axis=-1, eps=1e-05):
    m = jnp.mean(x, axis=axis, keepdims=True)
    v = jnp.var(x, axis=axis, keepdims=True)
    return (x - m) / jnp.sqrt(v + eps)

def _scatter_add(tgt, idx, src, axis=0):
    return tgt.at[idx].add(src)

def _segment_sum(src, seg, n):
    return jax.ops.segment_sum(src, seg, n)
kernel_name = 'mk_hybrid_d1_jaxref_r4_eaad6e'

def setup_inputs(seed: int=0):
    np.random.seed(seed)
    _w = jnp.asarray

    def _L0_attn_a_setup():
        import jax, jax.numpy as jnp
        import numpy as np
        B, L, D, N = (2, 512, 256, 16)
        DT = 0.1
        key = jax.random.key(seed)
        ks = jax.random.split(key, 10)

        def w(k, shape, scale=0.02):
            return jax.random.normal(k, shape, jnp.float32) * scale
        log_min, log_max = (float(np.log(0.001)), float(np.log(0.1)))
        dt_bias = jax.random.uniform(ks[1], (D,), jnp.float32) * (log_max - log_min) + log_min
        return {'x': jax.random.normal(ks[0], (B, L, D), jnp.float32), 'delta_W': w(ks[2], (D, D)), 'delta_b': jnp.zeros((D,), jnp.float32), 'B_W': w(ks[3], (N, D)), 'B_b': jnp.zeros((N,), jnp.float32), 'C_W': w(ks[4], (N, D)), 'C_b': jnp.zeros((N,), jnp.float32), 'A_log': jnp.zeros((D, N), jnp.float32), 'dt_bias': dt_bias, 'tau': jnp.ones((N,), jnp.float32), 'Wi_W': w(ks[5], (N, D)), 'Wi_b': jnp.zeros((N,), jnp.float32), 'Wr_W': w(ks[6], (N, N)), 'sel_W': w(ks[7], (D, N)), 'sel_b': jnp.zeros((D,), jnp.float32), 'h0': jnp.zeros((1, N), jnp.float32)}
    _L0_attn_a_in = _L0_attn_a_setup()

    def _L0_attn_b_setup():
        import jax, jax.numpy as jnp
        import numpy as np
        B, N, D, H = (4, 1024, 256, 16)
        HD = D // H
        EPS_NORM = 1e-12
        EPS_LN = 1e-05

        def _silu(x):
            return x * jax.nn.sigmoid(x)

        def _simple_gla(q, k, v, f):
            qT = jnp.moveaxis(q, 1, 0)
            kT = jnp.moveaxis(k, 1, 0)
            vT = jnp.moveaxis(v, 1, 0)
            fT = jnp.moveaxis(f, 1, 0)

            def step(S, inp):
                qt, kt, vt, ft = inp
                S = jnp.exp(ft)[..., None, None] * S + kt[..., :, None] * vt[..., None, :]
                o = jnp.einsum('bhk,bhkv->bhv', qt, S)
                return (S, o)
            S0 = jnp.zeros((q.shape[0], q.shape[2], q.shape[3], v.shape[3]), q.dtype)
            _, o = jax.lax.scan(step, S0, (qT, kT, vT, fT))
            return jnp.moveaxis(o, 0, 1)
        key = jax.random.key(seed)
        ks = jax.random.split(key, 9)
        s = 0.02
        return {'x': jax.random.normal(ks[0], (B, N, D), jnp.float32), 'Wq': jax.random.normal(ks[1], (D, D), jnp.float32) * s, 'Wk': jax.random.normal(ks[2], (D, D), jnp.float32) * s, 'Wv': jax.random.normal(ks[3], (D, D), jnp.float32) * s, 'Wf': jax.random.normal(ks[4], (H, D), jnp.float32) * s, 'Wg1': jax.random.normal(ks[5], (HD, D), jnp.float32) * s, 'Wg2': jax.random.normal(ks[6], (D, HD), jnp.float32) * s, 'ln_w': jnp.ones((D,), jnp.float32), 'Wo': jax.random.normal(ks[7], (D, D), jnp.float32) * s}
    _L0_attn_b_in = _L0_attn_b_setup()

    def _L0_ffn_setup():
        import jax, jax.numpy as jnp
        import numpy as np
        N_EXPERTS = 8
        CAP_FACTOR = 1.25
        BATCH, SEQ, DMODEL, DFF = (4, 512, 256, 1024)
        key = jax.random.key(seed)
        k0, k1, k2, k3 = jax.random.split(key, 4)
        x = jax.random.normal(k0, (BATCH, SEQ, DMODEL), dtype=jnp.float32)
        Wr = jax.random.normal(k1, (DMODEL, N_EXPERTS), dtype=jnp.float32) * 0.02
        W1 = jax.random.normal(k2, (N_EXPERTS, DMODEL, DFF), dtype=jnp.float32) * 0.02
        W2 = jax.random.normal(k3, (N_EXPERTS, DFF, DMODEL), dtype=jnp.float32) * 0.02
        return {'x': x, 'Wr': Wr, 'W1': W1, 'W2': W2}
    _L0_ffn_in = _L0_ffn_setup()
    _d = {'L0_attn_a_x': _L0_attn_a_in['x'], 'L0_attn_a_delta_W': _L0_attn_a_in['delta_W'], 'L0_attn_a_delta_b': _L0_attn_a_in['delta_b'], 'L0_attn_a_B_W': _L0_attn_a_in['B_W'], 'L0_attn_a_B_b': _L0_attn_a_in['B_b'], 'L0_attn_a_C_W': _L0_attn_a_in['C_W'], 'L0_attn_a_C_b': _L0_attn_a_in['C_b'], 'L0_attn_a_A_log': _L0_attn_a_in['A_log'], 'L0_attn_a_dt_bias': _L0_attn_a_in['dt_bias'], 'L0_attn_a_tau': _L0_attn_a_in['tau'], 'L0_attn_a_Wi_W': _L0_attn_a_in['Wi_W'], 'L0_attn_a_Wi_b': _L0_attn_a_in['Wi_b'], 'L0_attn_a_Wr_W': _L0_attn_a_in['Wr_W'], 'L0_attn_a_sel_W': _L0_attn_a_in['sel_W'], 'L0_attn_a_sel_b': _L0_attn_a_in['sel_b'], 'L0_attn_a_h0': _L0_attn_a_in['h0'], 'L0_attn_b_Wq': _L0_attn_b_in['Wq'], 'L0_attn_b_Wk': _L0_attn_b_in['Wk'], 'L0_attn_b_Wv': _L0_attn_b_in['Wv'], 'L0_attn_b_Wf': _L0_attn_b_in['Wf'], 'L0_attn_b_Wg1': _L0_attn_b_in['Wg1'], 'L0_attn_b_Wg2': _L0_attn_b_in['Wg2'], 'L0_attn_b_ln_w': _L0_attn_b_in['ln_w'], 'L0_attn_b_Wo': _L0_attn_b_in['Wo'], 'L0_ffn_Wr': _L0_ffn_in['Wr'], 'L0_ffn_W1': _L0_ffn_in['W1'], 'L0_ffn_W2': _L0_ffn_in['W2']}
    _x0 = _d['L0_attn_a_x']
    _d['L0_attn_a_x'] = jax.random.normal(jax.random.fold_in(jax.random.key(seed), 1), (8, 1024, 256), dtype=_x0.dtype)
    del _x0
    return _d

def reference(L0_attn_a_x, L0_attn_a_delta_W, L0_attn_a_delta_b, L0_attn_a_B_W, L0_attn_a_B_b, L0_attn_a_C_W, L0_attn_a_C_b, L0_attn_a_A_log, L0_attn_a_dt_bias, L0_attn_a_tau, L0_attn_a_Wi_W, L0_attn_a_Wi_b, L0_attn_a_Wr_W, L0_attn_a_sel_W, L0_attn_a_sel_b, L0_attn_a_h0, L0_attn_b_Wq, L0_attn_b_Wk, L0_attn_b_Wv, L0_attn_b_Wf, L0_attn_b_Wg1, L0_attn_b_Wg2, L0_attn_b_ln_w, L0_attn_b_Wo, L0_ffn_Wr, L0_ffn_W1, L0_ffn_W2):

    def _L0_attn_a_ref(x, delta_W, delta_b, B_W, B_b, C_W, C_b, A_log, dt_bias, tau, Wi_W, Wi_b, Wr_W, sel_W, sel_b, h0):
        import jax, jax.numpy as jnp
        import numpy as np
        B, L, D, N = (2, 512, 256, 16)
        DT = 0.1
        Bsz, Ls, Dm = x.shape
        Ns = A_log.shape[1]
        gc = x.mean(axis=1)
        inp_sig = gc @ Wi_W.T + Wi_b
        cur = jnp.broadcast_to(h0, (Bsz, Ns))
        rec = cur @ Wr_W.T
        tau_c = jnp.clip(tau, 0.1, 10.0)
        dh_dt = (-cur + jnp.tanh(inp_sig + rec)) / tau_c[None, :]
        new_h = cur + DT * dh_dt
        sel = jax.nn.sigmoid(new_h @ sel_W.T + sel_b)
        xs = x * sel[:, None, :]
        delta = jax.nn.softplus(xs @ delta_W.T + delta_b + dt_bias)
        Bm = xs @ B_W.T + B_b
        Cm = xs @ C_W.T + C_b
        A = -jnp.exp(A_log)
        A_d = jnp.exp(A[None, None] * delta[..., None])
        factor = jnp.where(jnp.abs(A)[None, None] < 1e-06, delta[..., None], (A_d - 1.0) / A[None, None])
        B_d = factor * Bm[:, :, None, :]

        def step(h, inputs):
            Ad_t, Bd_t, x_t, C_t = inputs
            h = Ad_t * h + Bd_t * x_t[..., None]
            y = jnp.einsum('bdn,bn->bd', h, C_t)
            return (h, y)
        h_init = jnp.zeros((Bsz, Dm, Ns), x.dtype)
        _, ys = jax.lax.scan(step, h_init, (A_d.transpose(1, 0, 2, 3), B_d.transpose(1, 0, 2, 3), xs.transpose(1, 0, 2), Cm.transpose(1, 0, 2)))
        return ys.transpose(1, 0, 2)

    def _L0_attn_b_ref(x, Wq, Wk, Wv, Wf, Wg1, Wg2, ln_w, Wo):
        import jax, jax.numpy as jnp
        import numpy as np
        B, N, D, H = (4, 1024, 256, 16)
        HD = D // H
        EPS_NORM = 1e-12
        EPS_LN = 1e-05

        def _silu(x):
            return x * jax.nn.sigmoid(x)

        def _simple_gla(q, k, v, f):
            qT = jnp.moveaxis(q, 1, 0)
            kT = jnp.moveaxis(k, 1, 0)
            vT = jnp.moveaxis(v, 1, 0)
            fT = jnp.moveaxis(f, 1, 0)

            def step(S, inp):
                qt, kt, vt, ft = inp
                S = jnp.exp(ft)[..., None, None] * S + kt[..., :, None] * vt[..., None, :]
                o = jnp.einsum('bhk,bhkv->bhv', qt, S)
                return (S, o)
            S0 = jnp.zeros((q.shape[0], q.shape[2], q.shape[3], v.shape[3]), q.dtype)
            _, o = jax.lax.scan(step, S0, (qT, kT, vT, fT))
            return jnp.moveaxis(o, 0, 1)
        b, n, d = x.shape
        q = _silu(x @ Wq.T).reshape(b, n, H, HD)
        k = _silu(x @ Wk.T).reshape(b, n, H, HD)
        v = _silu(x @ Wv.T).reshape(b, n, H, HD)
        f = jax.nn.log_sigmoid(x @ Wf.T)
        k = k / jnp.maximum(jnp.linalg.norm(k, axis=-1, keepdims=True), EPS_NORM)
        o = _simple_gla(q, k, v, f).reshape(b, n, d)
        gate = jax.nn.sigmoid(x @ Wg1.T @ Wg2.T)
        o = o * gate
        mu = jnp.mean(o, axis=-1, keepdims=True)
        xc = o - mu
        var = jnp.mean(xc * xc, axis=-1, keepdims=True)
        o = xc / jnp.sqrt(var + EPS_LN) * ln_w
        return o @ Wo.T

    def _L0_ffn_ref(x, Wr, W1, W2):
        import jax, jax.numpy as jnp
        import numpy as np
        N_EXPERTS = 8
        CAP_FACTOR = 1.25
        BATCH, SEQ, DMODEL, DFF = (4, 512, 256, 1024)
        B, S, D = x.shape
        E = W1.shape[0]
        cap = int(CAP_FACTOR * B * S / E)
        t = x.reshape(-1, D)
        probs = jax.nn.softmax(t @ Wr, axis=-1)
        idx = jnp.argmax(probs, axis=-1)
        pmax = jnp.max(probs, axis=-1)
        onehot = jax.nn.one_hot(idx, E, dtype=jnp.int32)
        pos = jnp.sum(jnp.cumsum(onehot, axis=0) * onehot, axis=-1) - 1
        kept = pos < cap
        flat = idx * cap + jnp.minimum(pos, cap - 1)
        disp = jnp.zeros((E * cap, D), t.dtype).at[flat].add(t * kept[:, None].astype(t.dtype))
        ein = disp.reshape(E, cap, D)
        h = jax.nn.relu(jnp.einsum('ecd,edf->ecf', ein, W1))
        eout = jnp.einsum('ecf,efd->ecd', h, W2).reshape(E * cap, D)
        comb = jnp.where(kept[:, None], eout[flat], t)
        factor = jnp.where(kept, pmax, jnp.ones_like(pmax))
        out = (comb * factor[:, None]).reshape(B, S, D)
        return out
    x = L0_attn_a_x
    x = x + _L0_attn_a_ref(_layernorm(x, axis=-1), L0_attn_a_delta_W, L0_attn_a_delta_b, L0_attn_a_B_W, L0_attn_a_B_b, L0_attn_a_C_W, L0_attn_a_C_b, L0_attn_a_A_log, L0_attn_a_dt_bias, L0_attn_a_tau, L0_attn_a_Wi_W, L0_attn_a_Wi_b, L0_attn_a_Wr_W, L0_attn_a_sel_W, L0_attn_a_sel_b, L0_attn_a_h0)
    x = x + _L0_ffn_ref(_layernorm(x, axis=-1), L0_ffn_Wr, L0_ffn_W1, L0_ffn_W2)
    x = x + _L0_attn_b_ref(_layernorm(x, axis=-1), L0_attn_b_Wq, L0_attn_b_Wk, L0_attn_b_Wv, L0_attn_b_Wf, L0_attn_b_Wg1, L0_attn_b_Wg2, L0_attn_b_ln_w, L0_attn_b_Wo)
    x = x + _L0_ffn_ref(_layernorm(x, axis=-1), L0_ffn_Wr, L0_ffn_W1, L0_ffn_W2)
    return x

_drawn_inputs = setup_inputs


def setup_inputs(seed=0):
    import zlib

    import numpy as np

    out = dict(_drawn_inputs(seed))
    spreads = {'L0_attn_a_delta_b': (0.0, 2.0),
     'L0_attn_a_B_b': (0.0, 2.0),
     'L0_attn_a_C_b': (0.0, 2.0),
     'L0_attn_a_A_log': (0.0, 2.0),
     'L0_attn_a_tau': (1.0, 0.6),
     'L0_attn_a_Wi_b': (0.0, 2.0),
     'L0_attn_a_sel_b': (0.0, 2.0),
     'L0_attn_a_h0': (0.0, 2.0),
     'L0_attn_b_ln_w': (1.0, 0.2)}
    factors = {'L0_attn_a_delta_W': 64.0,
     'L0_attn_a_B_W': 55.168,
     'L0_attn_a_C_W': 56.864,
     'L0_attn_a_dt_bias': 64.0,
     'L0_attn_a_Wi_W': 64.0,
     'L0_attn_a_Wr_W': 64.0,
     'L0_attn_a_sel_W': 64.0,
     'L0_attn_b_Wg1': 8.0,
     'L0_attn_b_Wg2': 8.0}
    for name, (base, spread) in spreads.items():
        noise = np.random.default_rng([zlib.crc32(name.encode()), seed]).standard_normal(out[name].shape)
        drawn = base * np.exp(spread * noise) if base else spread * noise
        out[name] = jnp.asarray(drawn.astype(out[name].dtype))
    for name, factor in factors.items():
        out[name] = (out[name] * factor).astype(out[name].dtype)
    return out
```

```python
from contextlib import ExitStack

import numpy as np

import concourse.bass as bass
from concourse import mybir

ALU = mybir.AluOpType
ACT = mybir.ActivationFunctionType
AX = mybir.AxisListType
F32 = mybir.dt.float32
BF16 = mybir.dt.bfloat16
U32 = mybir.dt.uint32

P = 128
B, S, D = 8, 1024, 256
T = B * S
NT = T // P
TB = S // P
DC = D // P
NS = 16
E, FF = 8, 1024
FC = FF // P
CAP = int(1.25 * T / E)
SLOTS = E * CAP + P
H, HD = 16, 16
HALF = 512
DT = 0.1
EPS = 1e-5
NEG = -1e30


def until(eng, sem, value):
    eng.wait_ge(sem, value + 1)


def until_moved(eng, sem, value):
    eng.wait_ge(sem, value)


class Tally:

    def __init__(self, sem, base=0):
        self.sem, self.base, self.n = sem, base, 0

    def inc(self, ins, k=1):
        ins.then_inc(self.sem, k)
        self.n += k
        return ins

    def here(self):
        return self.base + self.n


def link(eng, tally, ins):
    tally.inc(ins)
    until(eng, tally.sem, tally.here())


class Waits:

    def __init__(self, eng, tick):
        self.eng, self.tick = eng, tick

    def ge(self, sem, value):
        until(self.eng, sem, value)
        self.eng.sem_inc(self.tick, 1)

    def link(self, tally, ins):
        tally.inc(ins)
        self.ge(tally.sem, tally.here())


class Mem:

    def __init__(self, nc, stack, tag):
        self.nc, self.stack, self.tag, self.sems, self.ordinary = nc, stack, tag, [], []
        stack.callback(self.clear)

    def sb(self, name, shape, dt=F32):
        return self.stack.enter_context(self.nc.sbuf_tensor(self.tag + name, shape, dt))

    def ps(self, name, shape=(P, HALF), dt=F32):
        return self.stack.enter_context(self.nc.psum_tensor(self.tag + name, list(shape), dt))

    def sem(self, name, moved=False):
        self.sems.append(self.nc.alloc_semaphore(self.tag + name))
        if not moved:
            self.ordinary.append(self.sems[-1])
        return self.sems[-1]

    def start(self):
        for s in self.ordinary:
            self.nc.sync.sem_inc(s, 1)
        self.nc.all_engine_barrier()

    def clear(self):
        if self.sems:
            self.nc.clear_and_free_semaphores(self.sems)
            self.nc.all_engine_barrier()


def load_inputs(nc, g, dram):
    with ExitStack() as stack:
        m = Mem(nc, stack, "ld_")
        s_ld = m.sem("s_ld")
        m.start()
        with nc.Block() as block:
            @block.sync
            def _(sp):
                for b in range(B):
                    sp.dma_start(g.xres[:, TB * b:TB * b + TB, :],
                                 dram["x"][S * b:S * b + S, :].rearrange("(i p) d -> p i d", p=P)).then_inc(s_ld, 16)
                sp.dma_start(g.ident[:, :], dram["ident"]).then_inc(s_ld, 16)
                until(sp, s_ld, 16 * (B + 1))


def norm_stats(nc, g, tag):
    with ExitStack() as stack:
        m = Mem(nc, stack, tag)
        st = m.sb("st", [P, NT, 6])
        dm, q, ve, ln, y0, yy = (m.sb(n, [P, NT]) for n in ("dm", "q", "ve", "ln", "y0", "yy"))
        s_dv, s_ve, s_y0 = m.sem("s_dv"), m.sem("s_ve"), m.sem("s_y0")
        m.start()
        with nc.Block() as block:
            @block.vector
            def _(v):
                c = Tally(s_dv)
                with v.Fori(0, NT // 4) as i:
                    for j in range(4):
                        v.bn_stats(st[:, bass.ds(4 * i + j, 1), :], g.xres[:, bass.ds(4 * i + j, 1), :]).then_inc(s_dv, 1)
                c.n = NT
                until(v, s_dv, NT)
                c.inc(v.tensor_tensor(dm[:, :], st[:, :, 1], st[:, :, 4], ALU.subtract))
                c.inc(v.tensor_tensor(q[:, :], st[:, :, 1], st[:, :, 4], ALU.add))
                link(v, c, v.tensor_tensor(ve[:, :], st[:, :, 2], st[:, :, 5], ALU.add))
                c.inc(v.tensor_scalar(g.mean[:, :], q[:, :], 0.5, None, ALU.mult))
                link(v, c, v.tensor_tensor(dm[:, :], dm[:, :], dm[:, :], ALU.mult))
                link(v, c, v.tensor_scalar(dm[:, :], dm[:, :], 0.25, EPS, ALU.mult, ALU.add))
                v.scalar_tensor_tensor(ve[:, :], ve[:, :], 1.0 / D, dm[:, :], ALU.mult, ALU.add).then_inc(s_ve, 1)
                until(v, s_y0, 1)
                c.n += 1
                link(v, c, v.tensor_tensor(yy[:, :], y0[:, :], y0[:, :], ALU.mult))
                link(v, c, v.tensor_tensor(yy[:, :], yy[:, :], ve[:, :], ALU.mult))
                link(v, c, v.tensor_scalar(yy[:, :], yy[:, :], -0.5, 1.5, ALU.mult, ALU.add))
                link(v, c, v.tensor_tensor(g.rstd[:, :], yy[:, :], y0[:, :], ALU.mult))

            @block.scalar
            def _(a):
                a.preload_act_table_set("natural_log_exp_and_others")
                until(a, s_ve, 1)
                a.activation(ln[:, :], ve[:, :], ACT.Ln).then_inc(s_dv, 1)
                until(a, s_dv, NT + 7)
                a.activation(y0[:, :], ln[:, :], ACT.Exp, scale=-0.5).then_inc(s_y0, 1)


def norm_tile(v, g, out, i):
    return v.tensor_scalar(out, g.xres[:, bass.ds(i, 1), :], g.mean[:, bass.ds(i, 1)], g.rstd[:, bass.ds(i, 1)],
                           ALU.subtract, ALU.mult)


def ssm_layer(nc, g, dram):
    with ExitStack() as stack:
        m = Mem(nc, stack, "ssm_")
        dWT = m.sb("dWT", [P, DC, D])
        bcT = m.sb("bcT", [P, DC, 96])
        bcb = m.sb("bcb", [96, 1])
        db = m.sb("db", [P, DC])
        db2 = m.sb("db2", [P, DC])
        alog = m.sb("alog", [P, DC, NS])
        absA = m.sb("absA", [P, DC, NS])
        negA = m.sb("negA", [P, DC, NS])
        tiny = m.sb("tiny", [P, DC, NS])
        rest = m.sb("rest", [P, DC, NS])
        invA = m.sb("invA", [P, DC, NS])
        rep = m.sb("rep", [96, 2 * NS, P], BF16)
        WiT = m.sb("WiT", [P, DC, NS])
        Wib = m.sb("Wib", [NS, 1])
        WrT = m.sb("WrT", [NS, NS])
        h0 = m.sb("h0", [NS, 1])
        tau = m.sb("tau", [NS, 1])
        dtau = m.sb("dtau", [NS, 1])
        bias2 = m.sb("bias2", [NS, 1])
        selWT = m.sb("selWT", [NS, D])
        selb = m.sb("selb", [P, DC])
        nselb = m.sb("nselb", [P, DC])
        ones = m.sb("ones", [P, 1])
        tsum = m.sb("tsum", [P, 1])
        flag = m.sb("flag", [1, 1], U32)
        xn = [m.sb(f"xn{j}", [P, D]) for j in range(2)]
        xnT = m.sb("xnT", [P, DC, S])
        gp = m.sb("gp", [P, DC, 4])
        gcs = m.sb("gcs", [P, DC])
        nh = [m.sb(f"nh{j}", [NS, 1]) for j in range(5)]
        es = [m.sb(f"es{j}", [P, DC]) for j in range(3)]
        xs = m.sb("xs", [P, DC, S])
        delta = m.sb("delta", [P, DC, S])
        ab = m.sb("ab", [P, 2, HALF])
        ee = m.sb("ee", [P, 2, HALF])
        ll = m.sb("ll", [P, 2, HALF])
        dd = m.sb("dd", [P, 2, HALF])
        bcv = m.sb("bcv", [96, 2, HALF])
        br = m.sb("br", [96, 2, HALF])
        parts = m.sb("parts", [96, S], BF16)
        bcs = m.sb("bcs", [P, 2, 2, S])
        Ad = m.sb("Ad", [P, DC, S])
        xB = m.sb("xB", [P, DC, S])
        u = m.sb("u", [P, DC, S])
        hh = m.sb("hh", [P, DC, S])
        hc = m.sb("hc", [P, DC, S])
        ysb = m.sb("ysb", [P, DC, S])
        ring = [m.ps(f"ring{j}") for j in range(2)]
        misc = [m.ps(f"misc{j}") for j in range(2)]
        yps = m.ps("yps", [P, DC, 2, HALF])

        s_w, s_pre, s_prep, s_flag = m.sem("s_w"), m.sem("s_pre"), m.sem("s_prep"), m.sem("s_flag")
        s_dv, s_xn, s_tp, s_use, s_free = m.sem("s_dv"), m.sem("s_xn"), m.sem("s_tp"), m.sem("s_use"), m.sem("s_free")
        s_gc, s_z, s_nh, s_es, s_xs = m.sem("s_gc"), m.sem("s_z"), m.sem("s_nh"), m.sem("s_es"), m.sem("s_xs")
        s_dd, s_act, s_ll, s_pool, s_dl = m.sem("s_dd"), m.sem("s_act"), m.sem("s_ll"), m.sem("s_pool"), m.sem("s_dl")
        s_bcv, s_pt, s_bc, s_ev = m.sem("s_bcv"), m.sem("s_pt"), m.sem("s_bc"), m.sem("s_ev")
        s_ad, s_xb, s_u, s_h, s_hc, s_y = (m.sem(n) for n in ("s_ad", "s_xb", "s_u", "s_h", "s_hc", "s_y"))
        s_yev, s_yt, s_tick = m.sem("s_yev"), m.sem("s_yt"), m.sem("s_tick")

        loads = [(dWT[:, :, :], dram["dWT"].rearrange("(c p) n -> p c n", p=P)),
                 (bcT[:, :, :], dram["bcT"].rearrange("(c p) n -> p c n", p=P)),
                 (bcb[:, :], dram["bcb"]),
                 (db[:, :], dram["delta_b"]),
                 (db2[:, :], dram["dt_bias"]),
                 (alog[:, :, :], dram["A_log"].rearrange("(c p) n -> p c n", p=P)),
                 (rep[:, :, :], dram["rep"].bitcast(BF16).rearrange("k (n q) -> k n q", q=P)),
                 (WiT[:, :, :], dram["WiT"].rearrange("(c p) n -> p c n", p=P)),
                 (Wib[:, :], dram["Wi_b"]),
                 (WrT[:, :], dram["WrT"]),
                 (h0[:, :], dram["h0"]),
                 (tau[:, :], dram["tau"]),
                 (selWT[:, :], dram["selWT"]),
                 (selb[:, :], dram["sel_b"])]
        USES = 16
        T0, UZ, US, UD, UB, UY = 0, 4, 5, 6, 10, 12

        m.start()
        with nc.Block() as block:
            @block.sync
            def _(sp):
                for out, src in loads:
                    sp.dma_start(out, src).then_inc(s_w, 16)

            @block.tensor
            def _(pe):
                until(pe, s_w, 16 * len(loads))
                nc.tensor.matmul(misc[0][0:NS, 0:1], WrT[:, :], h0[:, :], start=True, stop=True).then_inc(s_pre, 1)
                until(pe, s_prep, 2)
                nc.tensor.matmul(misc[1][0:1, 0:1], tsum[:, :], ones[:, :], start=True, stop=True).then_inc(s_pre, 1)
                until(pe, s_flag, 1)
                with pe.Fori(0, B) as b:
                    def use(n, free):
                        until(pe, s_free, b * USES + free)
                        return misc[n % 2]

                    for jp in range(4):
                        bank = use(T0 + jp, max(jp - 1, 0))
                        for jj in range(2):
                            until(pe, s_xn, b * TB + 2 * jp + jj + 1)
                            for c in range(DC):
                                last = nc.tensor.transpose(bank[:, c * 256 + jj * P:c * 256 + jj * P + P],
                                                           xn[jj][:, c * P:c * P + P], g.ident[:, :])
                            last.then_inc(s_tp, 1)
                    until(pe, s_gc, b + 1)
                    bank = use(UZ, UZ)
                    for c in range(DC):
                        last = nc.tensor.matmul(bank[0:NS, 0:1], WiT[:, c, :], gcs[:, c:c + 1], start=(c == 0), stop=(c == DC - 1))
                    last.then_inc(s_use, 1)
                    until(pe, s_nh, b + 1)
                    bank = use(US, US)
                    for c in range(DC):
                        last = nc.tensor.matmul(bank[:, c:c + 1], selWT[:, c * P:c * P + P], nh[4][:, :], start=True, stop=True)
                    last.then_inc(s_use, 1)
                    until(pe, s_xs, b + 1)
                    for q in range(4):
                        c, h = q // 2, q % 2
                        bank = use(UD + q, UD + max(q - 1, 0))
                        for k in range(DC):
                            last = nc.tensor.matmul(bank[:, :], dWT[:, k, c * P:c * P + P], xs[:, k, h * HALF:(h + 1) * HALF],
                                                    start=(k == 0), stop=(k == DC - 1))
                        last.then_inc(s_use, 1)
                    for h in range(2):
                        bank = use(UB + h, UB + h - 1)
                        for k in range(DC):
                            last = nc.tensor.matmul(bank[0:96, :], bcT[:, k, :], xs[:, k, h * HALF:(h + 1) * HALF],
                                                    start=(k == 0), stop=(k == DC - 1))
                        last.then_inc(s_use, 1)

                    def reduce_states(n):
                        for c in range(DC):
                            until(pe, s_hc, b * 2 * NS + 2 * n + c + 1)
                            for h in range(2):
                                last = nc.tensor.matmul(yps[:, c, h, :], g.ident[:, :], hc[:, c, h * HALF:(h + 1) * HALF],
                                                        start=(n == 0), stop=(n == NS - 1))
                            last.then_inc(s_y, 1)

                    until(pe, s_pt, (b + 1) * 2)
                    until(pe, s_yev, b * 4)
                    for n in range(NS):
                        for q in range(4):
                            w, h = q // 2, q % 2
                            if n or q > 1:
                                until(pe, s_ev, b * 4 * NS + 4 * n + q - 1)
                            elif q == 0:
                                until(pe, s_ev, b * 4 * NS)
                            nc.tensor.matmul(ring[q % 2][:, :], rep[:, w * NS + n, :], parts[:, h * HALF:(h + 1) * HALF],
                                             start=True, stop=True).then_inc(s_bc, 1)
                        if n:
                            reduce_states(n - 1)
                    reduce_states(NS - 1)
                    until(pe, s_yev, (b + 1) * 4)
                    for jp in range(4):
                        bank = use(UY + jp, UY + max(jp - 1, 0))
                        for jj in range(2):
                            for c in range(DC):
                                t = (2 * jp + jj) * P
                                last = nc.tensor.transpose(bank[:, jj * D + c * P:jj * D + c * P + P], ysb[:, c, t:t + P], g.ident[:, :])
                        last.then_inc(s_yt, 1)

            @block.scalar
            def _(a):
                a.preload_act_table_set("natural_log_exp_and_others")
                until(a, s_w, 16 * len(loads))
                a.activation(absA[:, :, :], alog[:, :, :], ACT.Exp).then_inc(s_prep, 1)
                with a.Fori(0, B) as b:
                    c_act = Tally(s_act, b * 4)
                    for jp in range(4):
                        until(a, s_tp, b * TB + 2 * jp + 2)
                        for c in range(DC):
                            ins = a.activation(xnT[:, c, jp * 256:(jp + 1) * 256], misc[jp % 2][:, c * 256:(c + 1) * 256],
                                               ACT.Copy, accum_out=gp[:, c, jp:jp + 1])
                        ins.then_inc(s_free, 1)
                    until(a, s_use, b * 8 + 1)
                    a.activation(nh[0][:, :], misc[UZ % 2][0:NS, 0:1], ACT.Exp, scale=2.0 / S, bias=bias2[:, :]).then_inc(s_z, 1)
                    until(a, s_z, b + 1)
                    a.sem_inc(s_free, 1)
                    until(a, s_use, b * 8 + 2)
                    for c in range(DC):
                        ins = a.activation(es[0][:, c:c + 1], misc[US % 2][:, c:c + 1], ACT.Exp, scale=-1.0, bias=nselb[:, c:c + 1])
                    ins.then_inc(s_es, 1)
                    until(a, s_es, b + 1)
                    a.sem_inc(s_free, 1)
                    for q in range(4):
                        c, h = q // 2, q % 2
                        ps = misc[(UD + q) % 2]
                        until(a, s_use, b * 8 + 3 + q)
                        if q == 0:
                            until(a, s_dl, b * 4)
                            until(a, s_hc, b * 2 * NS)
                        if q >= 2:
                            until(a, s_dl, b * 4 + q - 1)
                        a.activation(delta[:, c, h * HALF:(h + 1) * HALF], ps[:, :], ACT.Relu, bias=db[:, c:c + 1])
                        a.activation(ab[:, q % 2, :], ps[:, :], ACT.Abs, bias=db[:, c:c + 1]).then_inc(s_free, 1)
                        until(a, s_free, b * USES + UD + q + 1)
                        c_act.inc(a.activation(ee[:, q % 2, :], ab[:, q % 2, :], ACT.Exp, scale=-1.0))
                        until(a, s_act, c_act.here())
                        a.activation(ll[:, q % 2, :], ee[:, q % 2, :], ACT.Ln, bias=1.0).then_inc(s_ll, 1)
                    for h in range(2):
                        until(a, s_use, b * 8 + 7 + h)
                        until(a, s_pt, b * 2)
                        a.activation(bcv[:, h, :], misc[(UB + h) % 2][0:96, :], ACT.Identity, bias=bcb[:, :]).then_inc(s_bcv, 1)
                        until(a, s_bcv, b * 2 + h + 1)
                        a.sem_inc(s_free, 1)
                    until(a, s_dl, b * 4 + 4)
                    for n in range(NS):
                        for q in range(4):
                            w, h = q // 2, q % 2
                            until(a, s_bc, b * 4 * NS + 4 * n + q + 1)
                            if q == 0 and n >= 2:
                                until(a, s_hc, b * 2 * NS + 2 * (n - 1))
                            a.activation(bcs[:, n % 2, w, h * HALF:(h + 1) * HALF], ring[q % 2][:, :], ACT.Copy).then_inc(s_ev, 1)
                        for c in range(DC):
                            until(a, s_h, b * 2 * NS + max(2 * (n - 1) + c + 1, 0))
                            a.activation(Ad[:, c, :], delta[:, c, :], ACT.Exp, scale=negA[:, c, n:n + 1]).then_inc(s_ad, 1)
                    until(a, s_y, (b + 1) * 2 * NS)
                    until(a, s_yt, b * 4)
                    for c in range(DC):
                        for h in range(2):
                            a.activation(ysb[:, c, h * HALF:(h + 1) * HALF], yps[:, c, h, :], ACT.Copy).then_inc(s_yev, 1)

            @block.gpsimd
            def _(gp_):
                w = Waits(gp_, s_tick)
                with gp_.Fori(0, B) as b:
                    c = Tally(s_pool, b * (4 * 2 + 2 * 4))
                    for q in range(4):
                        w.ge(s_ll, b * 4 + q + 1)
                        e_, l_, d_ = ee[:, q % 2, :], ll[:, q % 2, :], dd[:, q % 2, :]
                        w.link(c, gp_.tensor_scalar(d_, e_, 1.0, 1.0, ALU.add, ALU.subtract))
                        w.link(c, gp_.tensor_tensor(d_, e_, d_, ALU.subtract))
                        gp_.tensor_tensor(d_, d_, l_, ALU.add).then_inc(s_dd, 1)
                    for h in range(2):
                        w.ge(s_bcv, b * 2 + h + 1)
                        w.ge(s_bc, b * 4 * NS)
                        pt, bv, r = parts[:, h * HALF:(h + 1) * HALF], bcv[:, h, :], br[:, h, :]
                        w.link(c, gp_.tensor_copy(pt, bv))
                        w.link(c, gp_.tensor_tensor(r, bv, pt, ALU.subtract))
                        w.link(c, gp_.tensor_copy(pt[32:64, :], r[32:64, :]))
                        w.link(c, gp_.tensor_copy(pt[64:96, :], r[64:96, :]))
                        gp_.tensor_tensor(pt[64:96, :], r[64:96, :], pt[64:96, :], ALU.subtract).then_inc(s_pt, 1)
                        w.ge(s_pt, b * 2 + h + 1)

            @block.vector
            def _(v):
                until(v, s_w, 16 * len(loads))
                c = Tally(s_dv)
                v.memset(ones[:, :], 1.0)
                c.inc(v.tensor_tensor(db[:, :], db[:, :], db2[:, :], ALU.add))
                c.inc(v.tensor_scalar(nselb[:, :], selb[:, :], -1.0, None, ALU.mult))
                link(v, c, v.tensor_scalar(tau[:, :], tau[:, :], 0.1, 10.0, ALU.max, ALU.min))
                link(v, c, v.reciprocal(dtau[:, :], tau[:, :]))
                c.inc(v.tensor_scalar(dtau[:, :], dtau[:, :], DT, None, ALU.mult))
                until(v, s_pre, 1)
                link(v, c, v.tensor_tensor(bias2[:, :], misc[0][0:NS, 0:1], Wib[:, :], ALU.add))
                c.inc(v.tensor_scalar(bias2[:, :], bias2[:, :], 2.0, None, ALU.mult))
                until(v, s_prep, 1)
                c.inc(v.tensor_scalar(negA[:, :, :], absA[:, :, :], -1.0, None, ALU.mult))
                link(v, c, v.tensor_scalar(tiny[:, :, :], absA[:, :, :], 1e-6, None, ALU.is_lt))
                v.tensor_reduce(tsum[:, :], tiny[:, :, :], AX.XY, ALU.add).then_inc(s_prep, 1)
                link(v, c, v.tensor_scalar(rest[:, :, :], tiny[:, :, :], -1.0, 1.0, ALU.mult, ALU.add))
                link(v, c, v.tensor_tensor(invA[:, :, :], absA[:, :, :], rest[:, :, :], ALU.mult))
                link(v, c, v.tensor_tensor(invA[:, :, :], invA[:, :, :], tiny[:, :, :], ALU.add))
                link(v, c, v.reciprocal(invA[:, :, :], invA[:, :, :]))
                link(v, c, v.tensor_tensor(invA[:, :, :], invA[:, :, :], rest[:, :, :], ALU.mult))
                link(v, c, v.tensor_tensor(invA[:, :, :], tiny[:, :, :], invA[:, :, :], ALU.subtract))
                until(v, s_pre, 2)
                link(v, c, v.tensor_copy(flag[:, :], misc[1][0:1, 0:1]))
                v.sem_inc(s_flag, 1)
                some_tiny = v.value_load(flag[0:1, 0:1], min_val=0, max_val=D * NS)
                pre = c.n
                with v.Fori(0, B) as b:
                    c = Tally(s_dv, pre + b * 10)
                    for j in range(TB):
                        if j >= 2:
                            until(v, s_tp, b * TB + j - 1)
                        norm_tile(v, g, xn[j % 2][:, :], b * TB + j).then_inc(s_xn, 1)
                    until(v, s_free, b * USES + 4)
                    v.tensor_reduce(gcs[:, :], gp[:, :, :], AX.X, ALU.add).then_inc(s_gc, 1)
                    until(v, s_z, b + 1)
                    link(v, c, v.tensor_scalar(nh[1][:, :], nh[0][:, :], 1.0, None, ALU.add))
                    link(v, c, v.reciprocal(nh[2][:, :], nh[1][:, :]))
                    link(v, c, v.tensor_scalar(nh[2][:, :], nh[2][:, :], -2.0, 1.0, ALU.mult, ALU.add))
                    link(v, c, v.tensor_tensor(nh[3][:, :], nh[2][:, :], h0[:, :], ALU.subtract))
                    v.scalar_tensor_tensor(nh[4][:, :], nh[3][:, :], dtau[:, :], h0[:, :], ALU.mult, ALU.add).then_inc(s_nh, 1)
                    until(v, s_es, b + 1)
                    link(v, c, v.tensor_scalar(es[1][:, :], es[0][:, :], 1.0, None, ALU.add))
                    link(v, c, v.reciprocal(es[2][:, :], es[1][:, :]))
                    for ch in range(DC):
                        ins = v.tensor_scalar(xs[:, ch, :], xnT[:, ch, :], es[2][:, ch:ch + 1], None, ALU.mult)
                    ins.then_inc(s_xs, 1)
                    for q in range(4):
                        until(v, s_dd, b * 4 + q + 1)
                        link(v, c, v.tensor_tensor(dd[:, q % 2, :], dd[:, q % 2, :], ee[:, q % 2, :], ALU.min))
                        dl = delta[:, q // 2, (q % 2) * HALF:(q % 2 + 1) * HALF]
                        v.tensor_tensor(dl, dl, dd[:, q % 2, :], ALU.add).then_inc(s_dl, 1)
                    until(v, s_xs, b + 1)
                    for n in range(NS):
                        k = b * 2 * NS + 2 * n
                        Bn, Cn = bcs[:, n % 2, 0, :], bcs[:, n % 2, 1, :]
                        until(v, s_ev, b * 4 * NS + 4 * n + 2)
                        for ch in range(DC):
                            v.tensor_tensor(xB[:, ch, :], xs[:, ch, :], Bn, ALU.mult).then_inc(s_xb, 1)
                        for ch in range(DC):
                            until(v, s_ad, k + ch + 1)
                            until(v, s_xb, k + ch + 1)
                            v.scalar_tensor_tensor(u[:, ch, :], Ad[:, ch, :], -1.0, xB[:, ch, :], ALU.add, ALU.mult).then_inc(s_u, 1)
                        with v.If(some_tiny > 0):
                            until(v, s_u, k + 2)
                            for ch in range(DC):
                                v.tensor_scalar(u[:, ch, :], u[:, ch, :], rest[:, ch, n:n + 1], None, ALU.mult)
                                v.scalar_tensor_tensor(xB[:, ch, :], xB[:, ch, :], tiny[:, ch, n:n + 1], delta[:, ch, :], ALU.mult, ALU.mult)
                                v.drain()
                                v.tensor_tensor(u[:, ch, :], u[:, ch, :], xB[:, ch, :], ALU.add)
                            v.drain()
                        for ch in range(DC):
                            until(v, s_u, k + ch + 1)
                            v.tensor_tensor_scan(hh[:, ch, :], Ad[:, ch, :], u[:, ch, :], 0.0, ALU.mult, ALU.add).then_inc(s_h, 1)
                        until(v, s_ev, b * 4 * NS + 4 * n + 4)
                        for ch in range(DC):
                            until(v, s_h, k + ch + 1)
                            until(v, s_y, b * 2 * NS + max(2 * (n - 1) + ch + 1, 0))
                            v.scalar_tensor_tensor(hc[:, ch, :], hh[:, ch, :], invA[:, ch, n:n + 1], Cn, ALU.mult, ALU.mult).then_inc(s_hc, 1)
                    for jp in range(4):
                        until(v, s_yt, b * 4 + jp + 1)
                        xr = g.xres[:, bass.ds(b * TB + 2 * jp, 2), :]
                        v.tensor_tensor(xr, xr, misc[(UY + jp) % 2][:, :].rearrange("p (j d) -> p j d", j=2), ALU.add).then_inc(s_free, 1)


def fill_slots(nc, g, dram):
    rows = SLOTS // P
    step = 9
    with ExitStack() as stack:
        m = Mem(nc, stack, "fs_")
        zero = m.sb("zero", [P, step * D])
        s_z, s_st = m.sem("s_z"), m.sem("s_st")
        m.start()
        with nc.Block() as block:
            @block.vector
            def _(v):
                v.memset(zero[:, :], 0.0).then_inc(s_z, 1)

            @block.sync
            def _(sp):
                until(sp, s_z, 1)
                view = dram["slots"].rearrange("(p r) d -> p (r d)", r=rows)
                for k in range(rows // step):
                    sp.dma_start(view[:, k * step * D:(k + 1) * step * D], zero[:, :]).then_inc(s_st, 16)
                until(sp, s_st, 16 * (rows // step))


def route(nc, g, dram, tag):
    U = 4
    with ExitStack() as stack:
        m = Mem(nc, stack, tag)
        Wr = m.sb("Wr", [P, DC, E])
        tri = m.sb("tri", [P, P], BF16)
        oneb = m.sb("oneb", [P, P], BF16)
        jrow = m.sb("jrow", [P, 1, E])
        reset = m.sb("reset", [P, E * NT])
        trash = m.sb("trash", [P, 1])
        xn = [m.sb(f"xn{j}", [P, D]) for j in range(U)]
        xT = [m.sb(f"xT{j}", [P, D]) for j in range(U)]
        lg, d, ex, cnd, posm = (m.sb(n, [P, NT, E]) for n in ("lg", "d", "ex", "cnd", "posm"))
        ohb = m.sb("ohb", [P, NT, E], BF16)
        tot, pre = m.sb("tot", [P, E, NT]), m.sb("pre", [P, E, NT])
        mx, mn, idx, ssum, pos1, kept, slot, gf, tr = (
            m.sb(n, [P, NT]) for n in ("mx", "mn", "idx", "ssum", "pos1", "kept", "slot", "gf", "tr"))
        sidx = m.sb("sidx", [P, NT], U32)
        row = [m.sb(f"row{j}", [P, D]) for j in range(2 * U)]
        at = [m.sb(f"at{j}", [P, 1], U32) for j in range(2 * U)]
        psT = [m.ps(f"psT{j}") for j in range(U)]
        psL = [m.ps(f"psL{j}") for j in range(U)]
        s_w, s_xn, s_tp, s_xT, s_lp, s_lg = (m.sem(n) for n in ("s_w", "s_xn", "s_tp", "s_xT", "s_lp", "s_lg"))
        s_dv, s_d, s_ex, s_oh, s_cum, s_row, s_tick = (m.sem(n) for n in ("s_dv", "s_d", "s_ex", "s_oh", "s_cum", "s_row", "s_tick"))
        s_sc = [m.sem(f"s_sc{j}", moved=True) for j in range(2)]
        loads = [(Wr[:, :, :], dram["Wr"].rearrange("(c p) e -> p c e", p=P)), (tri[:, :], dram["tri"].bitcast(BF16)),
                 (oneb[:, :], dram["oneb"].bitcast(BF16)), (jrow[:, 0, :], dram["jrow"]), (reset[:, :], dram["reset"]),
                 (trash[:, :], dram["trash"])]
        m.start()
        with nc.Block() as block:
            @block.sync
            def _(sp):
                for out, src in loads:
                    sp.dma_start(out, src).then_inc(s_w, 16)

            @block.tensor
            def _(pe):
                until(pe, s_w, 16 * len(loads))
                with pe.Fori(0, NT // U) as it:
                    for j in range(U):
                        until(pe, s_xn, it * U + j + 1)
                        until(pe, s_xT, it * U)
                        for c in range(DC):
                            last = nc.tensor.transpose(psT[j][:, c * P:(c + 1) * P], xn[j][:, c * P:(c + 1) * P], g.ident[:, :])
                        last.then_inc(s_tp, 1)
                    for j in range(U):
                        until(pe, s_xT, it * U + j + 1)
                        until(pe, s_lg, it * U)
                        for c in range(DC):
                            last = nc.tensor.matmul(psL[j][:, 0:E], xT[j][:, c * P:(c + 1) * P], Wr[:, c, :], start=(c == 0), stop=(c == DC - 1))
                        last.then_inc(s_lp, 1)
                until(pe, s_oh, 1)
                flat = ohb[:, :, :].rearrange("p i e -> p (i e)")
                nc.tensor.matmul(psT[0][:, :], tri[:, :], flat, start=True, stop=True)
                nc.tensor.matmul(psT[1][:, :], oneb[:, :], flat, start=True, stop=True).then_inc(s_cum, 1)

            @block.scalar
            def _(a):
                with a.Fori(0, NT // U) as it:
                    for j in range(U):
                        until(a, s_tp, it * U + j + 1)
                        until(a, s_lp, it * U)
                        a.activation(xT[j][:, :], psT[j][:, 0:D], ACT.Copy).then_inc(s_xT, 1)
                until(a, s_d, 1)
                a.activation(ex[:, :, :], d[:, :, :], ACT.Exp).then_inc(s_ex, 1)

            @block.gpsimd
            def _(p_):
                w = Waits(p_, s_tick)
                with p_.Fori(0, NT // (2 * U)) as it:
                    for j in range(2 * U):
                        w.ge(s_row, it * 2 * U + j + 1)
                        p_.indirect_dma_start(dram["slots"], bass.IndirectOffsetOnAxis(ap=at[j][:, :], axis=0),
                                              row[j][:, :], None).then_inc(s_sc[j // U], 16)
                for q in range(2):
                    until_moved(p_, s_sc[q], 16 * NT // 2)

            @block.vector
            def _(v):
                with v.Fori(0, NT // U) as it:
                    for j in range(U):
                        until(v, s_tp, it * U)
                        norm_tile(v, g, xn[j][:, :], it * U + j).then_inc(s_xn, 1)
                    for j in range(U):
                        until(v, s_lp, it * U + j + 1)
                        v.tensor_copy(lg[:, bass.ds(it * U + j, 1), :], psL[j][:, 0:E]).then_inc(s_lg, 1)
                until(v, s_lg, NT)
                until(v, s_w, 16 * len(loads))
                c = Tally(s_dv)
                wide = lambda t: t[:, :].unsqueeze(2).broadcast_to([P, NT, E])
                link(v, c, v.tensor_reduce(mx[:, :], lg[:, :, :], AX.X, ALU.max))
                v.tensor_tensor(d[:, :, :], lg[:, :, :], wide(mx), ALU.subtract).then_inc(s_d, 1)
                until(v, s_d, 1)
                link(v, c, v.tensor_scalar(cnd[:, :, :], d[:, :, :], 0.0, -float(E), ALU.is_ge, ALU.mult))
                link(v, c, v.tensor_tensor(cnd[:, :, :], cnd[:, :, :], jrow[:, :, :].broadcast_to([P, NT, E]), ALU.add))
                link(v, c, v.tensor_reduce(mn[:, :], cnd[:, :, :], AX.X, ALU.min))
                v.tensor_tensor(ohb[:, :, :], cnd[:, :, :], wide(mn), ALU.is_equal).then_inc(s_oh, 1)
                c.inc(v.tensor_scalar(idx[:, :], mn[:, :], float(E), None, ALU.add))
                until(v, s_ex, 1)
                link(v, c, v.tensor_reduce(ssum[:, :], ex[:, :, :], AX.X, ALU.add))
                link(v, c, v.reciprocal(ssum[:, :], ssum[:, :]))
                until(v, s_cum, 1)
                link(v, c, v.tensor_copy(tot[:, :, :], psT[1][:, :].rearrange("p (i e) -> p e i", e=E)))
                fl = lambda t: t[:, :, :].rearrange("p e i -> p (e i)")
                link(v, c, v.tensor_tensor_scan(fl(pre), reset[:, :], fl(tot), 0.0, ALU.mult, ALU.add))
                link(v, c, v.tensor_tensor(pre[:, :, :], pre[:, :, :], tot[:, :, :], ALU.subtract))
                link(v, c, v.tensor_tensor(posm[:, :, :], psT[0][:, :].rearrange("p (i e) -> p i e", e=E),
                                           pre[:, :, :].rearrange("p e i -> p i e"), ALU.add))
                link(v, c, v.tensor_tensor(posm[:, :, :], posm[:, :, :], ohb[:, :, :], ALU.mult))
                link(v, c, v.tensor_reduce(pos1[:, :], posm[:, :, :], AX.X, ALU.add))
                c.inc(v.tensor_scalar(kept[:, :], pos1[:, :], float(CAP), None, ALU.is_le))
                link(v, c, v.tensor_scalar(slot[:, :], pos1[:, :], float(CAP), -1.0, ALU.min, ALU.add))
                c.inc(v.tensor_scalar(g.nk[:, :], kept[:, :], -1.0, 1.0, ALU.mult, ALU.add))
                c.inc(v.tensor_tensor(g.fe[:, :], kept[:, :], ssum[:, :], ALU.mult))
                link(v, c, v.scalar_tensor_tensor(gf[:, :], idx[:, :], float(CAP), slot[:, :], ALU.mult, ALU.add))
                c.inc(v.tensor_copy(g.gidx[:, :], gf[:, :]))
                link(v, c, v.tensor_scalar(tr[:, :], gf[:, :], -1.0, trash[:, :], ALU.mult, ALU.add))
                link(v, c, v.tensor_tensor(tr[:, :], tr[:, :], g.nk[:, :], ALU.mult))
                link(v, c, v.tensor_tensor(sidx[:, :], tr[:, :], gf[:, :], ALU.add))

                def send(it, j):
                    v.tensor_copy(at[j][:, :], sidx[:, bass.ds(it * 2 * U + j, 1)]).then_inc(s_dv, 1)
                    norm_tile(v, g, row[j][:, :], it * 2 * U + j).then_inc(s_row, 1)

                for j in range(2 * U):
                    send(0, j)
                with v.Fori(1, NT // (2 * U)) as it:
                    for j in range(2 * U):
                        if j % U == 0:
                            until_moved(v, s_sc[j // U], it * (16 * U))
                        send(it, j)


def experts(nc, g, dram, tag):
    BLK, PAIR = 256, 2
    NB = CAP // BLK
    NK = PAIR * NB
    BT = BLK // P
    with ExitStack() as stack:
        m = Mem(nc, stack, tag)
        w1 = [m.sb(f"w1{q}", [P, DC, FF]) for q in range(PAIR)]
        w2 = [m.sb(f"w2{q}", [P, FC, D]) for q in range(PAIR)]
        rows = [m.sb(f"rows{q}", [P, BT, D]) for q in range(2)]
        xT = [m.sb(f"xT{q}", [P, DC, BLK]) for q in range(2)]
        h = [m.sb(f"h{q}", [P, FC, BLK]) for q in range(2)]
        out = [m.sb(f"out{q}", [P, BT, D]) for q in range(2)]
        psX = [m.ps(f"psX{q}") for q in range(2)]
        psH = [m.ps(f"psH{q}") for q in range(4)]
        psO = [m.ps(f"psO{q}") for q in range(2)]
        s_w = [m.sem(f"s_w{q}") for q in range(PAIR)]
        s_in = [m.sem(f"s_in{q}") for q in range(2)]
        s_out = [m.sem(f"s_out{q}") for q in range(2)]
        s_t, s_x, s_m1, s_h, s_m2, s_o = (m.sem(n) for n in ("s_t", "s_x", "s_m1", "s_h", "s_m2", "s_o"))
        m.start()
        with nc.Block() as block:
            @block.sync
            def _(sp):
                def weights(e, q):
                    sp.dma_start(w1[q][:, :, :], dram["W1"][bass.ds(e * D, D), :].rearrange("(c p) f -> p c f", p=P)).then_inc(s_w[q], 16)
                    sp.dma_start(w2[q][:, :, :], dram["W2"][bass.ds(e * FF, FF), :].rearrange("(c p) f -> p c f", p=P)).then_inc(s_w[q], 16)

                def view(t, it, k):
                    return dram[t][bass.ds(it * NK * BLK + k * BLK, BLK), :].rearrange("(j p) d -> p j d", p=P)

                with sp.Fori(0, E // PAIR) as it:
                    def store(k):
                        until(sp, s_o, it * NK + k + 1)
                        sp.dma_start(view("eout", it, k), out[k % 2][:, :, :]).then_inc(s_out[k % 2], 16)

                    for k in range(NK):
                        if k % NB == 0:
                            until(sp, s_m2, it * NK)
                            weights(it * PAIR + k // NB, k // NB)
                        if k >= 2:
                            until(sp, s_t, it * NK + k - 1)
                        elif k == 0:
                            until(sp, s_t, it * NK)
                        sp.dma_start(rows[k % 2][:, :, :], view("slots", it, k)).then_inc(s_in[k % 2], 16)
                        if k >= 2:
                            store(k - 2)
                    store(NK - 2)
                    store(NK - 1)
                for q in range(2):
                    until(sp, s_out[q], 16 * E * NB // 2)

            @block.tensor
            def _(pe):
                with pe.Fori(0, E // PAIR) as it:
                    def turn(k):
                        until(pe, s_in[k % 2], it * (16 * NK // 2) + 16 * (k // 2 + 1))
                        until(pe, s_x, it * NK + max(k - 1, 0))
                        for j in range(BT):
                            for c in range(DC):
                                last = nc.tensor.transpose(psX[k % 2][:, c * BLK + j * P:c * BLK + (j + 1) * P],
                                                           rows[k % 2][:, j, c * P:(c + 1) * P], g.ident[:, :])
                        last.then_inc(s_t, 1)

                    def up(k):
                        q = k // NB
                        until(pe, s_x, it * NK + k + 1)
                        until(pe, s_w[q], it * 32 + 32)
                        for f in range(FC):
                            bank, half = psH[f // 2], f % 2
                            if half == 0:
                                until(pe, s_h, it * NK * 4 + max((k - 1) * 4 + f // 2 + 1, 0))
                            for c in range(DC):
                                last = nc.tensor.matmul(bank[:, half * BLK:(half + 1) * BLK], w1[q][:, c, f * P:(f + 1) * P],
                                                        xT[k % 2][:, c, :], start=(c == 0), stop=(c == DC - 1))
                            if half:
                                last.then_inc(s_m1, 1)

                    def down(k):
                        q = k // NB
                        until(pe, s_h, it * NK * 4 + 4 * k + 4)
                        until(pe, s_o, it * NK + max(k - 1, 0))
                        for j in range(BT):
                            for f in range(FC):
                                last = nc.tensor.matmul(psO[k % 2][:, j * D:(j + 1) * D], h[k % 2][:, f, j * P:(j + 1) * P],
                                                        w2[q][:, f, :], start=(f == 0), stop=(f == FC - 1))
                        last.then_inc(s_m2, 1)

                    for k in range(NK):
                        turn(k)
                        if k:
                            up(k - 1)
                        if k > 1:
                            down(k - 2)
                    up(NK - 1)
                    down(NK - 2)
                    down(NK - 1)

            @block.scalar
            def _(a):
                with a.Fori(0, E // PAIR) as it:
                    for k in range(NK):
                        for q in range(4):
                            until(a, s_m1, it * NK * 4 + 4 * k + q + 1)
                            until(a, s_m2, it * NK + max(k - 1, 0))
                            a.activation(h[k % 2][:, 2 * q:2 * q + 2, :], psH[q][:, :].rearrange("p (f t) -> p f t", f=2),
                                         ACT.Relu).then_inc(s_h, 1)

            @block.vector
            def _(v):
                with v.Fori(0, E // PAIR) as it:
                    def copy_turned(k):
                        until(v, s_t, it * NK + k + 1)
                        until(v, s_m1, it * NK * 4 + max(4 * (k - 1), 0))
                        v.tensor_copy(xT[k % 2][:, :, :], psX[k % 2][:, :].rearrange("p (c t) -> p c t", c=DC)).then_inc(s_x, 1)

                    def copy_out(k):
                        until(v, s_m2, it * NK + k + 1)
                        until(v, s_out[k % 2], it * (16 * NK // 2) + 16 * (k // 2))
                        v.tensor_copy(out[k % 2][:, :, :], psO[k % 2][:, :].rearrange("p (j d) -> p j d", j=BT)).then_inc(s_o, 1)

                    for k in range(NK):
                        copy_turned(k)
                        if k > 1:
                            copy_out(k - 2)
                    copy_out(NK - 2)
                    copy_out(NK - 1)


def combine(nc, g, dram, tag):
    U = 8
    NI = NT // (2 * U)
    with ExitStack() as stack:
        m = Mem(nc, stack, tag)
        at = [m.sb(f"at{j}", [P, 1], U32) for j in range(2 * U)]
        got = [m.sb(f"got{j}", [P, D]) for j in range(2 * U)]
        t = [m.sb(f"t{j}", [P, D]) for j in range(2 * U)]
        s_at, s_use, s_t, s_a, s_tick = (m.sem(n) for n in ("s_at", "s_use", "s_t", "s_a", "s_tick"))
        s_get = [m.sem(f"s_get{j}", moved=True) for j in range(2 * U)]
        m.start()
        with nc.Block() as block:
            @block.gpsimd
            def _(p_):
                w = Waits(p_, s_tick)
                with p_.Fori(0, NI) as it:
                    for j in range(2 * U):
                        w.ge(s_at, it * 2 * U + j + 1)
                        if j % U == 0:
                            w.ge(s_use, it * 2 * U + max(j - U, 0))
                        p_.indirect_dma_start(got[j][:, :], None, dram["eout"],
                                              bass.IndirectOffsetOnAxis(ap=at[j][:, :], axis=0)).then_inc(s_get[j], 16)

            @block.vector
            def _(v):
                def slots(it, group):
                    for j in range(group * U, group * U + U):
                        v.tensor_copy(at[j][:, :], g.gidx[:, bass.ds(it * 2 * U + j, 1)]).then_inc(s_at, 1)

                def add(it, group):
                    js = range(group * U, group * U + U)
                    i = [it * 2 * U + j for j in range(2 * U)]
                    x = [g.xres[:, bass.ds(k, 1), :].rearrange("p o d -> p (o d)") for k in i]
                    until(v, s_use, it * 2 * U + max((group - 1) * U, 0))
                    for j in js:
                        norm_tile(v, g, t[j][:, :], i[j]).then_inc(s_t, 1)
                    for j in js:
                        until(v, s_t, i[j] + 1)
                        v.scalar_tensor_tensor(t[j][:, :], t[j][:, :], g.nk[:, bass.ds(i[j], 1)], x[j], ALU.mult, ALU.add).then_inc(s_a, 1)
                    for j in js:
                        until(v, s_a, i[j] + 1)
                        until_moved(v, s_get[j], it * 16 + 16)
                        v.scalar_tensor_tensor(x[j], got[j][:, :], g.fe[:, bass.ds(i[j], 1)], t[j][:, :], ALU.mult, ALU.add).then_inc(s_use, 1)

                slots(0, 0)
                slots(0, 1)
                with v.Fori(0, NI - 1) as it:
                    for group in range(2):
                        add(it, group)
                        slots(it + 1, group)
                for group in range(2):
                    add(NI - 1, group)


def moe_layer(nc, g, dram, tag):
    norm_stats(nc, g, tag + "n_")
    route(nc, g, dram, tag + "r_")
    experts(nc, g, dram, tag + "e_")
    combine(nc, g, dram, tag + "c_")


class Event:

    def __init__(self, sem, per):
        self.sem, self.per = sem, per

    def wait(self, eng, it, i):
        until(eng, self.sem, it * self.per + i + 1)

    def wait_all_before(self, eng, it):
        until(eng, self.sem, it * self.per)


class Banks:

    def __init__(self, m, plan):
        self.bank = [m.ps(f"bank{q}") for q in range(8)]
        self.full = [m.sem(f"s_full{q}") for q in range(8)]
        self.free = [m.sem(f"s_free{q}") for q in range(8)]
        self.where, self.uses = {}, [0] * 8
        for n, name in enumerate(plan):
            self.where[name] = (n % 8, self.uses[n % 8])
            self.uses[n % 8] += 1

    def fill(self, pe, it, name):
        q, k = self.where[name]
        until(pe, self.free[q], it * self.uses[q] + k)
        return self.bank[q]

    def filled(self, ins, name):
        ins.then_inc(self.full[self.where[name][0]], 1)

    def read(self, eng, it, name):
        q, k = self.where[name]
        until(eng, self.full[q], it * self.uses[q] + k + 1)
        return self.bank[q]

    def released(self, eng, name):
        eng.sem_inc(self.free[self.where[name][0]], 1)


def gla_layer(nc, g, dram):
    C, G, HP = TB, 4, 32
    HG = H // G
    with ExitStack() as stack:
        m = Mem(nc, stack, "gla_")
        Wqkv = m.sb("Wqkv", [P, DC, 3 * D])
        WfT = m.sb("WfT", [P, DC, H])
        Wg1T = m.sb("Wg1T", [P, DC, HD])
        Wg2T = m.sb("Wg2T", [HD, D])
        WoT = m.sb("WoT", [P, DC, D])
        lnw = m.sb("lnw", [P, DC])
        trif = m.sb("trif", [P, P])
        onef = m.sb("onef", [P, P])
        identb = m.sb("identb", [P, P], BF16)
        later = m.sb("later", [P, HALF], BF16)
        heads = m.sb("heads", [96, H * P], BF16)
        bmask = m.sb("bmask", [P, D])
        hmask = m.sb("hmask", [P, HG])
        xn2 = [m.sb(f"xn{j}", [P, 2, D]) for j in range(2)]
        xn = [xn2[j // 2][:, j % 2, :] for j in range(4)]
        xnT = m.sb("xnT", [P, DC, S])
        g1T = m.sb("g1T", [HD, S])
        th = [m.sb(f"th{j}", [P, HALF]) for j in range(2)]
        tv = m.sb("tv", [P, 2, D])
        qpad = m.sb("qpad", [P, C * H, HP])
        kpad = m.sb("kpad", [P, C * H, HP])
        ktil = [m.sb(f"ktil{j}", [P, H, HP]) for j in range(2)]
        v2 = m.sb("v2", [P, C * D + HD])
        gt = m.sb("gt", [P, C, D])
        og = gt
        small = lambda n: m.sb(n, [P, C * H])
        zc, za, ze, zl, zr, f = (small(n) for n in ("zc", "za", "ze", "zl", "zr", "f"))
        f3 = m.sb("f3", [P, C, 3, HP])
        n2, nl, ny, nt, rn = (small(n) for n in ("n2", "nl", "ny", "nt", "rn"))
        Ft, dF, eF, dec, wk = (small(n) for n in ("Ft", "dF", "eF", "dec", "wk"))
        ftv = m.sb("ftv", [96, HALF])
        ftr = m.sb("ftr", [96, HALF])
        FP = m.sb("FP", [96, S], BF16)
        FN = m.sb("FN", [96, S], BF16)
        qT = [m.sb(f"qT{j}", [P, G, P]) for j in range(3)]
        kT = [m.sb(f"kT{j}", [P, G, P]) for j in range(3)]
        Dg = [m.sb(f"Dg{j}", [P, HG, P]) for j in range(2)]
        odd = m.sb("odd", [P, G, HALF])
        sq = odd[:, :, :].rearrange("p g t -> p (g t)").rearrange("p (h k) -> p h k", k=HD)
        Ag = [t.rearrange("p (h t) -> p h t", h=HG) for t in
              [xnT[:, q // 2, (q % 2) * HALF:(q % 2 + 1) * HALF] for q in range(G)] + [odd[:, q, :] for q in range(G)]]
        St = [m.sb(f"St{j}", [P, H, HD]) for j in range(2)]
        Um = m.sb("Um", [P, H, HD])
        Sd = m.sb("Sd", [P, H, HD])
        o1 = [m.sb(f"o1{j}", [P, H, HD]) for j in range(2)]
        bst = m.sb("bst", [P, C, 6])
        bdm, bq, bve, bl, by, bt, bmean, brs = (m.sb(n, [P, C]) for n in ("bdm", "bq", "bve", "bl", "by", "bt", "bmean", "brs"))
        onT = th
        Qd = [t[:, :].rearrange("p (h t) -> p h t", h=HG) for t in th] + \
             [t[:, :, :].rearrange("p a b -> p (a b)").rearrange("p (h t) -> p h t", h=HG) for t in xn2]
        oT = tv[:, :, :].rearrange("p a b -> p (a b)")

        plan = [f"x{j}" for j in range(4)] + ["zf", "g0", "g1"]
        for c in range(C):
            plan += [f"qk{c}", f"vg{c}"]
        plan += ["Fn", "FT0", "FT1"]
        plan += ["qT0", "kT0"]
        for c in range(C):
            if c + 1 < C:
                plan += [f"qT{c + 1}", f"kT{c + 1}"]
            for q in range(G):
                plan += [f"S{c}{q}", f"G{c}{q}"]
                if c and q == 1:
                    plan += [f"t{c - 1}", f"i{c - 1}"]
                if c and q == 2:
                    plan += [f"o{c - 1}"]
            plan += [f"U{c}"]
        plan += [f"t{C - 1}", f"i{C - 1}", f"o{C - 1}"]
        for j in range(4):
            plan += [f"n{j}"]
        for j in range(4):
            plan += [f"W{j}"]
        banks = Banks(m, plan)

        ev = lambda name, per: Event(m.sem("s_" + name), per)
        e_xn, e_xp, e_xT, e_g1, e_th, e_tv, e_gt = ev("xn", C), ev("xp", C), ev("xT", 4), ev("g1", 2), ev("th", C), ev("tv", C), ev("gt", C)
        e_q, e_k, e_v = ev("q", C), ev("k", C), ev("v", C)
        e_zc, e_za, e_ze, e_zl, e_zr, e_f3, e_n2, e_nl, e_ny, e_kp = (ev(n, 1) for n in ("zc", "za", "ze", "zl", "zr", "f3", "n2", "nl", "ny", "kp"))
        e_Ft, e_dF, e_wk, e_ftv, e_FP, e_FN = ev("Ft", 3), ev("dF", 1), ev("wk", 1), ev("ftv", 2), ev("FP", 2), ev("FN", 2)
        e_qT, e_kT, e_kt, e_D, e_A, e_au = ev("qT", C), ev("kT", C), ev("kt", C), ev("D", C * G), ev("A", C * G), ev("au", C)
        e_st, e_og, e_tp, e_bv, e_bl, e_by, e_on, e_onp, e_onT, e_x, e_U = (
            ev("st", C + 1), ev("og", C), ev("tp", C), ev("bv", 1), ev("bl", 1), ev("by", 1), ev("on", C), ev("onp", 4), ev("onT", 4),
            ev("x", 4), ev("U", C))
        e_Qd, e_oT = ev("Qd", C * G), ev("oT", C)
        s_w, s_pre, s_dv, s_split, s_tick, s_pre8, s_ln = (m.sem(n) for n in ("s_w", "s_pre", "s_dv", "s_split", "s_tick", "s_chunk", "s_ln"))
        loads = [(Wqkv[:, :, :], dram["Wqkv"].rearrange("(c p) n -> p c n", p=P)), (WfT[:, :, :], dram["WfT"].rearrange("(c p) n -> p c n", p=P)),
                 (Wg1T[:, :, :], dram["Wg1T"].rearrange("(c p) n -> p c n", p=P)), (Wg2T[:, :], dram["Wg2T"]),
                 (WoT[:, :, :], dram["WoT"].rearrange("(c p) n -> p c n", p=P)), (lnw[:, :], dram["ln_w"]),
                 (trif[:, :], dram["trif"]), (onef[:, :], dram["onef"]), (identb[:, :], dram["identb"].bitcast(BF16)),
                 (later[:, :], dram["later"].bitcast(BF16)), (heads[:, :], dram["heads"].bitcast(BF16)), (bmask[:, :], dram["bmask"]),
                 (hmask[:, :], dram["hmask"])]
        flat = lambda t: t[:, :, :].rearrange("p a b -> p (a b)")

        m.start()
        with nc.Block() as block:
            @block.sync
            def _(sp):
                for out, src in loads:
                    sp.dma_start(out, src).then_inc(s_w, 16)

            @block.tensor
            def _(pe):
                until(pe, s_w, 16 * len(loads))
                until(pe, s_pre, 1)
                with pe.Fori(0, B) as b:
                    fill = lambda name: banks.fill(pe, b, name)
                    for jp in range(4):
                        bank = fill(f"x{jp}")
                        for jj in range(2):
                            e_xn.wait(pe, b, 2 * jp + jj)
                            for c in range(DC):
                                last = nc.tensor.transpose(bank[:, c * 256 + jj * P:c * 256 + jj * P + P],
                                                           xn[(2 * jp + jj) % 4][:, c * P:c * P + P], g.ident[:, :])
                        banks.filled(last, f"x{jp}")
                    e_xT.wait(pe, b, 3)
                    bank = fill("zf")
                    for c in range(C):
                        for k in range(DC):
                            last = nc.tensor.matmul(bank[:, c * H:(c + 1) * H], xnT[:, k, c * P:(c + 1) * P], WfT[:, k, :],
                                                    start=(k == 0), stop=(k == DC - 1))
                    banks.filled(last, "zf")
                    for h in range(2):
                        bank = fill(f"g{h}")
                        for k in range(DC):
                            last = nc.tensor.matmul(bank[0:HD, :], Wg1T[:, k, :], xnT[:, k, h * HALF:(h + 1) * HALF],
                                                    start=(k == 0), stop=(k == DC - 1))
                        banks.filled(last, f"g{h}")
                    for c in range(C):
                        bank = fill(f"qk{c}")
                        for k in range(DC):
                            last = nc.tensor.matmul(bank[:, :], xnT[:, k, c * P:(c + 1) * P], Wqkv[:, k, 0:2 * D],
                                                    start=(k == 0), stop=(k == DC - 1))
                        banks.filled(last, f"qk{c}")
                        bank = fill(f"vg{c}")
                        for k in range(DC):
                            nc.tensor.matmul(bank[:, 0:D], xnT[:, k, c * P:(c + 1) * P], Wqkv[:, k, 2 * D:3 * D],
                                             start=(k == 0), stop=(k == DC - 1))
                        e_g1.wait(pe, b, c // 4)
                        last = nc.tensor.matmul(bank[:, D:2 * D], g1T[:, c * P:(c + 1) * P], Wg2T[:, :], start=True, stop=True)
                        banks.filled(last, f"vg{c}")
                    e_f3.wait(pe, b, 0)
                    bank = fill("Fn")
                    nc.tensor.matmul(bank[:, 0:C * H], trif[:, :], f[:, :], start=True, stop=True)
                    last = nc.tensor.matmul(bank[:, C * H:2 * C * H], onef[:, :], f[:, :], start=True, stop=True)
                    banks.filled(last, "Fn")
                    for h in range(2):
                        bank = fill(f"FT{h}")
                        for q in range(4):
                            last = nc.tensor.matmul(bank[0:96, q * P:(q + 1) * P], f3[:, 4 * h + q, :, :].rearrange("p a b -> p (a b)"),
                                                    trif[:, :], start=True, stop=True)
                        banks.filled(last, f"FT{h}")

                    def turn(c):
                        e_q.wait(pe, b, c)
                        for name, pad in (("qT", qpad), ("kT", kpad)):
                            if name == "kT":
                                e_kp.wait(pe, b, 0)
                            bank = fill(f"{name}{c}")
                            for q in range(G):
                                src = pad[:, c * H + HG * q:c * H + HG * (q + 1), :].rearrange("p a b -> p (a b)")
                                last = nc.tensor.transpose(bank[:, q * P:(q + 1) * P], src, g.ident[:, :])
                            banks.filled(last, f"{name}{c}")

                    def intra(c):
                        bank = fill(f"t{c}")
                        e_v.wait(pe, b, c)
                        for q in range(G):
                            e_A.wait(pe, b, c * G + q)
                            for j in range(HG):
                                w = c * D + (HG * q + j) * HD
                                last = nc.tensor.matmul(bank[HP * j:HP * (j + 1), q * P:(q + 1) * P], v2[:, w:w + HP],
                                                        Ag[(c % 2) * G + q][:, j, :], start=True, stop=True)
                        banks.filled(last, f"t{c}")

                    def inter(c):
                        bank = fill(f"i{c}")
                        e_st.wait(pe, b, c)
                        for q in range(G):
                            last = nc.tensor.matmul(bank[:, q * HG * HD:(q + 1) * HG * HD], qT[c % 3][:, q, :],
                                                    St[c % 2][:, HG * q:HG * (q + 1), :].rearrange("p a b -> p (a b)"), start=True, stop=True)
                        banks.filled(last, f"i{c}")

                    def turn_back(c):
                        bank = fill(f"o{c}")
                        e_oT.wait(pe, b, c)
                        for q in range(G):
                            last = nc.tensor.transpose(bank[:, q * P:(q + 1) * P], oT[:, q * P:(q + 1) * P], g.ident[:, :])
                        banks.filled(last, f"o{c}")

                    turn(0)
                    for c in range(C):
                        if c + 1 < C:
                            turn(c + 1)
                        e_qT.wait(pe, b, c)
                        e_kT.wait(pe, b, c)
                        e_FN.wait(pe, b, c // 4)
                        for q in range(G):
                            bank = fill(f"S{c}{q}")
                            e_Qd.wait(pe, b, c * G + q)
                            last = nc.tensor.matmul(bank[:, :], kT[c % 3][:, q, :], Qd[q].rearrange("p h t -> p (h t)"), start=True, stop=True)
                            banks.filled(last, f"S{c}{q}")
                            bank = fill(f"G{c}{q}")
                            nc.tensor.matmul(bank[:, :], identb[:, :], later[:, :], start=True, stop=False)
                            for j in range(HG):
                                h = HG * q + j
                                nc.tensor.matmul(bank[:, j * P:(j + 1) * P], heads[:, h * P:(h + 1) * P], FP[:, c * P:(c + 1) * P],
                                                 start=False, stop=False, skip_group_check=True)
                            last = nc.tensor.matmul(bank[:, :], FN[:, c * P:(c + 1) * P], heads[:, q * HALF:(q + 1) * HALF],
                                                    start=False, stop=True)
                            banks.filled(last, f"G{c}{q}")
                            if c and q == 1:
                                intra(c - 1)
                                inter(c - 1)
                            if c and q == 2:
                                turn_back(c - 1)
                        bank = fill(f"U{c}")
                        e_kt.wait(pe, b, c)
                        e_v.wait(pe, b, c)
                        for q in range(G):
                            w = slice(q * HG * HD, (q + 1) * HG * HD)
                            last = nc.tensor.matmul(bank[:, w], ktil[c % 2][:, HG * q:HG * (q + 1), :].rearrange("p a b -> p (a b)"),
                                                    v2[:, c * D + q * HG * HD:c * D + (q + 1) * HG * HD], start=True, stop=True)
                        banks.filled(last, f"U{c}")
                    intra(C - 1)
                    inter(C - 1)
                    turn_back(C - 1)
                    for jp in range(4):
                        bank = fill(f"n{jp}")
                        for jj in range(2):
                            e_on.wait(pe, b, 2 * jp + jj)
                            for c in range(DC):
                                last = nc.tensor.transpose(bank[:, c * 256 + jj * P:c * 256 + jj * P + P],
                                                           og[:, 2 * jp + jj, c * P:(c + 1) * P], g.ident[:, :])
                        banks.filled(last, f"n{jp}")
                    for jp in range(4):
                        e_onT.wait(pe, b, jp)
                        bank = fill(f"W{jp}")
                        for jj in range(2):
                            for k in range(DC):
                                last = nc.tensor.matmul(bank[:, jj * D:(jj + 1) * D], onT[jp % 2][:, k * 256 + jj * P:k * 256 + jj * P + P],
                                                        WoT[:, k, :], start=(k == 0), stop=(k == DC - 1))
                        banks.filled(last, f"W{jp}")

            @block.scalar
            def _(a):
                with a.Fori(0, B) as b:
                    read = lambda name: banks.read(a, b, name)
                    for jp in range(4):
                        bank = read(f"x{jp}")
                        if jp == 0:
                            e_og.wait_all_before(a, b)
                        a.activation(xnT[:, :, jp * 256:(jp + 1) * 256], bank[:, :].rearrange("p (c t) -> p c t", c=DC),
                                     ACT.Copy).then_inc(e_xT.sem, 1)
                        e_xT.wait(a, b, jp)
                        banks.released(a, f"x{jp}")
                    bank = read("zf")
                    e_f3.wait_all_before(a, b)
                    a.activation(zc[:, :], bank[:, 0:C * H], ACT.Copy).then_inc(e_zc.sem, 1)
                    e_zc.wait(a, b, 0)
                    banks.released(a, "zf")
                    a.activation(za[:, :], zc[:, :], ACT.Abs).then_inc(e_za.sem, 1)
                    for h in range(2):
                        bank = read(f"g{h}")
                        a.activation(g1T[:, h * HALF:(h + 1) * HALF], bank[0:HD, :], ACT.Copy).then_inc(e_g1.sem, 1)
                        e_g1.wait(a, b, h)
                        banks.released(a, f"g{h}")
                    e_za.wait(a, b, 0)
                    a.activation(ze[:, :], za[:, :], ACT.Exp, scale=-1.0).then_inc(e_ze.sem, 1)
                    for c in range(C):
                        bank = read(f"qk{c}")
                        if c >= 2:
                            e_k.wait(a, b, c - 2)
                        elif c == 0:
                            e_x.wait_all_before(a, b)
                        a.activation(th[c % 2][:, :], bank[:, :], ACT.Tanh, scale=0.5).then_inc(e_th.sem, 1)
                        bank = read(f"vg{c}")
                        if c >= 2:
                            e_v.wait(a, b, c - 2)
                        a.activation(tv[:, c % 2, :], bank[:, 0:D], ACT.Tanh, scale=0.5)
                        a.activation(gt[:, c, :], bank[:, D:2 * D], ACT.Tanh, scale=0.5).then_inc(e_tv.sem, 1)
                    a.activation(zl[:, :], ze[:, :], ACT.Ln, bias=1.0).then_inc(e_zl.sem, 1)
                    e_n2.wait(a, b, 0)
                    a.activation(nl[:, :], n2[:, :], ACT.Ln, scale=float(2 ** 20)).then_inc(e_nl.sem, 1)
                    e_nl.wait(a, b, 0)
                    a.activation(ny[:, :], nl[:, :], ACT.Exp, scale=-0.5).then_inc(e_ny.sem, 1)
                    bank = read("Fn")
                    e_kt.wait_all_before(a, b)
                    a.activation(Ft[:, :], bank[:, C * H:2 * C * H], ACT.Copy).then_inc(e_Ft.sem, 1)
                    a.activation(eF[:, :], bank[:, 0:C * H], ACT.Exp).then_inc(e_Ft.sem, 1)
                    a.activation(dec[:, :], bank[:, C * H:2 * C * H], ACT.Exp).then_inc(e_Ft.sem, 1)
                    for h in range(2):
                        bank = read(f"FT{h}")
                        if h:
                            e_FP.wait(a, b, 0)
                        a.activation(ftv[:, :], bank[0:96, :], ACT.Copy).then_inc(e_ftv.sem, 1)
                        e_ftv.wait(a, b, h)
                        banks.released(a, f"FT{h}")
                        if h == 0:
                            e_dF.wait(a, b, 0)
                            a.activation(wk[:, :], dF[:, :], ACT.Exp).then_inc(e_wk.sem, 1)

                    def negate(h):
                        e_FP.wait(a, b, h)
                        a.activation(FN[:, h * HALF:(h + 1) * HALF], FP[:, h * HALF:(h + 1) * HALF], ACT.Copy, scale=-1.0).then_inc(e_FN.sem, 1)

                    def copies(c):
                        for name, out, e in (("qT", qT, e_qT), ("kT", kT, e_kT)):
                            bank = read(f"{name}{c}")
                            if c >= 3:
                                e_og.wait(a, b, c - 3)
                            a.activation(out[c % 3][:, :, :], bank[:, :].rearrange("p (g t) -> p g t", g=G), ACT.Copy).then_inc(e.sem, 1)
                            e.wait(a, b, c)
                            banks.released(a, f"{name}{c}")

                    def copy_intra(c):
                        bank = read(f"t{c}")
                        if c:
                            e_og.wait(a, b, c - 1)
                        a.activation(oT[:, :], bank[:, :], ACT.Copy).then_inc(e_oT.sem, 1)
                        e_oT.wait(a, b, c)
                        banks.released(a, f"t{c}")

                    copies(0)
                    negate(0)
                    for c in range(C):
                        if c + 1 < C:
                            copies(c + 1)
                        for q in range(G):
                            n = c * G + q
                            bank = read(f"G{c}{q}")
                            if n >= 2:
                                e_A.wait(a, b, n - 2)
                            else:
                                e_A.wait_all_before(a, b)
                            a.activation(Dg[q % 2][:, :, :], bank[:, :].rearrange("p (h t) -> p h t", h=HG), ACT.Exp).then_inc(e_D.sem, 1)
                            e_D.wait(a, b, n)
                            banks.released(a, f"G{c}{q}")
                            if c and q == 1:
                                copy_intra(c - 1)
                        if c == 0:
                            negate(1)
                    copy_intra(C - 1)
                    e_bv.wait(a, b, 0)
                    a.activation(bl[:, :], bve[:, :], ACT.Ln).then_inc(e_bl.sem, 1)
                    e_bl.wait(a, b, 0)
                    a.activation(by[:, :], bl[:, :], ACT.Exp, scale=-0.5).then_inc(e_by.sem, 1)
                    for jp in range(4):
                        bank = read(f"n{jp}")
                        if jp >= 2:
                            read(f"W{jp - 2}")
                        a.activation(onT[jp % 2][:, :], bank[:, :], ACT.Copy).then_inc(e_onT.sem, 1)
                        e_onT.wait(a, b, jp)
                        banks.released(a, f"n{jp}")

            @block.gpsimd
            def _(p_):
                w = Waits(p_, s_tick)
                with p_.Fori(0, B) as b:
                    w.ge(e_wk.sem, b + 1)
                    w.ge(e_kp.sem, b + 1)

                    def spread(c):
                        w.ge(e_qT.sem, b * C + c + 1)
                        for q in range(G):
                            if c:
                                bq_, k = banks.where[f"S{c - 1}{q}"]
                                w.ge(banks.full[bq_], b * banks.uses[bq_] + k + 1)
                            p_.tensor_tensor(Qd[q], qT[c % 3][:, q, :].unsqueeze(1).broadcast_to([P, HG, P]),
                                             hmask[:, :].unsqueeze(2).broadcast_to([P, HG, P]), ALU.mult).then_inc(e_Qd.sem, 1)

                    spread(0)
                    for c in range(C):
                        if c >= 2:
                            w.ge(e_U.sem, b * C + c - 1)
                        wide = wk[:, c * H:(c + 1) * H].unsqueeze(2).broadcast_to([P, H, HD])
                        p_.tensor_tensor(ktil[c % 2][:, :, 0:HD], kpad[:, c * H:(c + 1) * H, 0:HD], wide, ALU.mult).then_inc(e_kt.sem, 1)
                        if c + 1 < C:
                            spread(c + 1)

            @block.vector
            def _(v):
                c0 = Tally(s_dv)
                until(v, s_w, 16 * len(loads))
                for t in (qpad, kpad):
                    c0.inc(v.memset(t[:, :, :], 0.0))
                for t in ktil:
                    c0.inc(v.memset(t[:, :, :], 0.0))
                c0.inc(v.memset(f3[:, :, :, :], 0.0))
                c0.inc(v.memset(v2[:, C * D:], 0.0))
                for c in range(DC):
                    c0.inc(v.tensor_scalar(WoT[:, c, :], WoT[:, c, :], lnw[:, c:c + 1], None, ALU.mult))
                until(v, s_dv, c0.n)
                v.sem_inc(s_pre, 1)
                pre = c0.n
                PER = 8
                with v.Fori(0, B) as b:
                    t_ = Tally(s_dv, pre + b * PER)
                    read = lambda name: banks.read(v, b, name)
                    for j in range(C):
                        if j >= 4:
                            banks.read(v, b, f"x{(j - 4) // 2}")
                        norm_tile(v, g, xn[j % 4], b * TB + j).then_inc(e_xn.sem, 1)
                    v.memset(St[0][:, :, :], 0.0).then_inc(e_st.sem, 1)
                    e_zc.wait(v, b, 0)
                    v.tensor_scalar(zr[:, :], zc[:, :], -1.0, 0.0, ALU.mult, ALU.max).then_inc(e_zr.sem, 1)
                    e_zr.wait(v, b, 0)
                    for c in range(C):
                        e_th.wait(v, b, c)
                        bank = read(f"qk{c}")
                        hv = lambda ap: ap.rearrange("p (h k) -> p h k", h=H)
                        v.scalar_tensor_tensor(qpad[:, c * H:(c + 1) * H, 0:HD], hv(th[c % 2][:, 0:D]), 1.0, hv(bank[:, 0:D]),
                                               ALU.add, ALU.mult).then_inc(e_q.sem, 1)
                        v.scalar_tensor_tensor(kpad[:, c * H:(c + 1) * H, 0:HD], hv(th[c % 2][:, D:2 * D]), 1.0, hv(bank[:, D:2 * D]),
                                               ALU.add, ALU.mult).then_inc(e_k.sem, 1)
                        e_k.wait(v, b, c)
                        e_q.wait(v, b, c)
                        banks.released(v, f"qk{c}")
                        e_tv.wait(v, b, c)
                        bank = read(f"vg{c}")
                        v.scalar_tensor_tensor(v2[:, c * D:(c + 1) * D], tv[:, c % 2, :], 1.0, bank[:, 0:D], ALU.add, ALU.mult).then_inc(e_v.sem, 1)
                        e_v.wait(v, b, c)
                        banks.released(v, f"vg{c}")
                    link(v, t_, v.tensor_tensor(sq, kpad[:, :, 0:HD], kpad[:, :, 0:HD], ALU.mult))
                    link(v, t_, v.tensor_reduce(n2[:, :], sq, AX.X, ALU.add))
                    v.tensor_scalar(n2[:, :], n2[:, :], 4e-24, None, ALU.max).then_inc(e_n2.sem, 1)
                    e_zl.wait(v, b, 0)
                    link(v, t_, v.scalar_tensor_tensor(f[:, :], zr[:, :], -1.0, zl[:, :], ALU.mult, ALU.subtract))
                    wide = f[:, :].rearrange("p (c h) -> p c h", c=C).unsqueeze(2).broadcast_to([P, C, 3, H])
                    v.tensor_copy(f3[:, :, :, 0:H], wide).then_inc(e_f3.sem, 1)
                    e_ny.wait(v, b, 0)
                    link(v, t_, v.tensor_scalar(ny[:, :], ny[:, :], 1024.0, None, ALU.mult))
                    link(v, t_, v.tensor_tensor(nt[:, :], ny[:, :], ny[:, :], ALU.mult))
                    link(v, t_, v.tensor_tensor(nt[:, :], nt[:, :], n2[:, :], ALU.mult))
                    link(v, t_, v.tensor_scalar(nt[:, :], nt[:, :], -0.5, 1.5, ALU.mult, ALU.add))
                    link(v, t_, v.tensor_tensor(rn[:, :], nt[:, :], ny[:, :], ALU.mult))
                    v.tensor_tensor(kpad[:, :, 0:HD], kpad[:, :, 0:HD], rn[:, :].unsqueeze(2).broadcast_to([P, C * H, HD]), ALU.mult).then_inc(e_kp.sem, 1)
                    bank = read("Fn")
                    e_Ft.wait(v, b, 2)
                    v.tensor_tensor(dF[:, :], Ft[:, :], bank[:, 0:C * H], ALU.subtract).then_inc(e_dF.sem, 1)
                    e_dF.wait(v, b, 0)
                    banks.released(v, "Fn")
                    c_ = Tally(s_split, b * 8)
                    for h in range(2):
                        e_ftv.wait(v, b, h)
                        fp, fv, r = FP[:, h * HALF:(h + 1) * HALF], ftv[:, :], ftr[:, :]
                        link(v, c_, v.tensor_copy(fp, fv))
                        link(v, c_, v.tensor_tensor(r, fv, fp, ALU.subtract))
                        c_.inc(v.tensor_copy(fp[32:64, :], r[32:64, :]))
                        link(v, c_, v.tensor_copy(fp[64:96, :], r[64:96, :]))
                        v.tensor_tensor(fp[64:96, :], r[64:96, :], fp[64:96, :], ALU.subtract).then_inc(e_FP.sem, 1)
                        e_FP.wait(v, b, h)

                    def out_of(c):
                        held, turned = read(f"i{c}"), read(f"o{c}")
                        hv = lambda ap: ap.rearrange("p (h k) -> p h k", h=H)
                        t1 = o1[c % 2]
                        link(v, t8, v.tensor_tensor(t1[:, :, :], hv(held[:, 0:D]), eF[:, c * H:(c + 1) * H].unsqueeze(2).broadcast_to([P, H, HD]), ALU.mult))
                        link(v, t8, v.tensor_tensor(t1[:, :, :], t1[:, :, :], turned[:, :].rearrange("p (h k) -> p h k", k=HP)[:, :, 0:HD], ALU.add))
                        banks.released(v, f"i{c}")
                        banks.released(v, f"o{c}")
                        v.scalar_tensor_tensor(og[:, c, :], gt[:, c, :], 1.0, flat(t1), ALU.add, ALU.mult).then_inc(e_og.sem, 1)
                        e_og.wait(v, b, c)
                        v.bn_stats(bst[:, c, :], og[:, c, :]).then_inc(e_tp.sem, 1)

                    t8 = Tally(s_pre8, b * (C * 4))
                    for c in range(C):
                        for q in range(G):
                            n = c * G + q
                            e_D.wait(v, b, n)
                            bank = read(f"S{c}{q}")
                            if c >= 2:
                                e_oT.wait(v, b, c - 2)
                            v.tensor_tensor(Ag[(c % 2) * G + q], bank[:, :].rearrange("p (h t) -> p h t", h=HG), Dg[q % 2][:, :, :],
                                            ALU.mult).then_inc(e_A.sem, 1)
                            e_A.wait(v, b, n)
                            banks.released(v, f"S{c}{q}")
                        bank = read(f"U{c}")
                        e_st.wait(v, b, c)
                        t8.inc(v.tensor_tensor(Um[:, :, :], bank[:, 0:D].rearrange("p (h k) -> p h k", h=H),
                                               bmask[:, :].rearrange("p (h k) -> p h k", h=H), ALU.mult))
                        link(v, t8, v.tensor_tensor(Sd[:, :, :], St[c % 2][:, :, :],
                                                    dec[:, c * H:(c + 1) * H].unsqueeze(2).broadcast_to([P, H, HD]), ALU.mult))
                        banks.released(v, f"U{c}")
                        v.sem_inc(e_U.sem, 1)
                        if c:
                            read(f"i{c - 1}")
                        v.tensor_tensor(St[(c + 1) % 2][:, :, :], Sd[:, :, :], Um[:, :, :], ALU.add).then_inc(e_st.sem, 1)
                        if c:
                            out_of(c - 1)
                    out_of(C - 1)
                    e_tp.wait(v, b, C - 1)
                    u = Tally(s_ln, b * 10)
                    u.inc(v.tensor_tensor(bdm[:, :], bst[:, :, 1], bst[:, :, 4], ALU.subtract))
                    u.inc(v.tensor_tensor(bq[:, :], bst[:, :, 1], bst[:, :, 4], ALU.add))
                    link(v, u, v.tensor_tensor(bve[:, :], bst[:, :, 2], bst[:, :, 5], ALU.add))
                    u.inc(v.tensor_scalar(bmean[:, :], bq[:, :], 0.5, None, ALU.mult))
                    link(v, u, v.tensor_tensor(bdm[:, :], bdm[:, :], bdm[:, :], ALU.mult))
                    link(v, u, v.tensor_scalar(bdm[:, :], bdm[:, :], 0.25, 64 * EPS, ALU.mult, ALU.add))
                    v.scalar_tensor_tensor(bve[:, :], bve[:, :], 1.0 / D, bdm[:, :], ALU.mult, ALU.add).then_inc(e_bv.sem, 1)
                    e_by.wait(v, b, 0)
                    link(v, u, v.tensor_tensor(bt[:, :], by[:, :], by[:, :], ALU.mult))
                    link(v, u, v.tensor_tensor(bt[:, :], bt[:, :], bve[:, :], ALU.mult))
                    link(v, u, v.tensor_scalar(bt[:, :], bt[:, :], -0.5, 1.5, ALU.mult, ALU.add))
                    link(v, u, v.tensor_tensor(brs[:, :], bt[:, :], by[:, :], ALU.mult))
                    for c in range(C):
                        v.tensor_scalar(og[:, c, :], og[:, c, :], bmean[:, c:c + 1], brs[:, c:c + 1], ALU.subtract, ALU.mult).then_inc(e_on.sem, 1)
                    for jp in range(4):
                        bank = read(f"W{jp}")
                        xr = g.xres[:, bass.ds(b * TB + 2 * jp, 2), :]
                        v.tensor_tensor(xr, xr, bank[:, :].rearrange("p (j d) -> p j d", j=2), ALU.add).then_inc(e_x.sem, 1)
                        e_x.wait(v, b, jp)
                        banks.released(v, f"W{jp}")


class Globals:
    pass


def hybrid_program(nc, dram, phases=("ssm", "ffn", "gla", "ffn2")):
    with ExitStack() as stack:
        m = Mem(nc, stack, "g_")
        g = Globals()
        g.xres = m.sb("xres", [P, NT, D])
        g.mean = m.sb("mean", [P, NT])
        g.rstd = m.sb("rstd", [P, NT])
        g.ident = m.sb("ident", [P, P])
        g.gidx = m.sb("gidx", [P, NT], U32)
        g.fe = m.sb("fe", [P, NT])
        g.nk = m.sb("nk", [P, NT])
        dram["slots"] = nc.dram_tensor("slots", (SLOTS, D), F32).ap()
        dram["eout"] = nc.dram_tensor("eout", (E * CAP, D), F32).ap()
        load_inputs(nc, g, dram)
        fill_slots(nc, g, dram)
        if "ssm" in phases:
            norm_stats(nc, g, "n1_")
            ssm_layer(nc, g, dram)
        if "ffn" in phases:
            moe_layer(nc, g, dram, "f1")
        if "gla" in phases:
            norm_stats(nc, g, "n3_")
            gla_layer(nc, g, dram)
        if "ffn2" in phases:
            moe_layer(nc, g, dram, "f2")
        s_out = m.sem("s_out")
        m.start()
        with nc.Block() as block:
            @block.sync
            def _(sp):
                for b in range(B):
                    sp.dma_start(dram["out"][S * b:S * b + S, :].rearrange("(i p) d -> p i d", p=P),
                                 g.xres[:, TB * b:TB * b + TB, :]).then_inc(s_out, 16)
                until(sp, s_out, 16 * B)


def constants():
    rep = np.zeros((96, 2 * NS, P), np.float32)
    for n in range(2 * NS):
        for part in range(3):
            rep[32 * part + n, n, :] = 1
    reset = np.ones((P, E, NT), np.float32)
    reset[:, :, 0] = 0
    tri = np.triu(np.ones((P, P), np.float32))
    heads = np.zeros((96, H, P), np.float32)
    for h in range(H):
        heads[[h, 32 + h, 64 + h], h, :] = 1
    later = np.where(np.arange(P)[:, None] > np.arange(P)[None, :], np.float32(NEG), np.float32(0))
    bmask = np.zeros((4, 32, 4, 4, HD), np.float32)
    for h in range(4):
        bmask[h, :, :, h, :] = 1
    hmask = (np.arange(P)[:, None] // 32 == np.arange(4)[None, :]).astype(np.float32)
    bits = lambda w: (np.ascontiguousarray(w, np.float32).view(np.uint32) >> 16).astype(np.uint16)
    return {"trif": tri, "onef": np.ones((P, P), np.float32), "identb": bits(np.eye(P)),
            "later": bits(np.tile(later, (1, 4))), "heads": bits(heads.reshape(96, -1)), "bmask": bmask.reshape(P, D), "hmask": hmask,
            "tri": bits(tri), "oneb": bits(np.ones((P, P))), "reset": reset.reshape(P, E * NT),
            "jrow": np.tile(np.arange(E, dtype=np.float32), (P, 1)),
            "trash": (E * CAP + np.arange(P, dtype=np.float32))[:, None],
            "ident": np.eye(P, dtype=np.float32), "rep": bits(rep.reshape(96, -1))}


def layout(i):
    a = {k: np.asarray(v) for k, v in i.items()}
    A, L = "L0_attn_a_", "L0_attn_b_"
    tr = lambda w: np.ascontiguousarray(w.T)
    by_chunk = lambda w: np.ascontiguousarray(w.reshape(DC, P).T)
    d = {"x": a[A + "x"].reshape(T, D), "dWT": tr(a[A + "delta_W"]),
         "bcT": np.ascontiguousarray(np.tile(np.concatenate([a[A + "B_W"], a[A + "C_W"]], 0).T, (1, 3))),
         "bcb": np.ascontiguousarray(np.tile(np.concatenate([a[A + "B_b"], a[A + "C_b"]]), 3)[:, None]),
         "delta_b": by_chunk(a[A + "delta_b"]), "dt_bias": by_chunk(a[A + "dt_bias"]), "A_log": a[A + "A_log"],
         "WiT": tr(a[A + "Wi_W"]), "Wi_b": a[A + "Wi_b"][:, None], "WrT": tr(a[A + "Wr_W"]), "h0": tr(a[A + "h0"]),
         "tau": a[A + "tau"][:, None], "selWT": tr(a[A + "sel_W"]), "sel_b": by_chunk(a[A + "sel_b"])}
    F = "L0_ffn_"
    d.update({"Wr": a[F + "Wr"], "W1": a[F + "W1"].reshape(E * D, FF), "W2": a[F + "W2"].reshape(E * FF, D)})
    d.update({"Wqkv": np.concatenate([a[L + "Wq"], a[L + "Wk"], a[L + "Wv"]], 0).T.copy(), "WfT": tr(a[L + "Wf"]),
              "Wg1T": tr(a[L + "Wg1"]), "Wg2T": tr(a[L + "Wg2"]), "WoT": tr(a[L + "Wo"]), "ln_w": by_chunk(a[L + "ln_w"])})
    d.update(constants())
    return d


PHASES = ("ssm", "ffn", "gla", "ffn2")


def kernel(**inputs):
    import concourse.bacc as bacc
    from concourse.bass_utils import run_bass_kernel_spmd

    nc = bacc.Bacc("TRN2", target_bir_lowering=False, num_devices=1)
    arrays, dram = {}, {}
    for name, a in layout(inputs).items():
        arrays[f"in_{name}"] = a
        dram[name] = nc.dram_tensor(f"in_{name}", a.shape, mybir.dt.from_np(a.dtype), kind="ExternalInput").ap()
    dram["out"] = nc.dram_tensor("out_x", (T, D), F32, kind="ExternalOutput").ap()
    hybrid_program(nc, dram, PHASES)
    r = run_bass_kernel_spmd(nc, [arrays], core_ids=[0])
    return r.results[0]["out_x"].reshape(B, S, D)
```

```python
from contextlib import ExitStack

import numpy as np

import concourse.bass as bass
from concourse import mybir

ALU = mybir.AluOpType
ACT = mybir.ActivationFunctionType
AX = mybir.AxisListType
F32 = mybir.dt.float32
BF16 = mybir.dt.bfloat16
U32 = mybir.dt.uint32

P = 128
B, S, D = 8, 1024, 256
T = B * S
NT = T // P
TB = S // P
DC = D // P
NS = 16
E, FF = 8, 1024
FC = FF // P
CAP = int(1.25 * T / E)
GROUP = 8
FILL = 3
SLOTS = E * CAP + P
H, HD = 16, 16
HALF = 512
DT = 0.1
EPS = 1e-5
NEG = -1e30


def until(eng, sem, value):
    eng.wait_ge(sem, value + 1)


def until_moved(eng, sem, value):
    eng.wait_ge(sem, value)


class Tally:

    def __init__(self, sem, base=0):
        self.sem, self.base, self.n = sem, base, 0

    def inc(self, ins, k=1):
        ins.then_inc(self.sem, k)
        self.n += k
        return ins

    def here(self):
        return self.base + self.n


def link(eng, tally, ins):
    tally.inc(ins)
    until(eng, tally.sem, tally.here())


class Waits:

    def __init__(self, eng, tick):
        self.eng, self.tick = eng, tick

    def ge(self, sem, value):
        until(self.eng, sem, value)
        self.eng.sem_inc(self.tick, 1)

    def link(self, tally, ins):
        tally.inc(ins)
        self.ge(tally.sem, tally.here())


class Mem:

    def __init__(self, nc, stack, tag):
        self.nc, self.stack, self.tag, self.sems, self.ordinary = nc, stack, tag, [], []
        stack.callback(self.clear)

    def sb(self, name, shape, dt=F32):
        return self.stack.enter_context(self.nc.sbuf_tensor(self.tag + name, shape, dt))

    def ps(self, name, shape=(P, HALF), dt=F32):
        return self.stack.enter_context(self.nc.psum_tensor(self.tag + name, list(shape), dt))

    def sem(self, name, moved=False):
        self.sems.append(self.nc.alloc_semaphore(self.tag + name))
        if not moved:
            self.ordinary.append(self.sems[-1])
        return self.sems[-1]

    def start(self):
        for s in self.ordinary:
            self.nc.sync.sem_inc(s, 1)
        self.nc.all_engine_barrier()

    def clear(self):
        if self.sems:
            self.nc.clear_and_free_semaphores(self.sems)
            self.nc.all_engine_barrier()


def start_loads(nc, g, dram, s_x, s_ident):
    for b in range(B):
        nc.sync.dma_start(g.xres[:, TB * b:TB * b + TB, :],
                          dram["x"][S * b:S * b + S, :].rearrange("(i p) d -> p i d", p=P)).then_inc(s_x[b], 16)
    nc.sync.dma_start(g.ident[:, :], dram["ident"]).then_inc(s_ident, 16)


def start_fill(nc, dram, zero, s_z, s_fill):
    rows = SLOTS // P
    nc.vector.memset(zero[:, :], 0.0).then_inc(s_z, 1)
    until(nc.sync, s_z, 1)
    view = dram["slots"].rearrange("(p r) d -> p (r d)", r=rows)
    for k in range(rows // FILL):
        nc.sync.dma_start(view[:, k * FILL * D:(k + 1) * FILL * D], zero[:, :]).then_inc(s_fill, 16)


def norm_stats(nc, g, tag, s_x=None, s_ident=None):
    with ExitStack() as stack:
        m = Mem(nc, stack, tag)
        st = m.sb("st", [P, NT, 6])
        dm, q, ve, ln, y0, yy = (m.sb(n, [P, NT]) for n in ("dm", "q", "ve", "ln", "y0", "yy"))
        s_dv, s_ve, s_y0 = m.sem("s_dv"), m.sem("s_ve"), m.sem("s_y0")
        m.start()
        with nc.Block() as block:
            @block.vector
            def _(v):
                c = Tally(s_dv)
                for b in range(B):
                    if s_x:
                        until(v, s_x[b], 16)
                    with v.Fori(TB // 4 * b, TB // 4 * (b + 1)) as i:
                        for j in range(4):
                            v.bn_stats(st[:, bass.ds(4 * i + j, 1), :], g.xres[:, bass.ds(4 * i + j, 1), :]).then_inc(s_dv, 1)
                c.n = NT
                until(v, s_dv, NT)
                c.inc(v.tensor_tensor(dm[:, :], st[:, :, 1], st[:, :, 4], ALU.subtract))
                c.inc(v.tensor_tensor(q[:, :], st[:, :, 1], st[:, :, 4], ALU.add))
                link(v, c, v.tensor_tensor(ve[:, :], st[:, :, 2], st[:, :, 5], ALU.add))
                c.inc(v.tensor_scalar(g.mean[:, :], q[:, :], 0.5, None, ALU.mult))
                link(v, c, v.tensor_tensor(dm[:, :], dm[:, :], dm[:, :], ALU.mult))
                link(v, c, v.tensor_scalar(dm[:, :], dm[:, :], 0.25, EPS, ALU.mult, ALU.add))
                v.scalar_tensor_tensor(ve[:, :], ve[:, :], 1.0 / D, dm[:, :], ALU.mult, ALU.add).then_inc(s_ve, 1)
                until(v, s_y0, 1)
                c.n += 1
                link(v, c, v.tensor_tensor(yy[:, :], y0[:, :], y0[:, :], ALU.mult))
                link(v, c, v.tensor_tensor(yy[:, :], yy[:, :], ve[:, :], ALU.mult))
                link(v, c, v.tensor_scalar(yy[:, :], yy[:, :], -0.5, 1.5, ALU.mult, ALU.add))
                link(v, c, v.tensor_tensor(g.rstd[:, :], yy[:, :], y0[:, :], ALU.mult))

            if s_ident:
                @block.sync
                def _(sp):
                    until(sp, s_ident, 16)

            @block.scalar
            def _(a):
                a.preload_act_table_set("natural_log_exp_and_others")
                until(a, s_ve, 1)
                a.activation(ln[:, :], ve[:, :], ACT.Ln).then_inc(s_dv, 1)
                until(a, s_dv, NT + 7)
                a.activation(y0[:, :], ln[:, :], ACT.Exp, scale=-0.5).then_inc(s_y0, 1)


def norm_tile(v, g, out, i):
    return v.tensor_scalar(out, g.xres[:, bass.ds(i, 1), :], g.mean[:, bass.ds(i, 1)], g.rstd[:, bass.ds(i, 1)],
                           ALU.subtract, ALU.mult)


def ssm_layer(nc, g, dram):
    with ExitStack() as stack:
        m = Mem(nc, stack, "ssm_")
        dWT = m.sb("dWT", [P, DC, D])
        bcT = m.sb("bcT", [P, DC, 96])
        bcb = m.sb("bcb", [96, 1])
        db = m.sb("db", [P, DC])
        db2 = m.sb("db2", [P, DC])
        alog = m.sb("alog", [P, DC, NS])
        absA = m.sb("absA", [P, DC, NS])
        negA = m.sb("negA", [P, DC, NS])
        tiny = m.sb("tiny", [P, DC, NS])
        rest = m.sb("rest", [P, DC, NS])
        invA = m.sb("invA", [P, DC, NS])
        rep = m.sb("rep", [96, 2 * NS, P], BF16)
        WiT = m.sb("WiT", [P, DC, NS])
        Wib = m.sb("Wib", [NS, 1])
        WrT = m.sb("WrT", [NS, NS])
        h0 = m.sb("h0", [NS, 1])
        tau = m.sb("tau", [NS, 1])
        dtau = m.sb("dtau", [NS, 1])
        bias2 = m.sb("bias2", [NS, 1])
        selWT = m.sb("selWT", [NS, D])
        selb = m.sb("selb", [P, DC])
        nselb = m.sb("nselb", [P, DC])
        ones = m.sb("ones", [P, 1])
        tsum = m.sb("tsum", [P, 1])
        flag = m.sb("flag", [1, 1], U32)
        xn = [m.sb(f"xn{j}", [P, D]) for j in range(2)]
        xnT = m.sb("xnT", [P, DC, S])
        gp = m.sb("gp", [P, DC, 4])
        gcs = m.sb("gcs", [P, DC])
        nh = [m.sb(f"nh{j}", [NS, 1]) for j in range(5)]
        es = [m.sb(f"es{j}", [P, DC]) for j in range(3)]
        xs2 = [m.sb(f"xs{j}", [P, DC, S]) for j in range(2)]
        delta2 = [m.sb(f"delta{j}", [P, DC, S]) for j in range(2)]
        ab = m.sb("ab", [P, 2, HALF])
        ee = m.sb("ee", [P, 2, HALF])
        ll = m.sb("ll", [P, 2, HALF])
        dd = m.sb("dd", [P, 2, HALF])
        bcv = m.sb("bcv", [96, 2, HALF])
        br = m.sb("br", [96, 2, HALF])
        parts2 = [m.sb(f"parts{j}", [96, S], BF16) for j in range(2)]
        bcs = m.sb("bcs", [P, 2, 2, S])
        Ad = m.sb("Ad", [P, DC, S])
        u = m.sb("u", [P, DC, S])
        hh = m.sb("hh", [P, DC, S])
        hc = m.sb("hc", [P, DC, S])
        ysb = xnT
        ring = [m.ps(f"ring{j}") for j in range(2)]
        misc = [m.ps(f"misc{j}") for j in range(2)]
        yps = m.ps("yps", [P, DC, 2, HALF])

        s_w, s_pre, s_prep, s_flag = m.sem("s_w"), m.sem("s_pre"), m.sem("s_prep"), m.sem("s_flag")
        s_dv, s_xn, s_tp, s_use, s_free = m.sem("s_dv"), m.sem("s_xn"), m.sem("s_tp"), m.sem("s_use"), m.sem("s_free")
        s_gc, s_z, s_nh, s_es, s_xs = m.sem("s_gc"), m.sem("s_z"), m.sem("s_nh"), m.sem("s_es"), m.sem("s_xs")
        s_act, s_ll, s_dl = m.sem("s_act"), m.sem("s_ll"), m.sem("s_dl")
        s_bcv, s_rest, s_low, s_pt, s_bc, s_ev = (m.sem(n) for n in ("s_bcv", "s_rest", "s_low", "s_pt", "s_bc", "s_ev"))
        s_ad, s_xb, s_u, s_h, s_hc, s_y = (m.sem(n) for n in ("s_ad", "s_xb", "s_u", "s_h", "s_hc", "s_y"))
        s_yev, s_yt = m.sem("s_yev"), m.sem("s_yt")

        loads = [(dWT[:, :, :], dram["dWT"].rearrange("(c p) n -> p c n", p=P)),
                 (bcT[:, :, :], dram["bcT"].rearrange("(c p) n -> p c n", p=P)),
                 (bcb[:, :], dram["bcb"]),
                 (db[:, :], dram["delta_b"]),
                 (db2[:, :], dram["dt_bias"]),
                 (alog[:, :, :], dram["A_log"].rearrange("(c p) n -> p c n", p=P)),
                 (rep[:, :, :], dram["rep"].bitcast(BF16).rearrange("k (n q) -> k n q", q=P)),
                 (WiT[:, :, :], dram["WiT"].rearrange("(c p) n -> p c n", p=P)),
                 (Wib[:, :], dram["Wi_b"]),
                 (WrT[:, :], dram["WrT"]),
                 (h0[:, :], dram["h0"]),
                 (tau[:, :], dram["tau"]),
                 (selWT[:, :], dram["selWT"]),
                 (selb[:, :], dram["sel_b"])]
        T0, UZ, US, UD, UB, PREP, OUT = 0, 4, 5, 6, 10, 12, 4

        def prep_base(b):
            return 0 if isinstance(b, int) and b == 0 else b * (PREP + OUT) - OUT

        def y_base(b):
            return B * PREP + (B - 1) * OUT if isinstance(b, int) and b == B - 1 else b * (PREP + OUT) + 2 * PREP

        def run(eng, prepare, states, output, steps):
            prep0 = prepare(0, 0)
            for k in sorted(prep0):
                prep0[k]()

            def batch(b, par, first=False, last=False):
                todo = {}
                if not first:
                    todo.update({("y", k): f for k, f in output(b - 1).items()})
                if not last:
                    todo.update({("p", k): f for k, f in prepare(b + 1, 1 - par).items()})

                def after(n):
                    for key in steps.get(n, ()):
                        if key in todo:
                            todo.pop(key)()

                states(b, par, after)
                assert not todo

            batch(0, 0, first=True)
            with eng.Fori(0, (B - 2) // 2) as i:
                batch(i * 2 + 1, 1)
                batch(i * 2 + 2, 0)
            batch(B - 1, (B - 1) % 2, last=True)
            out = output(B - 1)
            for k in sorted(out):
                out[k]()

        m.start()
        with nc.Block() as block:
            @block.sync
            def _(sp):
                for out, src in loads:
                    sp.dma_start(out, src).then_inc(s_w, 16)

            @block.tensor
            def _(pe):
                until(pe, s_w, 16 * len(loads))
                nc.tensor.matmul(misc[0][0:NS, 0:1], WrT[:, :], h0[:, :], start=True, stop=True).then_inc(s_pre, 1)
                until(pe, s_prep, 2)
                nc.tensor.matmul(misc[1][0:1, 0:1], tsum[:, :], ones[:, :], start=True, stop=True).then_inc(s_pre, 1)
                until(pe, s_flag, 1)

                def prepare(b, par):
                    xs, base = xs2[par], prep_base(b)

                    def use(n, free):
                        until(pe, s_free, base + free)
                        return misc[n % 2]

                    def turn(jp):
                        bank = use(T0 + jp, max(jp - 1, 0))
                        for jj in range(2):
                            until(pe, s_xn, b * TB + 2 * jp + jj + 1)
                            for c in range(DC):
                                last = nc.tensor.transpose(bank[:, c * 256 + jj * P:c * 256 + jj * P + P],
                                                           xn[jj][:, c * P:c * P + P], g.ident[:, :])
                            last.then_inc(s_tp, 1)

                    def signal():
                        until(pe, s_gc, b + 1)
                        bank = use(UZ, UZ)
                        for c in range(DC):
                            last = nc.tensor.matmul(bank[0:NS, 0:1], WiT[:, c, :], gcs[:, c:c + 1], start=(c == 0), stop=(c == DC - 1))
                        last.then_inc(s_use, 1)

                    def select():
                        until(pe, s_nh, b + 1)
                        bank = use(US, US)
                        for c in range(DC):
                            last = nc.tensor.matmul(bank[:, c:c + 1], selWT[:, c * P:c * P + P], nh[4][:, :], start=True, stop=True)
                        last.then_inc(s_use, 1)

                    def steps(q):
                        until(pe, s_xs, b + 1)
                        c, h = q // 2, q % 2
                        bank = use(UD + q, UD + max(q - 1, 0))
                        for k in range(DC):
                            last = nc.tensor.matmul(bank[:, :], dWT[:, k, c * P:c * P + P], xs[:, k, h * HALF:(h + 1) * HALF],
                                                    start=(k == 0), stop=(k == DC - 1))
                        last.then_inc(s_use, 1)

                    def b_and_c(h):
                        bank = use(UB + h, UB + h - 1)
                        for k in range(DC):
                            last = nc.tensor.matmul(bank[0:96, :], bcT[:, k, :], xs[:, k, h * HALF:(h + 1) * HALF],
                                                    start=(k == 0), stop=(k == DC - 1))
                        last.then_inc(s_use, 1)

                    todo = [lambda jp=jp: turn(jp) for jp in range(4)] + [signal, select]
                    todo += [lambda k=k: steps(k) for k in range(4)] + [lambda h=h: b_and_c(h) for h in range(2)]
                    return dict(enumerate(todo))

                def states(b, par, after):
                    parts = parts2[par]

                    def reduce_states(n):
                        for c in range(DC):
                            until(pe, s_hc, b * 2 * NS + 2 * n + c + 1)
                            for h in range(2):
                                last = nc.tensor.matmul(yps[:, c, h, :], g.ident[:, :], hc[:, c, h * HALF:(h + 1) * HALF],
                                                        start=(n == 0), stop=(n == NS - 1))
                            last.then_inc(s_y, 1)

                    until(pe, s_pt, (b + 1) * 2)
                    for n in range(NS):
                        for q in range(4):
                            w, h = q // 2, q % 2
                            if n or q > 1:
                                until(pe, s_ev, b * 4 * NS + 4 * n + q - 1)
                            elif q == 0:
                                until(pe, s_ev, b * 4 * NS)
                            nc.tensor.matmul(ring[q % 2][:, :], rep[:, w * NS + n, :], parts[:, h * HALF:(h + 1) * HALF],
                                             start=True, stop=True).then_inc(s_bc, 1)
                        if n:
                            if n == 1:
                                until(pe, s_yev, b * 4)
                            reduce_states(n - 1)
                        after(n)
                    reduce_states(NS - 1)

                def output(b):
                    def turn(jp):
                        until(pe, s_yev, (b + 1) * 4)
                        until(pe, s_free, y_base(b) + max(jp - 1, 0))
                        for jj in range(2):
                            for c in range(DC):
                                t = (2 * jp + jj) * P
                                last = nc.tensor.transpose(misc[jp % 2][:, jj * D + c * P:jj * D + c * P + P], ysb[:, c, t:t + P], g.ident[:, :])
                        last.then_inc(s_yt, 1)

                    return {jp: lambda jp=jp: turn(jp) for jp in range(4)}

                run(pe, prepare, states, output,
                    {0: [("y", 0), ("y", 1)], 1: [("y", 2), ("y", 3)], 2: [("p", 0)], 3: [("p", 1)], 4: [("p", 2)], 5: [("p", 3)],
                     6: [("p", 4)], 7: [("p", 5)], 8: [("p", 6), ("p", 7)], 9: [("p", 8)], 10: [("p", 9)], 11: [("p", 10)], 12: [("p", 11)]})

            @block.scalar
            def _(a):
                a.preload_act_table_set("natural_log_exp_and_others")
                until(a, s_w, 16 * len(loads))
                a.activation(absA[:, :, :], alog[:, :, :], ACT.Exp).then_inc(s_prep, 1)

                def prepare(b, par):
                    delta, parts, base = delta2[par], parts2[par], prep_base(b)
                    c_act = Tally(s_act, b * 4)

                    def copy_turned(jp):
                        until(a, s_tp, b * TB + 2 * jp + 2)
                        if jp == 0 and not isinstance(b, int):
                            until(a, s_yt, b * 4 - 4)
                        for c in range(DC):
                            ins = a.activation(xnT[:, c, jp * 256:(jp + 1) * 256], misc[jp % 2][:, c * 256:(c + 1) * 256],
                                               ACT.Copy, accum_out=gp[:, c, jp:jp + 1])
                        ins.then_inc(s_free, 1)

                    def signal():
                        until(a, s_use, b * 8 + 1)
                        a.activation(nh[0][:, :], misc[UZ % 2][0:NS, 0:1], ACT.Exp, scale=2.0 / S, bias=bias2[:, :]).then_inc(s_z, 1)
                        until(a, s_z, b + 1)
                        a.sem_inc(s_free, 1)

                    def select():
                        until(a, s_use, b * 8 + 2)
                        for c in range(DC):
                            ins = a.activation(es[0][:, c:c + 1], misc[US % 2][:, c:c + 1], ACT.Exp, scale=-1.0, bias=nselb[:, c:c + 1])
                        ins.then_inc(s_es, 1)
                        until(a, s_es, b + 1)
                        a.sem_inc(s_free, 1)

                    def steps(q):
                        c, h = q // 2, q % 2
                        ps = misc[(UD + q) % 2]
                        until(a, s_use, b * 8 + 3 + q)
                        if q >= 2:
                            until(a, s_dl, b * 4 + q - 1)
                        elif q == 0:
                            until(a, s_dl, b * 4)
                        a.activation(delta[:, c, h * HALF:(h + 1) * HALF], ps[:, :], ACT.Relu, bias=db[:, c:c + 1])
                        a.activation(ab[:, q % 2, :], ps[:, :], ACT.Abs, bias=db[:, c:c + 1]).then_inc(s_free, 1)
                        until(a, s_free, base + UD + q + 1)
                        c_act.inc(a.activation(ee[:, q % 2, :], ab[:, q % 2, :], ACT.Exp, scale=-1.0))
                        until(a, s_act, c_act.here())
                        a.activation(ll[:, q % 2, :], ee[:, q % 2, :], ACT.Ln, bias=1.0).then_inc(s_ll, 1)

                    def b_and_c(h):
                        until(a, s_use, b * 8 + 7 + h)
                        until(a, s_pt, b * 2)
                        a.activation(bcv[:, h, :], misc[(UB + h) % 2][0:96, :], ACT.Identity, bias=bcb[:, :])
                        a.activation(parts[:, h * HALF:(h + 1) * HALF], misc[(UB + h) % 2][0:96, :], ACT.Identity, bias=bcb[:, :]).then_inc(s_bcv, 1)
                        until(a, s_bcv, b * 2 + h + 1)
                        a.sem_inc(s_free, 1)

                    def split():
                        for h in range(2):
                            until(a, s_rest, b * 2 + h + 1)
                            for rows in (slice(32, 64), slice(64, 96)):
                                ins = a.activation(parts[rows, h * HALF:(h + 1) * HALF], br[rows, h, :], ACT.Copy)
                            ins.then_inc(s_low, 1)

                    todo = [lambda jp=jp: copy_turned(jp) for jp in range(4)] + [signal, select]
                    todo += [lambda k=k: steps(k) for k in range(4)] + [lambda h=h: b_and_c(h) for h in range(2)] + [split]
                    return dict(enumerate(todo))

                def states(b, par, after):
                    until(a, s_dl, b * 4 + 4)
                    for n in range(NS):
                        for q in range(4):
                            w, h = q // 2, q % 2
                            until(a, s_bc, b * 4 * NS + 4 * n + q + 1)
                            if q == 0:
                                until(a, s_hc, b * 2 * NS + max(2 * (n - 1), 0))
                            a.activation(bcs[:, n % 2, w, h * HALF:(h + 1) * HALF], ring[q % 2][:, :], ACT.Copy).then_inc(s_ev, 1)
                        for c in range(DC):
                            until(a, s_h, b * 2 * NS + max(2 * (n - 1) + c + 1, 0))
                            a.activation(Ad[:, c, :], delta2[par][:, c, :], ACT.Exp, scale=negA[:, c, n:n + 1]).then_inc(s_ad, 1)
                        after(n)

                def output(b):
                    def copy_y():
                        until(a, s_y, (b + 1) * 2 * NS)
                        for c in range(DC):
                            for h in range(2):
                                a.activation(ysb[:, c, h * HALF:(h + 1) * HALF], yps[:, c, h, :], ACT.Copy).then_inc(s_yev, 1)

                    return {0: copy_y}

                run(a, prepare, states, output,
                    {0: [("y", 0)], 2: [("p", 0)], 3: [("p", 1)], 4: [("p", 2)], 5: [("p", 3)], 6: [("p", 4)], 7: [("p", 5)],
                     8: [("p", 6)], 9: [("p", 7)], 10: [("p", 8)], 11: [("p", 9)], 12: [("p", 10)], 13: [("p", 11)], 14: [("p", 12)]})

            @block.vector
            def _(v):
                until(v, s_w, 16 * len(loads))
                c = Tally(s_dv)
                v.memset(ones[:, :], 1.0)
                c.inc(v.tensor_tensor(db[:, :], db[:, :], db2[:, :], ALU.add))
                c.inc(v.tensor_scalar(nselb[:, :], selb[:, :], -1.0, None, ALU.mult))
                link(v, c, v.tensor_scalar(tau[:, :], tau[:, :], 0.1, 10.0, ALU.max, ALU.min))
                link(v, c, v.reciprocal(dtau[:, :], tau[:, :]))
                c.inc(v.tensor_scalar(dtau[:, :], dtau[:, :], DT, None, ALU.mult))
                until(v, s_pre, 1)
                link(v, c, v.tensor_tensor(bias2[:, :], misc[0][0:NS, 0:1], Wib[:, :], ALU.add))
                c.inc(v.tensor_scalar(bias2[:, :], bias2[:, :], 2.0, None, ALU.mult))
                until(v, s_prep, 1)
                c.inc(v.tensor_scalar(negA[:, :, :], absA[:, :, :], -1.0, None, ALU.mult))
                link(v, c, v.tensor_scalar(tiny[:, :, :], absA[:, :, :], 1e-6, None, ALU.is_lt))
                v.tensor_reduce(tsum[:, :], tiny[:, :, :], AX.XY, ALU.add).then_inc(s_prep, 1)
                link(v, c, v.tensor_scalar(rest[:, :, :], tiny[:, :, :], -1.0, 1.0, ALU.mult, ALU.add))
                link(v, c, v.tensor_tensor(invA[:, :, :], absA[:, :, :], rest[:, :, :], ALU.mult))
                link(v, c, v.tensor_tensor(invA[:, :, :], invA[:, :, :], tiny[:, :, :], ALU.add))
                link(v, c, v.reciprocal(invA[:, :, :], invA[:, :, :]))
                link(v, c, v.tensor_tensor(invA[:, :, :], invA[:, :, :], rest[:, :, :], ALU.mult))
                link(v, c, v.tensor_tensor(invA[:, :, :], tiny[:, :, :], invA[:, :, :], ALU.subtract))
                until(v, s_pre, 2)
                link(v, c, v.tensor_copy(flag[:, :], misc[1][0:1, 0:1]))
                v.sem_inc(s_flag, 1)
                some_tiny = v.value_load(flag[0:1, 0:1], min_val=0, max_val=D * NS)
                pre = c.n

                def prepare(b, par):
                    xs, delta, parts = xs2[par], delta2[par], parts2[par]
                    PER = 24
                    c = Tally(s_dv, pre + b * PER)

                    def norm(jp):
                        for j in (2 * jp, 2 * jp + 1):
                            if j >= 2:
                                until(v, s_tp, b * TB + j - 1)
                            norm_tile(v, g, xn[j % 2][:, :], b * TB + j).then_inc(s_xn, 1)

                    def mean():
                        until(v, s_free, prep_base(b) + 4)
                        v.tensor_reduce(gcs[:, :], gp[:, :, :], AX.X, ALU.add).then_inc(s_gc, 1)

                    def signal():
                        until(v, s_z, b + 1)
                        link(v, c, v.tensor_scalar(nh[1][:, :], nh[0][:, :], 1.0, None, ALU.add))
                        link(v, c, v.reciprocal(nh[2][:, :], nh[1][:, :]))
                        link(v, c, v.tensor_scalar(nh[2][:, :], nh[2][:, :], -2.0, 1.0, ALU.mult, ALU.add))
                        link(v, c, v.tensor_tensor(nh[3][:, :], nh[2][:, :], h0[:, :], ALU.subtract))
                        v.scalar_tensor_tensor(nh[4][:, :], nh[3][:, :], dtau[:, :], h0[:, :], ALU.mult, ALU.add).then_inc(s_nh, 1)

                    def select():
                        until(v, s_es, b + 1)
                        link(v, c, v.tensor_scalar(es[1][:, :], es[0][:, :], 1.0, None, ALU.add))
                        link(v, c, v.reciprocal(es[2][:, :], es[1][:, :]))
                        for ch in range(DC):
                            ins = v.tensor_scalar(xs[:, ch, :], xnT[:, ch, :], es[2][:, ch:ch + 1], None, ALU.mult)
                        ins.then_inc(s_xs, 1)

                    def softplus(q):
                        until(v, s_ll, b * 4 + q + 1)
                        e_, l_, d_ = ee[:, q % 2, :], ll[:, q % 2, :], dd[:, q % 2, :]
                        link(v, c, v.tensor_scalar(d_, e_, 1.0, 1.0, ALU.add, ALU.subtract))
                        link(v, c, v.tensor_tensor(d_, e_, d_, ALU.subtract))
                        link(v, c, v.tensor_tensor(d_, d_, l_, ALU.add))
                        link(v, c, v.tensor_tensor(d_, d_, e_, ALU.min))
                        dl = delta[:, q // 2, (q % 2) * HALF:(q % 2 + 1) * HALF]
                        v.tensor_tensor(dl, dl, d_, ALU.add).then_inc(s_dl, 1)
                        if q == 3:
                            assert c.n <= PER
                            v.sem_inc(s_dv, PER - c.n)

                    def split():
                        for h in range(2):
                            until(v, s_bcv, b * 2 + h + 1)
                            v.tensor_tensor(br[:, h, :], bcv[:, h, :], parts[:, h * HALF:(h + 1) * HALF], ALU.subtract).then_inc(s_rest, 1)

                    def split_last():
                        for h in range(2):
                            until(v, s_low, b * 2 + h + 1)
                            pt = parts[64:96, h * HALF:(h + 1) * HALF]
                            v.tensor_tensor(pt, br[64:96, h, :], pt, ALU.subtract).then_inc(s_pt, 1)

                    todo = [lambda jp=jp: norm(jp) for jp in range(4)] + [mean, signal, select]
                    todo += [lambda k=k: softplus(k) for k in range(4)] + [split, split_last]
                    return dict(enumerate(todo))

                def states(b, par, after):
                    xs, delta = xs2[par], delta2[par]
                    until(v, s_xs, b + 1)
                    for n in range(NS):
                        k = b * 2 * NS + 2 * n
                        Bn, Cn = bcs[:, n % 2, 0, :], bcs[:, n % 2, 1, :]
                        until(v, s_ev, b * 4 * NS + 4 * n + 2)
                        until(v, s_h, k)
                        for ch in range(DC):
                            v.tensor_tensor(u[:, ch, :], xs[:, ch, :], Bn, ALU.mult).then_inc(s_xb, 1)
                        for ch in range(DC):
                            until(v, s_ad, k + ch + 1)
                            until(v, s_xb, k + ch + 1)
                            v.scalar_tensor_tensor(u[:, ch, :], Ad[:, ch, :], -1.0, u[:, ch, :], ALU.add, ALU.mult).then_inc(s_u, 1)
                        with v.If(some_tiny > 0):
                            until(v, s_u, k + 2)
                            until(v, s_hc, k)
                            for ch in range(DC):
                                v.tensor_tensor(hh[:, ch, :], xs[:, ch, :], Bn, ALU.mult)
                                v.tensor_scalar(u[:, ch, :], u[:, ch, :], rest[:, ch, n:n + 1], None, ALU.mult)
                                v.drain()
                                v.scalar_tensor_tensor(hh[:, ch, :], hh[:, ch, :], tiny[:, ch, n:n + 1], delta[:, ch, :], ALU.mult, ALU.mult)
                                v.drain()
                                v.tensor_tensor(u[:, ch, :], u[:, ch, :], hh[:, ch, :], ALU.add)
                            v.drain()
                        for ch in range(DC):
                            until(v, s_u, k + ch + 1)
                            v.tensor_tensor_scan(hh[:, ch, :], Ad[:, ch, :], u[:, ch, :], 0.0, ALU.mult, ALU.add).then_inc(s_h, 1)
                        until(v, s_ev, b * 4 * NS + 4 * n + 4)
                        for ch in range(DC):
                            until(v, s_h, k + ch + 1)
                            until(v, s_y, b * 2 * NS + max(2 * (n - 1) + ch + 1, 0))
                            v.scalar_tensor_tensor(hc[:, ch, :], hh[:, ch, :], invA[:, ch, n:n + 1], Cn, ALU.mult, ALU.mult).then_inc(s_hc, 1)
                        after(n)

                def output(b):
                    def add(jp):
                        until(v, s_yt, b * 4 + jp + 1)
                        xr = g.xres[:, bass.ds(b * TB + 2 * jp, 2), :]
                        v.tensor_tensor(xr, xr, misc[jp % 2][:, :].rearrange("p (j d) -> p j d", j=2), ALU.add).then_inc(s_free, 1)

                    return {jp: lambda jp=jp: add(jp) for jp in range(4)}

                run(v, prepare, states, output,
                    {0: [("y", 0), ("y", 1)], 1: [("y", 2), ("y", 3), ("p", 0)], 2: [("p", 1)], 3: [("p", 2)], 4: [("p", 3)], 5: [("p", 4)],
                     6: [("p", 5)], 7: [("p", 6)], 9: [("p", 7)], 10: [("p", 8)], 11: [("p", 9)], 12: [("p", 10)], 13: [("p", 11)], 14: [("p", 12)]})


def route(nc, g, dram, tag, s_fill=None):
    U = GROUP
    NG = NT // U
    with ExitStack() as stack:
        m = Mem(nc, stack, tag)
        Wr = m.sb("Wr", [P, DC, E])
        tri = m.sb("tri", [P, P], BF16)
        oneb = m.sb("oneb", [P, P], BF16)
        jrow = m.sb("jrow", [P, 1, E])
        reset = m.sb("reset", [P, E * U])
        trash = m.sb("trash", [P, 1])
        xn = [m.sb(f"xn{j}", [P, D]) for j in range(2 * U)]
        at = [m.sb(f"at{j}", [P, 1], U32) for j in range(2 * U)]
        xT = [m.sb(f"xT{j}", [P, HALF]) for j in range(U // 2)]
        d, ex, cnd, posm = (m.sb(n, [P, U, E]) for n in ("d", "ex", "cnd", "posm"))
        ohb = m.sb("ohb", [P, U, E], BF16)
        tot, pre = m.sb("tot", [P, E, U]), m.sb("pre", [P, E, U])
        carry = m.sb("carry", [P, E])
        mx, mn, idx, ssum, pos1, kept, slot, gf, tr = (
            m.sb(n, [P, U]) for n in ("mx", "mn", "idx", "ssum", "pos1", "kept", "slot", "gf", "tr"))
        sidx = m.sb("sidx", [P, U], U32)
        psT = [m.ps(f"psT{j}") for j in range(U // 2)]
        psL = [m.ps(f"psL{j}") for j in range(2)]
        psC = [m.ps(f"psC{j}") for j in range(2)]
        s_w, s_xn, s_tp, s_xT, s_lp, s_lg = (m.sem(n) for n in ("s_w", "s_xn", "s_tp", "s_xT", "s_lp", "s_lg"))
        s_dv, s_ex, s_oh, s_cum, s_row, s_tick = (m.sem(n) for n in ("s_dv", "s_ex", "s_oh", "s_cum", "s_row", "s_tick"))
        s_sc = [m.sem(f"s_sc{j}", moved=True) for j in range(2)]
        loads = [(Wr[:, :, :], dram["Wr"].rearrange("(c p) e -> p c e", p=P)), (tri[:, :], dram["tri"].bitcast(BF16)),
                 (oneb[:, :], dram["oneb"].bitcast(BF16)), (jrow[:, 0, :], dram["jrow"]),
                 (reset[:, :], dram["reset"]), (trash[:, :], dram["trash"])]
        m.start()
        with nc.Block() as block:
            @block.sync
            def _(sp):
                for out, src in loads:
                    sp.dma_start(out, src).then_inc(s_w, 16)

            @block.tensor
            def _(pe):
                until(pe, s_w, 16 * len(loads))
                with pe.Fori(0, NG // 2) as it:
                    for par in range(2):
                        n = it * 2 + par
                        for jp in range(U // 2):
                            until(pe, s_xn, n * U + 2 * jp + 2)
                            until(pe, s_xT, n * (U // 2))
                            for jj in range(2):
                                for c in range(DC):
                                    last = nc.tensor.transpose(psT[jp][:, jj * D + c * P:jj * D + (c + 1) * P],
                                                               xn[par * U + 2 * jp + jj][:, c * P:(c + 1) * P], g.ident[:, :])
                            last.then_inc(s_tp, 1)
                        if par == 0:
                            until(pe, s_lg, it * 2)
                        for j in range(U):
                            until(pe, s_xT, n * (U // 2) + j // 2 + 1)
                            for c in range(DC):
                                last = nc.tensor.matmul(psL[par][:, j * E:(j + 1) * E], xT[j // 2][:, (j % 2) * D + c * P:(j % 2) * D + (c + 1) * P],
                                                        Wr[:, c, :], start=(c == 0), stop=(c == DC - 1))
                        last.then_inc(s_lp, 1)
                        until(pe, s_oh, n + 1)
                        flat = ohb[:, :, :].rearrange("p i e -> p (i e)")
                        nc.tensor.matmul(psC[par][:, 0:U * E], tri[:, :], flat, start=True, stop=True)
                        nc.tensor.matmul(psC[par][:, U * E:2 * U * E], oneb[:, :], flat, start=True, stop=True).then_inc(s_cum, 1)

            @block.scalar
            def _(a):
                with a.Fori(0, NG // 2) as it:
                    for par in range(2):
                        n = it * 2 + par
                        until(a, s_lp, n)
                        for jp in range(U // 2):
                            until(a, s_tp, n * (U // 2) + jp + 1)
                            a.activation(xT[jp][:, :], psT[jp][:, :], ACT.Copy).then_inc(s_xT, 1)
                        until(a, s_lg, n + 1)
                        a.activation(ex[:, :, :], d[:, :, :], ACT.Exp).then_inc(s_ex, 1)

            @block.gpsimd
            def _(p_):
                w = Waits(p_, s_tick)
                if s_fill:
                    w.ge(s_fill, 16 * (SLOTS // P // FILL))
                with p_.Fori(0, NG // 2) as it:
                    for j in range(2 * U):
                        w.ge(s_row, it * 2 * U + j + 1)
                        p_.indirect_dma_start(dram["slots"], bass.IndirectOffsetOnAxis(ap=at[j][:, :], axis=0),
                                              xn[j][:, :], None).then_inc(s_sc[j // U], 16)
                for q in range(2):
                    until_moved(p_, s_sc[q], 16 * NT // 2)

            @block.vector
            def _(v):
                PER = 21
                wide = lambda t: t[:, :].unsqueeze(2).broadcast_to([P, U, E])
                fl = lambda t: t[:, :, :].rearrange("p e i -> p (e i)")

                def norm(n, par):
                    for j in range(U):
                        norm_tile(v, g, xn[par * U + j][:, :], n * U + j).then_inc(s_xn, 1)

                def group(n, par, send_before, last=False):
                    c = Tally(s_dv, 1 + n * PER)
                    cols = bass.ds(n * U, U)
                    until(v, s_lp, n + 1)
                    scores = psL[par][:, 0:U * E].rearrange("p (i e) -> p i e", e=E)
                    link(v, c, v.tensor_reduce(mx[:, :], scores, AX.X, ALU.max))
                    v.tensor_tensor(d[:, :, :], scores, wide(mx), ALU.subtract).then_inc(s_lg, 1)
                    until(v, s_lg, n + 1)
                    link(v, c, v.tensor_scalar(cnd[:, :, :], d[:, :, :], 0.0, -float(E), ALU.is_ge, ALU.mult))
                    link(v, c, v.tensor_tensor(cnd[:, :, :], cnd[:, :, :], jrow[:, :, :].broadcast_to([P, U, E]), ALU.add))
                    link(v, c, v.tensor_reduce(mn[:, :], cnd[:, :, :], AX.X, ALU.min))
                    v.tensor_tensor(ohb[:, :, :], cnd[:, :, :], wide(mn), ALU.is_equal).then_inc(s_oh, 1)
                    c.inc(v.tensor_scalar(idx[:, :], mn[:, :], float(E), None, ALU.add))
                    if not last:
                        if send_before is not None:
                            until_moved(v, s_sc[1 - par], send_before)
                        norm(n + 1, 1 - par)
                    until(v, s_ex, n + 1)
                    link(v, c, v.tensor_reduce(ssum[:, :], ex[:, :, :], AX.X, ALU.add))
                    link(v, c, v.reciprocal(ssum[:, :], ssum[:, :]))
                    until(v, s_cum, n + 1)
                    within = psC[par][:, 0:U * E].rearrange("p (i e) -> p i e", e=E)
                    whole = psC[par][:, U * E:2 * U * E].rearrange("p (i e) -> p e i", e=E)
                    link(v, c, v.tensor_copy(tot[:, :, :], whole))
                    link(v, c, v.tensor_tensor(tot[:, :, 0], tot[:, :, 0], carry[:, :], ALU.add))
                    link(v, c, v.tensor_tensor_scan(fl(pre), reset[:, :], fl(tot), 0.0, ALU.mult, ALU.add))
                    link(v, c, v.tensor_copy(carry[:, :], pre[:, :, U - 1]))
                    link(v, c, v.tensor_tensor(pre[:, :, :], pre[:, :, :], whole, ALU.subtract))
                    link(v, c, v.tensor_tensor(posm[:, :, :], within, pre[:, :, :].rearrange("p e i -> p i e"), ALU.add))
                    link(v, c, v.tensor_tensor(posm[:, :, :], posm[:, :, :], ohb[:, :, :], ALU.mult))
                    link(v, c, v.tensor_reduce(pos1[:, :], posm[:, :, :], AX.X, ALU.add))
                    c.inc(v.tensor_scalar(kept[:, :], pos1[:, :], float(CAP), None, ALU.is_le))
                    link(v, c, v.tensor_scalar(slot[:, :], pos1[:, :], float(CAP), -1.0, ALU.min, ALU.add))
                    v.tensor_scalar(g.nk[:, cols], kept[:, :], -1.0, 1.0, ALU.mult, ALU.add)
                    v.tensor_tensor(g.fe[:, cols], kept[:, :], ssum[:, :], ALU.mult)
                    link(v, c, v.scalar_tensor_tensor(gf[:, :], idx[:, :], float(CAP), slot[:, :], ALU.mult, ALU.add))
                    v.tensor_copy(g.gidx[:, cols], gf[:, :])
                    link(v, c, v.tensor_scalar(tr[:, :], gf[:, :], -1.0, trash[:, :], ALU.mult, ALU.add))
                    link(v, c, v.tensor_tensor(tr[:, :], tr[:, :], g.nk[:, cols], ALU.mult))
                    assert c.n == PER - 1
                    link(v, c, v.tensor_tensor(sidx[:, :], tr[:, :], gf[:, :], ALU.add))
                    for j in range(U):
                        v.tensor_copy(at[par * U + j][:, :], sidx[:, j:j + 1]).then_inc(s_row, 1)

                until(v, s_w, 16 * len(loads))
                v.memset(carry[:, :], 0.0).then_inc(s_dv, 1)
                norm(0, 0)
                group(0, 0, None)
                group(1, 1, 16 * U)
                with v.Fori(1, NG // 2 - 1) as it:
                    group(it * 2, 0, it * (16 * U))
                    group(it * 2 + 1, 1, it * (16 * U) + 16 * U)
                group(NG - 2, 0, (NG // 2 - 1) * 16 * U)
                group(NG - 1, 1, None, last=True)


def experts(nc, g, dram, tag, w1, w2, s_w):
    BLK, PAIR = 256, 2
    NB = CAP // BLK
    NK = PAIR * NB
    BT = BLK // P
    ET = CAP // P
    with ExitStack() as stack:
        m = Mem(nc, stack, tag)
        rows = [m.sb(f"rows{q}", [P, ET, D]) for q in range(PAIR)]
        out = [m.sb(f"out{q}", [P, ET, D]) for q in range(PAIR)]
        xT = [m.sb(f"xT{q}", [P, DC, BLK]) for q in range(2)]
        h = [m.sb(f"h{q}", [P, FC, BLK]) for q in range(2)]
        psX = [m.ps(f"psX{q}") for q in range(2)]
        psH = [m.ps(f"psH{q}") for q in range(4)]
        psO = [m.ps(f"psO{q}") for q in range(2)]
        s_in = [m.sem(f"s_in{q}") for q in range(PAIR)]
        s_out = [m.sem(f"s_out{q}") for q in range(PAIR)]
        s_t, s_x, s_m1, s_h, s_m2, s_o = (m.sem(n) for n in ("s_t", "s_x", "s_m1", "s_h", "s_m2", "s_o"))
        m.start()
        with nc.Block() as block:
            @block.sync
            def _(sp):
                view = lambda t, e: dram[t][bass.ds(e * CAP, CAP), :].rearrange("(p j) d -> p j d", j=ET)

                def load_rows(e, q):
                    sp.dma_start(rows[q][:, :, :], view("slots", e)).then_inc(s_in[q], 16)

                def store(e, q):
                    until(sp, s_o, e * NB + NB)
                    sp.dma_start(view("eout", e), out[q][:, :, :]).then_inc(s_out[q], 16)

                load_rows(0, 0)
                load_rows(1, 1)
                with sp.Fori(0, E // PAIR - 1) as it:
                    for q in range(PAIR):
                        until(sp, s_m2, it * NK + (q + 1) * NB)
                        load_expert(sp, dram, w1[q], w2[q], s_w[q], it * PAIR + q + PAIR)
                        load_rows(it * PAIR + q + PAIR, q)
                        store(it * PAIR + q, q)
                for q in range(PAIR):
                    store(E - PAIR + q, q)
                for q in range(PAIR):
                    until(sp, s_out[q], 16 * E // PAIR)

            @block.tensor
            def _(pe):
                with pe.Fori(0, E // PAIR) as it:
                    def turn(k):
                        q = k // NB
                        until(pe, s_in[q], it * 16 + 16)
                        until(pe, s_x, it * NK + max(k - 1, 0))
                        for j in range(BT):
                            for c in range(DC):
                                last = nc.tensor.transpose(psX[k % 2][:, c * BLK + j * P:c * BLK + (j + 1) * P],
                                                           rows[q][:, (k % NB) * BT + j, c * P:(c + 1) * P], g.ident[:, :])
                        last.then_inc(s_t, 1)

                    def up(k):
                        q = k // NB
                        until(pe, s_x, it * NK + k + 1)
                        until(pe, s_w[q], it * 32 + 32)
                        for f in range(FC):
                            bank, half = psH[f // 2], f % 2
                            if half == 0:
                                until(pe, s_h, it * NK * 4 + max((k - 1) * 4 + f // 2 + 1, 0))
                            for c in range(DC):
                                last = nc.tensor.matmul(bank[:, half * BLK:(half + 1) * BLK], w1[q][:, c, f * P:(f + 1) * P],
                                                        xT[k % 2][:, c, :], start=(c == 0), stop=(c == DC - 1))
                            if half:
                                last.then_inc(s_m1, 1)

                    def down(k):
                        q = k // NB
                        until(pe, s_h, it * NK * 4 + 4 * k + 4)
                        until(pe, s_o, it * NK + max(k - 1, 0))
                        for j in range(BT):
                            for f in range(FC):
                                last = nc.tensor.matmul(psO[k % 2][:, j * D:(j + 1) * D], h[k % 2][:, f, j * P:(j + 1) * P],
                                                        w2[q][:, f, :], start=(f == 0), stop=(f == FC - 1))
                        last.then_inc(s_m2, 1)

                    for k in range(NK):
                        turn(k)
                        if k:
                            up(k - 1)
                        if k > 1:
                            down(k - 2)
                    up(NK - 1)
                    down(NK - 2)
                    down(NK - 1)

            @block.scalar
            def _(a):
                with a.Fori(0, E // PAIR) as it:
                    for k in range(NK):
                        for q in range(4):
                            until(a, s_m1, it * NK * 4 + 4 * k + q + 1)
                            until(a, s_m2, it * NK + max(k - 1, 0))
                            a.activation(h[k % 2][:, 2 * q:2 * q + 2, :], psH[q][:, :].rearrange("p (f t) -> p f t", f=2),
                                         ACT.Relu).then_inc(s_h, 1)

            @block.vector
            def _(v):
                with v.Fori(0, E // PAIR) as it:
                    def copy_turned(k):
                        until(v, s_t, it * NK + k + 1)
                        until(v, s_m1, it * NK * 4 + max(4 * (k - 1), 0))
                        v.tensor_copy(xT[k % 2][:, :, :], psX[k % 2][:, :].rearrange("p (c t) -> p c t", c=DC)).then_inc(s_x, 1)

                    def copy_out(k):
                        q = k // NB
                        until(v, s_m2, it * NK + k + 1)
                        until(v, s_out[q], it * 16)
                        v.tensor_copy(out[q][:, (k % NB) * BT:(k % NB + 1) * BT, :],
                                      psO[k % 2][:, :].rearrange("p (j d) -> p j d", j=BT)).then_inc(s_o, 1)

                    for k in range(NK):
                        copy_turned(k)
                        if k > 1:
                            copy_out(k - 2)
                    copy_out(NK - 2)
                    copy_out(NK - 1)


def combine(nc, g, dram, tag, out):
    U = 8
    NI = NT // (2 * U)
    with ExitStack() as stack:
        m = Mem(nc, stack, tag)
        at = [m.sb(f"at{j}", [P, 1], U32) for j in range(2 * U)]
        got = [m.sb(f"got{j}", [P, D]) for j in range(2 * U)]
        t = [m.sb(f"t{j}", [P, D]) for j in range(2 * U)]
        s_at, s_use, s_t, s_a, s_tick = (m.sem(n) for n in ("s_at", "s_use", "s_t", "s_a", "s_tick"))
        s_get = [m.sem(f"s_get{j}", moved=True) for j in range(2 * U)]
        s_out = m.sem("s_out")
        m.start()
        with nc.Block() as block:
            if out is not None:
                @block.sync
                def _(sp):
                    for b in range(B):
                        until(sp, s_use, (b + 1) * TB)
                        sp.dma_start(out[S * b:S * b + S, :].rearrange("(i p) d -> p i d", p=P),
                                     g.xres[:, TB * b:TB * b + TB, :]).then_inc(s_out, 16)
                    until(sp, s_out, 16 * B)

            @block.gpsimd
            def _(p_):
                w = Waits(p_, s_tick)
                with p_.Fori(0, NI) as it:
                    for j in range(2 * U):
                        w.ge(s_at, it * 2 * U + j + 1)
                        if j % U == 0:
                            w.ge(s_use, it * 2 * U + max(j - U, 0))
                        p_.indirect_dma_start(got[j][:, :], None, dram["eout"],
                                              bass.IndirectOffsetOnAxis(ap=at[j][:, :], axis=0)).then_inc(s_get[j], 16)

            @block.vector
            def _(v):
                def slots(it, group):
                    for j in range(group * U, group * U + U):
                        v.tensor_copy(at[j][:, :], g.gidx[:, bass.ds(it * 2 * U + j, 1)]).then_inc(s_at, 1)

                def add(it, group):
                    js = range(group * U, group * U + U)
                    i = [it * 2 * U + j for j in range(2 * U)]
                    x = [g.xres[:, bass.ds(k, 1), :].rearrange("p o d -> p (o d)") for k in i]
                    until(v, s_use, it * 2 * U + max((group - 1) * U, 0))
                    for j in js:
                        norm_tile(v, g, t[j][:, :], i[j]).then_inc(s_t, 1)
                    for j in js:
                        until(v, s_t, i[j] + 1)
                        v.scalar_tensor_tensor(t[j][:, :], t[j][:, :], g.nk[:, bass.ds(i[j], 1)], x[j], ALU.mult, ALU.add).then_inc(s_a, 1)
                    for j in js:
                        until(v, s_a, i[j] + 1)
                        until_moved(v, s_get[j], it * 16 + 16)
                        v.scalar_tensor_tensor(x[j], got[j][:, :], g.fe[:, bass.ds(i[j], 1)], t[j][:, :], ALU.mult, ALU.add).then_inc(s_use, 1)

                slots(0, 0)
                slots(0, 1)
                with v.Fori(0, NI - 1) as it:
                    for group in range(2):
                        add(it, group)
                        slots(it + 1, group)
                for group in range(2):
                    add(NI - 1, group)


def load_expert(sp, dram, w1, w2, sem, e):
    sp.dma_start(w1[:, :, :], dram["W1"][bass.ds(e * D, D), :].rearrange("(c p) f -> p c f", p=P)).then_inc(sem, 16)
    sp.dma_start(w2[:, :, :], dram["W2"][bass.ds(e * FF, FF), :].rearrange("(c p) f -> p c f", p=P)).then_inc(sem, 16)


def moe_layer(nc, g, dram, tag, s_fill=None, out=None):
    with ExitStack() as stack:
        m = Mem(nc, stack, tag)
        w1 = [m.sb(f"w1{q}", [P, DC, FF]) for q in range(2)]
        w2 = [m.sb(f"w2{q}", [P, FC, D]) for q in range(2)]
        s_w = [m.sem(f"s_w{q}") for q in range(2)]
        m.start()
        for q in range(2):
            load_expert(nc.sync, dram, w1[q], w2[q], s_w[q], q)
        norm_stats(nc, g, tag + "n_")
        route(nc, g, dram, tag + "r_", s_fill)
        experts(nc, g, dram, tag + "e_", w1, w2, s_w)
    combine(nc, g, dram, tag + "c_", out)


class Event:

    def __init__(self, sem, per):
        self.sem, self.per = sem, per

    def wait(self, eng, it, i):
        until(eng, self.sem, it * self.per + i + 1)

    def wait_all_before(self, eng, it):
        until(eng, self.sem, it * self.per)


class Banks:

    def __init__(self, m, plan):
        self.bank = [m.ps(f"bank{q}") for q in range(8)]
        self.full = [m.sem(f"s_full{q}") for q in range(8)]
        self.free = [m.sem(f"s_free{q}") for q in range(8)]
        self.where, self.uses = {}, [0] * 8
        for n, name in enumerate(plan):
            self.where[name] = (n % 8, self.uses[n % 8])
            self.uses[n % 8] += 1

    def fill(self, pe, it, name):
        q, k = self.where[name]
        until(pe, self.free[q], it * self.uses[q] + k)
        return self.bank[q]

    def filled(self, ins, name):
        ins.then_inc(self.full[self.where[name][0]], 1)

    def read(self, eng, it, name):
        q, k = self.where[name]
        until(eng, self.full[q], it * self.uses[q] + k + 1)
        return self.bank[q]

    def released(self, eng, name):
        eng.sem_inc(self.free[self.where[name][0]], 1)


def gla_layer(nc, g, dram):
    C, G, HP = TB, 4, 32
    HG = H // G
    with ExitStack() as stack:
        m = Mem(nc, stack, "gla_")
        Wqkv = m.sb("Wqkv", [P, DC, 3 * D])
        WfT = m.sb("WfT", [P, DC, H])
        Wg1T = m.sb("Wg1T", [P, DC, HD])
        Wg2T = m.sb("Wg2T", [HD, D])
        WoT = m.sb("WoT", [P, DC, D])
        lnw = m.sb("lnw", [P, DC])
        trif = m.sb("trif", [P, P])
        onef = m.sb("onef", [P, P])
        identb = m.sb("identb", [P, P], BF16)
        later = m.sb("later", [P, HALF], BF16)
        heads = m.sb("heads", [96, H * P], BF16)
        bmask = m.sb("bmask", [P, D])
        hmask = m.sb("hmask", [P, HG])
        xn2 = [m.sb(f"xn{j}", [P, 2, D]) for j in range(2)]
        xn = [xn2[j // 2][:, j % 2, :] for j in range(4)]
        xnT = m.sb("xnT", [P, DC, S])
        g1T = m.sb("g1T", [HD, S])
        th = [m.sb(f"th{j}", [P, HALF]) for j in range(2)]
        tv = m.sb("tv", [P, 2, D])
        qpad = m.sb("qpad", [P, C * H, HP])
        kpad = m.sb("kpad", [P, C * H, HP])
        ktil = [m.sb(f"ktil{j}", [P, H, HP]) for j in range(2)]
        v2 = m.sb("v2", [P, C * D + HD])
        gt = m.sb("gt", [P, C, D])
        og = gt
        small = lambda n: m.sb(n, [P, C * H])
        zc, za, ze, zl, zr, f = (small(n) for n in ("zc", "za", "ze", "zl", "zr", "f"))
        f3 = m.sb("f3", [P, C, 3, HP])
        n2, nl, ny, nt, rn = (small(n) for n in ("n2", "nl", "ny", "nt", "rn"))
        Ft, dF, eF, dec, wk = (small(n) for n in ("Ft", "dF", "eF", "dec", "wk"))
        ftv = m.sb("ftv", [96, HALF])
        ftr = m.sb("ftr", [96, HALF])
        FP = m.sb("FP", [96, S], BF16)
        FN = m.sb("FN", [96, S], BF16)
        qT = [m.sb(f"qT{j}", [P, G, P]) for j in range(3)]
        kT = [m.sb(f"kT{j}", [P, G, P]) for j in range(3)]
        Dg = [m.sb(f"Dg{j}", [P, HG, P]) for j in range(2)]
        odd = m.sb("odd", [P, G, HALF])
        sq = odd[:, :, :].rearrange("p g t -> p (g t)").rearrange("p (h k) -> p h k", k=HD)
        Ag = [t.rearrange("p (h t) -> p h t", h=HG) for t in
              [xnT[:, q // 2, (q % 2) * HALF:(q % 2 + 1) * HALF] for q in range(G)] + [odd[:, q, :] for q in range(G)]]
        St = [m.sb(f"St{j}", [P, H, HD]) for j in range(2)]
        Um = m.sb("Um", [P, H, HD])
        Sd = m.sb("Sd", [P, H, HD])
        o1 = [m.sb(f"o1{j}", [P, H, HD]) for j in range(2)]
        bst = m.sb("bst", [P, C, 6])
        bdm, bq, bve, bl, by, bt, bmean, brs = (m.sb(n, [P, C]) for n in ("bdm", "bq", "bve", "bl", "by", "bt", "bmean", "brs"))
        onT = th
        Qd = [t[:, :].rearrange("p (h t) -> p h t", h=HG) for t in th] + \
             [t[:, :, :].rearrange("p a b -> p (a b)").rearrange("p (h t) -> p h t", h=HG) for t in xn2]
        oT = tv[:, :, :].rearrange("p a b -> p (a b)")

        plan = [f"x{j}" for j in range(4)] + ["zf", "g0", "g1"]
        for c in range(C):
            plan += [f"qk{c}", f"vg{c}"]
        plan += ["Fn", "FT0", "FT1"]
        plan += ["qT0", "kT0"]
        for c in range(C):
            if c + 1 < C:
                plan += [f"qT{c + 1}", f"kT{c + 1}"]
            for q in range(G):
                plan += [f"S{c}{q}", f"G{c}{q}"]
                if c and q == 1:
                    plan += [f"t{c - 1}", f"i{c - 1}"]
                if c and q == 2:
                    plan += [f"o{c - 1}"]
            plan += [f"U{c}"]
        plan += [f"t{C - 1}", f"i{C - 1}", f"o{C - 1}"]
        for j in range(4):
            plan += [f"n{j}"]
        for j in range(4):
            plan += [f"W{j}"]
        banks = Banks(m, plan)

        ev = lambda name, per: Event(m.sem("s_" + name), per)
        e_xn, e_xp, e_xT, e_g1, e_th, e_tv, e_gt = ev("xn", C), ev("xp", C), ev("xT", 4), ev("g1", 2), ev("th", C), ev("tv", C), ev("gt", C)
        e_q, e_k, e_v = ev("q", C), ev("k", C), ev("v", C)
        e_zc, e_za, e_ze, e_zl, e_zr, e_f3, e_n2, e_nl, e_ny, e_kp = (ev(n, 1) for n in ("zc", "za", "ze", "zl", "zr", "f3", "n2", "nl", "ny", "kp"))
        e_Ft, e_dF, e_wk, e_ftv, e_FP, e_FN = ev("Ft", 3), ev("dF", 1), ev("wk", 1), ev("ftv", 2), ev("FP", 2), ev("FN", 2)
        e_qT, e_kT, e_kt, e_D, e_A, e_au = ev("qT", C), ev("kT", C), ev("kt", C), ev("D", C * G), ev("A", C * G), ev("au", C)
        e_st, e_og, e_tp, e_bv, e_bl, e_by, e_on, e_onp, e_onT, e_x, e_U = (
            ev("st", C + 1), ev("og", C), ev("tp", C), ev("bv", 1), ev("bl", 1), ev("by", 1), ev("on", C), ev("onp", 4), ev("onT", 4),
            ev("x", 4), ev("U", C))
        e_Qd, e_oT = ev("Qd", C * G), ev("oT", C)
        s_w, s_pre, s_dv, s_split, s_tick, s_pre8, s_ln = (m.sem(n) for n in ("s_w", "s_pre", "s_dv", "s_split", "s_tick", "s_chunk", "s_ln"))
        loads = [(Wqkv[:, :, :], dram["Wqkv"].rearrange("(c p) n -> p c n", p=P)), (WfT[:, :, :], dram["WfT"].rearrange("(c p) n -> p c n", p=P)),
                 (Wg1T[:, :, :], dram["Wg1T"].rearrange("(c p) n -> p c n", p=P)), (Wg2T[:, :], dram["Wg2T"]),
                 (WoT[:, :, :], dram["WoT"].rearrange("(c p) n -> p c n", p=P)), (lnw[:, :], dram["ln_w"]),
                 (trif[:, :], dram["trif"]), (onef[:, :], dram["onef"]), (identb[:, :], dram["identb"].bitcast(BF16)),
                 (later[:, :], dram["later"].bitcast(BF16)), (heads[:, :], dram["heads"].bitcast(BF16)), (bmask[:, :], dram["bmask"]),
                 (hmask[:, :], dram["hmask"])]
        flat = lambda t: t[:, :, :].rearrange("p a b -> p (a b)")

        m.start()
        with nc.Block() as block:
            @block.sync
            def _(sp):
                for out, src in loads:
                    sp.dma_start(out, src).then_inc(s_w, 16)

            @block.tensor
            def _(pe):
                until(pe, s_w, 16 * len(loads))
                until(pe, s_pre, 1)
                with pe.Fori(0, B) as b:
                    fill = lambda name: banks.fill(pe, b, name)
                    for jp in range(4):
                        bank = fill(f"x{jp}")
                        for jj in range(2):
                            e_xn.wait(pe, b, 2 * jp + jj)
                            for c in range(DC):
                                last = nc.tensor.transpose(bank[:, c * 256 + jj * P:c * 256 + jj * P + P],
                                                           xn[(2 * jp + jj) % 4][:, c * P:c * P + P], g.ident[:, :])
                        banks.filled(last, f"x{jp}")
                    e_xT.wait(pe, b, 3)
                    bank = fill("zf")
                    for c in range(C):
                        for k in range(DC):
                            last = nc.tensor.matmul(bank[:, c * H:(c + 1) * H], xnT[:, k, c * P:(c + 1) * P], WfT[:, k, :],
                                                    start=(k == 0), stop=(k == DC - 1))
                    banks.filled(last, "zf")
                    for h in range(2):
                        bank = fill(f"g{h}")
                        for k in range(DC):
                            last = nc.tensor.matmul(bank[0:HD, :], Wg1T[:, k, :], xnT[:, k, h * HALF:(h + 1) * HALF],
                                                    start=(k == 0), stop=(k == DC - 1))
                        banks.filled(last, f"g{h}")
                    for c in range(C):
                        bank = fill(f"qk{c}")
                        for k in range(DC):
                            last = nc.tensor.matmul(bank[:, :], xnT[:, k, c * P:(c + 1) * P], Wqkv[:, k, 0:2 * D],
                                                    start=(k == 0), stop=(k == DC - 1))
                        banks.filled(last, f"qk{c}")
                        bank = fill(f"vg{c}")
                        for k in range(DC):
                            nc.tensor.matmul(bank[:, 0:D], xnT[:, k, c * P:(c + 1) * P], Wqkv[:, k, 2 * D:3 * D],
                                             start=(k == 0), stop=(k == DC - 1))
                        e_g1.wait(pe, b, c // 4)
                        last = nc.tensor.matmul(bank[:, D:2 * D], g1T[:, c * P:(c + 1) * P], Wg2T[:, :], start=True, stop=True)
                        banks.filled(last, f"vg{c}")
                    e_f3.wait(pe, b, 0)
                    bank = fill("Fn")
                    nc.tensor.matmul(bank[:, 0:C * H], trif[:, :], f[:, :], start=True, stop=True)
                    last = nc.tensor.matmul(bank[:, C * H:2 * C * H], onef[:, :], f[:, :], start=True, stop=True)
                    banks.filled(last, "Fn")
                    for h in range(2):
                        bank = fill(f"FT{h}")
                        for q in range(4):
                            last = nc.tensor.matmul(bank[0:96, q * P:(q + 1) * P], f3[:, 4 * h + q, :, :].rearrange("p a b -> p (a b)"),
                                                    trif[:, :], start=True, stop=True)
                        banks.filled(last, f"FT{h}")

                    def turn(c):
                        e_q.wait(pe, b, c)
                        for name, pad in (("qT", qpad), ("kT", kpad)):
                            if name == "kT":
                                e_kp.wait(pe, b, 0)
                            bank = fill(f"{name}{c}")
                            for q in range(G):
                                src = pad[:, c * H + HG * q:c * H + HG * (q + 1), :].rearrange("p a b -> p (a b)")
                                last = nc.tensor.transpose(bank[:, q * P:(q + 1) * P], src, g.ident[:, :])
                            banks.filled(last, f"{name}{c}")

                    def intra(c):
                        bank = fill(f"t{c}")
                        e_v.wait(pe, b, c)
                        for q in range(G):
                            e_A.wait(pe, b, c * G + q)
                            for j in range(HG):
                                w = c * D + (HG * q + j) * HD
                                last = nc.tensor.matmul(bank[HP * j:HP * (j + 1), q * P:(q + 1) * P], v2[:, w:w + HP],
                                                        Ag[(c % 2) * G + q][:, j, :], start=True, stop=True)
                        banks.filled(last, f"t{c}")

                    def inter(c):
                        bank = fill(f"i{c}")
                        e_st.wait(pe, b, c)
                        for q in range(G):
                            last = nc.tensor.matmul(bank[:, q * HG * HD:(q + 1) * HG * HD], qT[c % 3][:, q, :],
                                                    St[c % 2][:, HG * q:HG * (q + 1), :].rearrange("p a b -> p (a b)"), start=True, stop=True)
                        banks.filled(last, f"i{c}")

                    def turn_back(c):
                        bank = fill(f"o{c}")
                        e_oT.wait(pe, b, c)
                        for q in range(G):
                            last = nc.tensor.transpose(bank[:, q * P:(q + 1) * P], oT[:, q * P:(q + 1) * P], g.ident[:, :])
                        banks.filled(last, f"o{c}")

                    turn(0)
                    for c in range(C):
                        if c + 1 < C:
                            turn(c + 1)
                        e_qT.wait(pe, b, c)
                        e_kT.wait(pe, b, c)
                        e_FN.wait(pe, b, c // 4)
                        for q in range(G):
                            bank = fill(f"S{c}{q}")
                            e_Qd.wait(pe, b, c * G + q)
                            last = nc.tensor.matmul(bank[:, :], kT[c % 3][:, q, :], Qd[q].rearrange("p h t -> p (h t)"), start=True, stop=True)
                            banks.filled(last, f"S{c}{q}")
                            bank = fill(f"G{c}{q}")
                            nc.tensor.matmul(bank[:, :], identb[:, :], later[:, :], start=True, stop=False)
                            for j in range(HG):
                                h = HG * q + j
                                nc.tensor.matmul(bank[:, j * P:(j + 1) * P], heads[:, h * P:(h + 1) * P], FP[:, c * P:(c + 1) * P],
                                                 start=False, stop=False, skip_group_check=True)
                            last = nc.tensor.matmul(bank[:, :], FN[:, c * P:(c + 1) * P], heads[:, q * HALF:(q + 1) * HALF],
                                                    start=False, stop=True)
                            banks.filled(last, f"G{c}{q}")
                            if c and q == 1:
                                intra(c - 1)
                                inter(c - 1)
                            if c and q == 2:
                                turn_back(c - 1)
                        bank = fill(f"U{c}")
                        e_kt.wait(pe, b, c)
                        e_v.wait(pe, b, c)
                        for q in range(G):
                            w = slice(q * HG * HD, (q + 1) * HG * HD)
                            last = nc.tensor.matmul(bank[:, w], ktil[c % 2][:, HG * q:HG * (q + 1), :].rearrange("p a b -> p (a b)"),
                                                    v2[:, c * D + q * HG * HD:c * D + (q + 1) * HG * HD], start=True, stop=True)
                        banks.filled(last, f"U{c}")
                    intra(C - 1)
                    inter(C - 1)
                    turn_back(C - 1)
                    for jp in range(4):
                        bank = fill(f"n{jp}")
                        for jj in range(2):
                            e_on.wait(pe, b, 2 * jp + jj)
                            for c in range(DC):
                                last = nc.tensor.transpose(bank[:, c * 256 + jj * P:c * 256 + jj * P + P],
                                                           og[:, 2 * jp + jj, c * P:(c + 1) * P], g.ident[:, :])
                        banks.filled(last, f"n{jp}")
                    for jp in range(4):
                        e_onT.wait(pe, b, jp)
                        bank = fill(f"W{jp}")
                        for jj in range(2):
                            for k in range(DC):
                                last = nc.tensor.matmul(bank[:, jj * D:(jj + 1) * D], onT[jp % 2][:, k * 256 + jj * P:k * 256 + jj * P + P],
                                                        WoT[:, k, :], start=(k == 0), stop=(k == DC - 1))
                        banks.filled(last, f"W{jp}")

            @block.scalar
            def _(a):
                with a.Fori(0, B) as b:
                    read = lambda name: banks.read(a, b, name)
                    for jp in range(4):
                        bank = read(f"x{jp}")
                        if jp == 0:
                            e_og.wait_all_before(a, b)
                        a.activation(xnT[:, :, jp * 256:(jp + 1) * 256], bank[:, :].rearrange("p (c t) -> p c t", c=DC),
                                     ACT.Copy).then_inc(e_xT.sem, 1)
                        e_xT.wait(a, b, jp)
                        banks.released(a, f"x{jp}")
                    bank = read("zf")
                    e_f3.wait_all_before(a, b)
                    a.activation(zc[:, :], bank[:, 0:C * H], ACT.Copy).then_inc(e_zc.sem, 1)
                    e_zc.wait(a, b, 0)
                    banks.released(a, "zf")
                    a.activation(za[:, :], zc[:, :], ACT.Abs).then_inc(e_za.sem, 1)
                    for h in range(2):
                        bank = read(f"g{h}")
                        a.activation(g1T[:, h * HALF:(h + 1) * HALF], bank[0:HD, :], ACT.Copy).then_inc(e_g1.sem, 1)
                        e_g1.wait(a, b, h)
                        banks.released(a, f"g{h}")
                    e_za.wait(a, b, 0)
                    a.activation(ze[:, :], za[:, :], ACT.Exp, scale=-1.0).then_inc(e_ze.sem, 1)
                    for c in range(C):
                        bank = read(f"qk{c}")
                        if c >= 2:
                            e_k.wait(a, b, c - 2)
                        elif c == 0:
                            e_x.wait_all_before(a, b)
                        a.activation(th[c % 2][:, :], bank[:, :], ACT.Tanh, scale=0.5).then_inc(e_th.sem, 1)
                        bank = read(f"vg{c}")
                        if c >= 2:
                            e_v.wait(a, b, c - 2)
                        a.activation(tv[:, c % 2, :], bank[:, 0:D], ACT.Tanh, scale=0.5)
                        a.activation(gt[:, c, :], bank[:, D:2 * D], ACT.Tanh, scale=0.5).then_inc(e_tv.sem, 1)
                    a.activation(zl[:, :], ze[:, :], ACT.Ln, bias=1.0).then_inc(e_zl.sem, 1)
                    e_n2.wait(a, b, 0)
                    a.activation(nl[:, :], n2[:, :], ACT.Ln, scale=float(2 ** 20)).then_inc(e_nl.sem, 1)
                    e_nl.wait(a, b, 0)
                    a.activation(ny[:, :], nl[:, :], ACT.Exp, scale=-0.5).then_inc(e_ny.sem, 1)
                    bank = read("Fn")
                    e_kt.wait_all_before(a, b)
                    a.activation(Ft[:, :], bank[:, C * H:2 * C * H], ACT.Copy).then_inc(e_Ft.sem, 1)
                    a.activation(eF[:, :], bank[:, 0:C * H], ACT.Exp).then_inc(e_Ft.sem, 1)
                    a.activation(dec[:, :], bank[:, C * H:2 * C * H], ACT.Exp).then_inc(e_Ft.sem, 1)
                    for h in range(2):
                        bank = read(f"FT{h}")
                        if h:
                            e_FP.wait(a, b, 0)
                        a.activation(ftv[:, :], bank[0:96, :], ACT.Copy).then_inc(e_ftv.sem, 1)
                        e_ftv.wait(a, b, h)
                        banks.released(a, f"FT{h}")
                        if h == 0:
                            e_dF.wait(a, b, 0)
                            a.activation(wk[:, :], dF[:, :], ACT.Exp).then_inc(e_wk.sem, 1)

                    def negate(h):
                        e_FP.wait(a, b, h)
                        a.activation(FN[:, h * HALF:(h + 1) * HALF], FP[:, h * HALF:(h + 1) * HALF], ACT.Copy, scale=-1.0).then_inc(e_FN.sem, 1)

                    def copies(c):
                        for name, out, e in (("qT", qT, e_qT), ("kT", kT, e_kT)):
                            bank = read(f"{name}{c}")
                            if c >= 3:
                                e_og.wait(a, b, c - 3)
                            a.activation(out[c % 3][:, :, :], bank[:, :].rearrange("p (g t) -> p g t", g=G), ACT.Copy).then_inc(e.sem, 1)
                            e.wait(a, b, c)
                            banks.released(a, f"{name}{c}")

                    def copy_intra(c):
                        bank = read(f"t{c}")
                        if c:
                            e_og.wait(a, b, c - 1)
                        a.activation(oT[:, :], bank[:, :], ACT.Copy).then_inc(e_oT.sem, 1)
                        e_oT.wait(a, b, c)
                        banks.released(a, f"t{c}")

                    copies(0)
                    negate(0)
                    for c in range(C):
                        if c + 1 < C:
                            copies(c + 1)
                        for q in range(G):
                            n = c * G + q
                            bank = read(f"G{c}{q}")
                            if n >= 2:
                                e_A.wait(a, b, n - 2)
                            else:
                                e_A.wait_all_before(a, b)
                            a.activation(Dg[q % 2][:, :, :], bank[:, :].rearrange("p (h t) -> p h t", h=HG), ACT.Exp).then_inc(e_D.sem, 1)
                            e_D.wait(a, b, n)
                            banks.released(a, f"G{c}{q}")
                            if c and q == 1:
                                copy_intra(c - 1)
                        if c == 0:
                            negate(1)
                    copy_intra(C - 1)
                    e_bv.wait(a, b, 0)
                    a.activation(bl[:, :], bve[:, :], ACT.Ln).then_inc(e_bl.sem, 1)
                    e_bl.wait(a, b, 0)
                    a.activation(by[:, :], bl[:, :], ACT.Exp, scale=-0.5).then_inc(e_by.sem, 1)
                    for jp in range(4):
                        bank = read(f"n{jp}")
                        if jp >= 2:
                            read(f"W{jp - 2}")
                        a.activation(onT[jp % 2][:, :], bank[:, :], ACT.Copy).then_inc(e_onT.sem, 1)
                        e_onT.wait(a, b, jp)
                        banks.released(a, f"n{jp}")

            @block.gpsimd
            def _(p_):
                w = Waits(p_, s_tick)
                with p_.Fori(0, B) as b:
                    w.ge(e_wk.sem, b + 1)
                    w.ge(e_kp.sem, b + 1)

                    def spread(c):
                        w.ge(e_qT.sem, b * C + c + 1)
                        for q in range(G):
                            if c:
                                bq_, k = banks.where[f"S{c - 1}{q}"]
                                w.ge(banks.full[bq_], b * banks.uses[bq_] + k + 1)
                            p_.tensor_tensor(Qd[q], qT[c % 3][:, q, :].unsqueeze(1).broadcast_to([P, HG, P]),
                                             hmask[:, :].unsqueeze(2).broadcast_to([P, HG, P]), ALU.mult).then_inc(e_Qd.sem, 1)

                    spread(0)
                    for c in range(C):
                        if c >= 2:
                            w.ge(e_U.sem, b * C + c - 1)
                        wide = wk[:, c * H:(c + 1) * H].unsqueeze(2).broadcast_to([P, H, HD])
                        p_.tensor_tensor(ktil[c % 2][:, :, 0:HD], kpad[:, c * H:(c + 1) * H, 0:HD], wide, ALU.mult).then_inc(e_kt.sem, 1)
                        if c + 1 < C:
                            spread(c + 1)

            @block.vector
            def _(v):
                c0 = Tally(s_dv)
                until(v, s_w, 16 * len(loads))
                for t in (qpad, kpad):
                    c0.inc(v.memset(t[:, :, :], 0.0))
                for t in ktil:
                    c0.inc(v.memset(t[:, :, :], 0.0))
                c0.inc(v.memset(f3[:, :, :, :], 0.0))
                c0.inc(v.memset(v2[:, C * D:], 0.0))
                for c in range(DC):
                    c0.inc(v.tensor_scalar(WoT[:, c, :], WoT[:, c, :], lnw[:, c:c + 1], None, ALU.mult))
                until(v, s_dv, c0.n)
                v.sem_inc(s_pre, 1)
                pre = c0.n
                PER = 8
                with v.Fori(0, B) as b:
                    t_ = Tally(s_dv, pre + b * PER)
                    read = lambda name: banks.read(v, b, name)
                    for j in range(C):
                        if j >= 4:
                            banks.read(v, b, f"x{(j - 4) // 2}")
                        norm_tile(v, g, xn[j % 4], b * TB + j).then_inc(e_xn.sem, 1)
                    v.memset(St[0][:, :, :], 0.0).then_inc(e_st.sem, 1)
                    e_zc.wait(v, b, 0)
                    v.tensor_scalar(zr[:, :], zc[:, :], -1.0, 0.0, ALU.mult, ALU.max).then_inc(e_zr.sem, 1)
                    e_zr.wait(v, b, 0)
                    for c in range(C):
                        e_th.wait(v, b, c)
                        bank = read(f"qk{c}")
                        hv = lambda ap: ap.rearrange("p (h k) -> p h k", h=H)
                        v.scalar_tensor_tensor(qpad[:, c * H:(c + 1) * H, 0:HD], hv(th[c % 2][:, 0:D]), 1.0, hv(bank[:, 0:D]),
                                               ALU.add, ALU.mult).then_inc(e_q.sem, 1)
                        v.scalar_tensor_tensor(kpad[:, c * H:(c + 1) * H, 0:HD], hv(th[c % 2][:, D:2 * D]), 1.0, hv(bank[:, D:2 * D]),
                                               ALU.add, ALU.mult).then_inc(e_k.sem, 1)
                        e_k.wait(v, b, c)
                        e_q.wait(v, b, c)
                        banks.released(v, f"qk{c}")
                        e_tv.wait(v, b, c)
                        bank = read(f"vg{c}")
                        v.scalar_tensor_tensor(v2[:, c * D:(c + 1) * D], tv[:, c % 2, :], 1.0, bank[:, 0:D], ALU.add, ALU.mult).then_inc(e_v.sem, 1)
                        e_v.wait(v, b, c)
                        banks.released(v, f"vg{c}")
                    link(v, t_, v.tensor_tensor(sq, kpad[:, :, 0:HD], kpad[:, :, 0:HD], ALU.mult))
                    link(v, t_, v.tensor_reduce(n2[:, :], sq, AX.X, ALU.add))
                    v.tensor_scalar(n2[:, :], n2[:, :], 4e-24, None, ALU.max).then_inc(e_n2.sem, 1)
                    e_zl.wait(v, b, 0)
                    link(v, t_, v.scalar_tensor_tensor(f[:, :], zr[:, :], -1.0, zl[:, :], ALU.mult, ALU.subtract))
                    wide = f[:, :].rearrange("p (c h) -> p c h", c=C).unsqueeze(2).broadcast_to([P, C, 3, H])
                    v.tensor_copy(f3[:, :, :, 0:H], wide).then_inc(e_f3.sem, 1)
                    e_ny.wait(v, b, 0)
                    link(v, t_, v.tensor_scalar(ny[:, :], ny[:, :], 1024.0, None, ALU.mult))
                    link(v, t_, v.tensor_tensor(nt[:, :], ny[:, :], ny[:, :], ALU.mult))
                    link(v, t_, v.tensor_tensor(nt[:, :], nt[:, :], n2[:, :], ALU.mult))
                    link(v, t_, v.tensor_scalar(nt[:, :], nt[:, :], -0.5, 1.5, ALU.mult, ALU.add))
                    link(v, t_, v.tensor_tensor(rn[:, :], nt[:, :], ny[:, :], ALU.mult))
                    v.tensor_tensor(kpad[:, :, 0:HD], kpad[:, :, 0:HD], rn[:, :].unsqueeze(2).broadcast_to([P, C * H, HD]), ALU.mult).then_inc(e_kp.sem, 1)
                    bank = read("Fn")
                    e_Ft.wait(v, b, 2)
                    v.tensor_tensor(dF[:, :], Ft[:, :], bank[:, 0:C * H], ALU.subtract).then_inc(e_dF.sem, 1)
                    e_dF.wait(v, b, 0)
                    banks.released(v, "Fn")
                    c_ = Tally(s_split, b * 8)
                    for h in range(2):
                        e_ftv.wait(v, b, h)
                        fp, fv, r = FP[:, h * HALF:(h + 1) * HALF], ftv[:, :], ftr[:, :]
                        link(v, c_, v.tensor_copy(fp, fv))
                        link(v, c_, v.tensor_tensor(r, fv, fp, ALU.subtract))
                        c_.inc(v.tensor_copy(fp[32:64, :], r[32:64, :]))
                        link(v, c_, v.tensor_copy(fp[64:96, :], r[64:96, :]))
                        v.tensor_tensor(fp[64:96, :], r[64:96, :], fp[64:96, :], ALU.subtract).then_inc(e_FP.sem, 1)
                        e_FP.wait(v, b, h)

                    def out_of(c):
                        held, turned = read(f"i{c}"), read(f"o{c}")
                        hv = lambda ap: ap.rearrange("p (h k) -> p h k", h=H)
                        t1 = o1[c % 2]
                        link(v, t8, v.tensor_tensor(t1[:, :, :], hv(held[:, 0:D]), eF[:, c * H:(c + 1) * H].unsqueeze(2).broadcast_to([P, H, HD]), ALU.mult))
                        link(v, t8, v.tensor_tensor(t1[:, :, :], t1[:, :, :], turned[:, :].rearrange("p (h k) -> p h k", k=HP)[:, :, 0:HD], ALU.add))
                        banks.released(v, f"i{c}")
                        banks.released(v, f"o{c}")
                        v.scalar_tensor_tensor(og[:, c, :], gt[:, c, :], 1.0, flat(t1), ALU.add, ALU.mult).then_inc(e_og.sem, 1)
                        e_og.wait(v, b, c)
                        v.bn_stats(bst[:, c, :], og[:, c, :]).then_inc(e_tp.sem, 1)

                    t8 = Tally(s_pre8, b * (C * 4))
                    for c in range(C):
                        for q in range(G):
                            n = c * G + q
                            e_D.wait(v, b, n)
                            bank = read(f"S{c}{q}")
                            if c >= 2:
                                e_oT.wait(v, b, c - 2)
                            v.tensor_tensor(Ag[(c % 2) * G + q], bank[:, :].rearrange("p (h t) -> p h t", h=HG), Dg[q % 2][:, :, :],
                                            ALU.mult).then_inc(e_A.sem, 1)
                            e_A.wait(v, b, n)
                            banks.released(v, f"S{c}{q}")
                        bank = read(f"U{c}")
                        e_st.wait(v, b, c)
                        t8.inc(v.tensor_tensor(Um[:, :, :], bank[:, 0:D].rearrange("p (h k) -> p h k", h=H),
                                               bmask[:, :].rearrange("p (h k) -> p h k", h=H), ALU.mult))
                        link(v, t8, v.tensor_tensor(Sd[:, :, :], St[c % 2][:, :, :],
                                                    dec[:, c * H:(c + 1) * H].unsqueeze(2).broadcast_to([P, H, HD]), ALU.mult))
                        banks.released(v, f"U{c}")
                        v.sem_inc(e_U.sem, 1)
                        if c:
                            read(f"i{c - 1}")
                        v.tensor_tensor(St[(c + 1) % 2][:, :, :], Sd[:, :, :], Um[:, :, :], ALU.add).then_inc(e_st.sem, 1)
                        if c:
                            out_of(c - 1)
                    out_of(C - 1)
                    e_tp.wait(v, b, C - 1)
                    u = Tally(s_ln, b * 10)
                    u.inc(v.tensor_tensor(bdm[:, :], bst[:, :, 1], bst[:, :, 4], ALU.subtract))
                    u.inc(v.tensor_tensor(bq[:, :], bst[:, :, 1], bst[:, :, 4], ALU.add))
                    link(v, u, v.tensor_tensor(bve[:, :], bst[:, :, 2], bst[:, :, 5], ALU.add))
                    u.inc(v.tensor_scalar(bmean[:, :], bq[:, :], 0.5, None, ALU.mult))
                    link(v, u, v.tensor_tensor(bdm[:, :], bdm[:, :], bdm[:, :], ALU.mult))
                    link(v, u, v.tensor_scalar(bdm[:, :], bdm[:, :], 0.25, 64 * EPS, ALU.mult, ALU.add))
                    v.scalar_tensor_tensor(bve[:, :], bve[:, :], 1.0 / D, bdm[:, :], ALU.mult, ALU.add).then_inc(e_bv.sem, 1)
                    e_by.wait(v, b, 0)
                    link(v, u, v.tensor_tensor(bt[:, :], by[:, :], by[:, :], ALU.mult))
                    link(v, u, v.tensor_tensor(bt[:, :], bt[:, :], bve[:, :], ALU.mult))
                    link(v, u, v.tensor_scalar(bt[:, :], bt[:, :], -0.5, 1.5, ALU.mult, ALU.add))
                    link(v, u, v.tensor_tensor(brs[:, :], bt[:, :], by[:, :], ALU.mult))
                    for c in range(C):
                        v.tensor_scalar(og[:, c, :], og[:, c, :], bmean[:, c:c + 1], brs[:, c:c + 1], ALU.subtract, ALU.mult).then_inc(e_on.sem, 1)
                    for jp in range(4):
                        bank = read(f"W{jp}")
                        xr = g.xres[:, bass.ds(b * TB + 2 * jp, 2), :]
                        v.tensor_tensor(xr, xr, bank[:, :].rearrange("p (j d) -> p j d", j=2), ALU.add).then_inc(e_x.sem, 1)
                        e_x.wait(v, b, jp)
                        banks.released(v, f"W{jp}")


class Globals:
    pass


def hybrid_program(nc, dram, phases=("ssm", "ffn", "gla", "ffn2")):
    with ExitStack() as stack:
        m = Mem(nc, stack, "g_")
        g = Globals()
        g.xres = m.sb("xres", [P, NT, D])
        g.mean = m.sb("mean", [P, NT])
        g.rstd = m.sb("rstd", [P, NT])
        g.ident = m.sb("ident", [P, P])
        g.gidx = m.sb("gidx", [P, NT], U32)
        g.fe = m.sb("fe", [P, NT])
        g.nk = m.sb("nk", [P, NT])
        dram["slots"] = nc.dram_tensor("slots", (SLOTS, D), F32).ap()
        dram["eout"] = nc.dram_tensor("eout", (E * CAP, D), F32).ap()
        s_x = [m.sem(f"s_x{b}") for b in range(B)]
        s_ident, s_z, s_fill = m.sem("s_ident"), m.sem("s_z"), m.sem("s_fill")
        m.start()
        last = phases[-1]

        def is_last(phase):
            return dram["out"] if phase == last else None

        start_loads(nc, g, dram, s_x, s_ident)
        with nc.sbuf_tensor("zero", [P, FILL * D], F32) as zero:
            start_fill(nc, dram, zero, s_z, s_fill)
            norm_stats(nc, g, "n1_", s_x, s_ident)
            if "ssm" in phases:
                ssm_layer(nc, g, dram)
            if "ffn" in phases:
                moe_layer(nc, g, dram, "f1", s_fill, is_last("ffn"))
        if "gla" in phases:
            norm_stats(nc, g, "n3_")
            gla_layer(nc, g, dram)
        if "ffn2" in phases:
            moe_layer(nc, g, dram, "f2", None, is_last("ffn2"))
        if last in ("ssm", "gla"):
            store(nc, g, dram["out"])


def store(nc, g, out):
    with ExitStack() as stack:
        m = Mem(nc, stack, "st_")
        s_out = m.sem("s_out")
        m.start()
        with nc.Block() as block:
            @block.sync
            def _(sp):
                sp.dma_start(out.rearrange("(i p) d -> p i d", p=P), g.xres[:, :, :]).then_inc(s_out, 16)
                until(sp, s_out, 16)


def constants():
    rep = np.zeros((96, 2 * NS, P), np.float32)
    for n in range(2 * NS):
        for part in range(3):
            rep[32 * part + n, n, :] = 1
    reset = np.ones((P, E, GROUP), np.float32)
    reset[:, :, 0] = 0
    tri = np.triu(np.ones((P, P), np.float32))
    heads = np.zeros((96, H, P), np.float32)
    for h in range(H):
        heads[[h, 32 + h, 64 + h], h, :] = 1
    later = np.where(np.arange(P)[:, None] > np.arange(P)[None, :], np.float32(NEG), np.float32(0))
    bmask = np.zeros((4, 32, 4, 4, HD), np.float32)
    for h in range(4):
        bmask[h, :, :, h, :] = 1
    hmask = (np.arange(P)[:, None] // 32 == np.arange(4)[None, :]).astype(np.float32)
    bits = lambda w: (np.ascontiguousarray(w, np.float32).view(np.uint32) >> 16).astype(np.uint16)
    return {"trif": tri, "onef": np.ones((P, P), np.float32), "identb": bits(np.eye(P)),
            "later": bits(np.tile(later, (1, 4))), "heads": bits(heads.reshape(96, -1)), "bmask": bmask.reshape(P, D), "hmask": hmask,
            "tri": bits(tri), "oneb": bits(np.ones((P, P))), "reset": reset.reshape(P, E * GROUP),
            "jrow": np.tile(np.arange(E, dtype=np.float32), (P, 1)),
            "trash": (E * CAP + np.arange(P, dtype=np.float32))[:, None],
            "ident": np.eye(P, dtype=np.float32), "rep": bits(rep.reshape(96, -1))}


def layout(i):
    a = {k: np.asarray(v) for k, v in i.items()}
    A, L = "L0_attn_a_", "L0_attn_b_"
    tr = lambda w: np.ascontiguousarray(w.T)
    by_chunk = lambda w: np.ascontiguousarray(w.reshape(DC, P).T)
    d = {"x": a[A + "x"].reshape(T, D), "dWT": tr(a[A + "delta_W"]),
         "bcT": np.ascontiguousarray(np.tile(np.concatenate([a[A + "B_W"], a[A + "C_W"]], 0).T, (1, 3))),
         "bcb": np.ascontiguousarray(np.tile(np.concatenate([a[A + "B_b"], a[A + "C_b"]]), 3)[:, None]),
         "delta_b": by_chunk(a[A + "delta_b"]), "dt_bias": by_chunk(a[A + "dt_bias"]), "A_log": a[A + "A_log"],
         "WiT": tr(a[A + "Wi_W"]), "Wi_b": a[A + "Wi_b"][:, None], "WrT": tr(a[A + "Wr_W"]), "h0": tr(a[A + "h0"]),
         "tau": a[A + "tau"][:, None], "selWT": tr(a[A + "sel_W"]), "sel_b": by_chunk(a[A + "sel_b"])}
    F = "L0_ffn_"
    d.update({"Wr": a[F + "Wr"], "W1": a[F + "W1"].reshape(E * D, FF), "W2": a[F + "W2"].reshape(E * FF, D)})
    d.update({"Wqkv": np.concatenate([a[L + "Wq"], a[L + "Wk"], a[L + "Wv"]], 0).T.copy(), "WfT": tr(a[L + "Wf"]),
              "Wg1T": tr(a[L + "Wg1"]), "Wg2T": tr(a[L + "Wg2"]), "WoT": tr(a[L + "Wo"]), "ln_w": by_chunk(a[L + "ln_w"])})
    d.update(constants())
    return d


PHASES = ("ssm", "ffn", "gla", "ffn2")


def kernel(**inputs):
    import concourse.bacc as bacc
    from concourse.bass_utils import run_bass_kernel_spmd

    nc = bacc.Bacc("TRN2", target_bir_lowering=False, num_devices=1)
    arrays, dram = {}, {}
    for name, a in layout(inputs).items():
        arrays[f"in_{name}"] = a
        dram[name] = nc.dram_tensor(f"in_{name}", a.shape, mybir.dt.from_np(a.dtype), kind="ExternalInput").ap()
    dram["out"] = nc.dram_tensor("out_x", (T, D), F32, kind="ExternalOutput").ap()
    hybrid_program(nc, dram, PHASES)
    r = run_bass_kernel_spmd(nc, [arrays], core_ids=[0])
    return r.results[0]["out_x"].reshape(B, S, D)
```

```python
from contextlib import ExitStack

import numpy as np

import concourse.bass as bass
from concourse import mybir

ALU = mybir.AluOpType
ACT = mybir.ActivationFunctionType
AX = mybir.AxisListType
F32 = mybir.dt.float32
BF16 = mybir.dt.bfloat16
U32 = mybir.dt.uint32

P = 128
B, S, D = 8, 1024, 256
T = B * S
NT = T // P
TB = S // P
DC = D // P
NS = 16
E, FF = 8, 1024
FC = FF // P
CAP = int(1.25 * T / E)
GROUP = 8
FILL = 3
SLOTS = E * CAP + P
H, HD = 16, 16
HALF = 512
DT = 0.1
EPS = 1e-5
NEG = -1e30


def until(eng, sem, value):
    eng.wait_ge(sem, value + 1)


def until_moved(eng, sem, value):
    eng.wait_ge(sem, value)


class Tally:

    def __init__(self, sem, base=0):
        self.sem, self.base, self.n = sem, base, 0

    def inc(self, ins, k=1):
        ins.then_inc(self.sem, k)
        self.n += k
        return ins

    def here(self):
        return self.base + self.n


def link(eng, tally, ins):
    tally.inc(ins)
    until(eng, tally.sem, tally.here())


class Waits:

    def __init__(self, eng, tick):
        self.eng, self.tick = eng, tick

    def ge(self, sem, value):
        until(self.eng, sem, value)
        self.eng.sem_inc(self.tick, 1)

    def link(self, tally, ins):
        tally.inc(ins)
        self.ge(tally.sem, tally.here())


class Mem:

    def __init__(self, nc, stack, tag):
        self.nc, self.stack, self.tag, self.sems, self.ordinary = nc, stack, tag, [], []
        stack.callback(self.clear)

    def sb(self, name, shape, dt=F32):
        return self.stack.enter_context(self.nc.sbuf_tensor(self.tag + name, shape, dt))

    def ps(self, name, shape=(P, HALF), dt=F32):
        return self.stack.enter_context(self.nc.psum_tensor(self.tag + name, list(shape), dt))

    def sem(self, name, moved=False):
        self.sems.append(self.nc.alloc_semaphore(self.tag + name))
        if not moved:
            self.ordinary.append(self.sems[-1])
        return self.sems[-1]

    def start(self):
        for s in self.ordinary:
            self.nc.sync.sem_inc(s, 1)
        self.nc.all_engine_barrier()

    def clear(self):
        if self.sems:
            self.nc.clear_and_free_semaphores(self.sems)
            self.nc.all_engine_barrier()


def start_loads(nc, g, dram, s_x, s_ident):
    for b in range(B):
        nc.sync.dma_start(g.xres[:, TB * b:TB * b + TB, :],
                          dram["x"][S * b:S * b + S, :].rearrange("(i p) d -> p i d", p=P)).then_inc(s_x[b], 16)
    nc.sync.dma_start(g.ident[:, :], dram["ident"]).then_inc(s_ident, 16)


def start_fill(nc, dram, zero, s_z, s_fill):
    rows = SLOTS // P
    nc.vector.memset(zero[:, :], 0.0).then_inc(s_z, 1)
    until(nc.sync, s_z, 1)
    view = dram["slots"].rearrange("(p r) d -> p (r d)", r=rows)
    for k in range(rows // FILL):
        nc.sync.dma_start(view[:, k * FILL * D:(k + 1) * FILL * D], zero[:, :]).then_inc(s_fill, 16)


def norm_stats(nc, g, tag, s_x=None, s_ident=None, taken=False):
    with ExitStack() as stack:
        m = Mem(nc, stack, tag)
        st, tiles = g.st, 0 if taken else NT
        dm, q, ve, ln, y0, yy = (m.sb(n, [P, NT]) for n in ("dm", "q", "ve", "ln", "y0", "yy"))
        s_dv, s_ve, s_y0 = m.sem("s_dv"), m.sem("s_ve"), m.sem("s_y0")
        m.start()
        with nc.Block() as block:
            @block.vector
            def _(v):
                c = Tally(s_dv)
                for b in range(0 if taken else B):
                    if s_x:
                        until(v, s_x[b], 16)
                    with v.Fori(TB // 4 * b, TB // 4 * (b + 1)) as i:
                        for j in range(4):
                            v.bn_stats(st[:, bass.ds(4 * i + j, 1), :], g.xres[:, bass.ds(4 * i + j, 1), :]).then_inc(s_dv, 1)
                c.n = tiles
                until(v, s_dv, tiles)
                c.inc(v.tensor_tensor(dm[:, :], st[:, :, 1], st[:, :, 4], ALU.subtract))
                c.inc(v.tensor_tensor(q[:, :], st[:, :, 1], st[:, :, 4], ALU.add))
                link(v, c, v.tensor_tensor(ve[:, :], st[:, :, 2], st[:, :, 5], ALU.add))
                c.inc(v.tensor_scalar(g.mean[:, :], q[:, :], 0.5, None, ALU.mult))
                link(v, c, v.tensor_tensor(dm[:, :], dm[:, :], dm[:, :], ALU.mult))
                link(v, c, v.tensor_scalar(dm[:, :], dm[:, :], 0.25, EPS, ALU.mult, ALU.add))
                v.scalar_tensor_tensor(ve[:, :], ve[:, :], 1.0 / D, dm[:, :], ALU.mult, ALU.add).then_inc(s_ve, 1)
                until(v, s_y0, 1)
                c.n += 1
                link(v, c, v.tensor_tensor(yy[:, :], y0[:, :], y0[:, :], ALU.mult))
                link(v, c, v.tensor_tensor(yy[:, :], yy[:, :], ve[:, :], ALU.mult))
                link(v, c, v.tensor_scalar(yy[:, :], yy[:, :], -0.5, 1.5, ALU.mult, ALU.add))
                link(v, c, v.tensor_tensor(g.rstd[:, :], yy[:, :], y0[:, :], ALU.mult))

            if s_ident:
                @block.sync
                def _(sp):
                    until(sp, s_ident, 16)

            @block.scalar
            def _(a):
                a.preload_act_table_set("natural_log_exp_and_others")
                until(a, s_ve, 1)
                a.activation(ln[:, :], ve[:, :], ACT.Ln).then_inc(s_dv, 1)
                until(a, s_dv, tiles + 7)
                a.activation(y0[:, :], ln[:, :], ACT.Exp, scale=-0.5).then_inc(s_y0, 1)


def norm_tile(v, g, out, i):
    return v.tensor_scalar(out, g.xres[:, bass.ds(i, 1), :], g.mean[:, bass.ds(i, 1)], g.rstd[:, bass.ds(i, 1)],
                           ALU.subtract, ALU.mult)


def ssm_layer(nc, g, dram):
    with ExitStack() as stack:
        m = Mem(nc, stack, "ssm_")
        dWT = m.sb("dWT", [P, DC, D])
        bcT = m.sb("bcT", [P, DC, 96])
        bcb = m.sb("bcb", [96, 1])
        db = m.sb("db", [P, DC])
        db2 = m.sb("db2", [P, DC])
        alog = m.sb("alog", [P, DC, NS])
        absA = m.sb("absA", [P, DC, NS])
        negA = m.sb("negA", [P, DC, NS])
        tiny = m.sb("tiny", [P, DC, NS])
        rest = m.sb("rest", [P, DC, NS])
        invA = m.sb("invA", [P, DC, NS])
        rep = m.sb("rep", [96, 2 * NS, P], BF16)
        WiT = m.sb("WiT", [P, DC, NS])
        Wib = m.sb("Wib", [NS, 1])
        WrT = m.sb("WrT", [NS, NS])
        h0 = m.sb("h0", [NS, 1])
        tau = m.sb("tau", [NS, 1])
        dtau = m.sb("dtau", [NS, 1])
        bias2 = m.sb("bias2", [NS, 1])
        selWT = m.sb("selWT", [NS, D])
        selb = m.sb("selb", [P, DC])
        nselb = m.sb("nselb", [P, DC])
        ones = m.sb("ones", [P, 1])
        tsum = m.sb("tsum", [P, 1])
        flag = m.sb("flag", [1, 1], U32)
        xn = [m.sb(f"xn{j}", [P, D]) for j in range(2)]
        xnT = m.sb("xnT", [P, DC, S])
        gp = m.sb("gp", [P, DC, 4])
        gcs = m.sb("gcs", [P, DC])
        nh = [m.sb(f"nh{j}", [NS, 1]) for j in range(5)]
        es = [m.sb(f"es{j}", [P, DC]) for j in range(3)]
        xs2 = [m.sb(f"xs{j}", [P, DC, S]) for j in range(2)]
        delta2 = [m.sb(f"delta{j}", [P, DC, S]) for j in range(2)]
        ab = m.sb("ab", [P, 2, HALF])
        ee = m.sb("ee", [P, 2, HALF])
        ll = m.sb("ll", [P, 2, HALF])
        dd = m.sb("dd", [P, 2, HALF])
        bcv = m.sb("bcv", [96, 2, HALF])
        br = m.sb("br", [96, 2, HALF])
        parts2 = [m.sb(f"parts{j}", [96, S], BF16) for j in range(2)]
        bcs = m.sb("bcs", [P, 2, 2, S])
        Ad = m.sb("Ad", [P, DC, S])
        u = m.sb("u", [P, DC, S])
        hh = m.sb("hh", [P, DC, S])
        hc = m.sb("hc", [P, DC, S])
        ysb = xnT
        ring = [m.ps(f"ring{j}") for j in range(2)]
        misc = [m.ps(f"misc{j}") for j in range(2)]
        yps = m.ps("yps", [P, DC, 2, HALF])

        s_w, s_pre, s_prep, s_flag = m.sem("s_w"), m.sem("s_pre"), m.sem("s_prep"), m.sem("s_flag")
        s_dv, s_xn, s_tp, s_use, s_free = m.sem("s_dv"), m.sem("s_xn"), m.sem("s_tp"), m.sem("s_use"), m.sem("s_free")
        s_gc, s_z, s_nh, s_es, s_xs = m.sem("s_gc"), m.sem("s_z"), m.sem("s_nh"), m.sem("s_es"), m.sem("s_xs")
        s_act, s_ll, s_dl = m.sem("s_act"), m.sem("s_ll"), m.sem("s_dl")
        s_bcv, s_rest, s_low, s_pt, s_bc, s_ev = (m.sem(n) for n in ("s_bcv", "s_rest", "s_low", "s_pt", "s_bc", "s_ev"))
        s_ad, s_xb, s_u, s_h, s_hc, s_y = (m.sem(n) for n in ("s_ad", "s_xb", "s_u", "s_h", "s_hc", "s_y"))
        s_yev, s_yt = m.sem("s_yev"), m.sem("s_yt")

        loads = [(dWT[:, :, :], dram["dWT"].rearrange("(c p) n -> p c n", p=P)),
                 (bcT[:, :, :], dram["bcT"].rearrange("(c p) n -> p c n", p=P)),
                 (bcb[:, :], dram["bcb"]),
                 (db[:, :], dram["delta_b"]),
                 (db2[:, :], dram["dt_bias"]),
                 (alog[:, :, :], dram["A_log"].rearrange("(c p) n -> p c n", p=P)),
                 (rep[:, :, :], dram["rep"].bitcast(BF16).rearrange("k (n q) -> k n q", q=P)),
                 (WiT[:, :, :], dram["WiT"].rearrange("(c p) n -> p c n", p=P)),
                 (Wib[:, :], dram["Wi_b"]),
                 (WrT[:, :], dram["WrT"]),
                 (h0[:, :], dram["h0"]),
                 (tau[:, :], dram["tau"]),
                 (selWT[:, :], dram["selWT"]),
                 (selb[:, :], dram["sel_b"])]
        T0, UZ, US, UD, UB, PREP, OUT = 0, 4, 5, 6, 10, 12, 4

        def prep_base(b):
            return 0 if isinstance(b, int) and b == 0 else b * (PREP + OUT) - OUT

        def y_base(b):
            return B * PREP + (B - 1) * OUT if isinstance(b, int) and b == B - 1 else b * (PREP + OUT) + 2 * PREP

        def run(eng, prepare, states, output, steps):
            prep0 = prepare(0, 0)
            for k in sorted(prep0):
                prep0[k]()

            def batch(b, par, first=False, last=False):
                todo = {}
                if not first:
                    todo.update({("y", k): f for k, f in output(b - 1).items()})
                if not last:
                    todo.update({("p", k): f for k, f in prepare(b + 1, 1 - par).items()})

                def after(n):
                    for key in steps.get(n, ()):
                        if key in todo:
                            todo.pop(key)()

                states(b, par, after)
                assert not todo

            batch(0, 0, first=True)
            with eng.Fori(0, (B - 2) // 2) as i:
                batch(i * 2 + 1, 1)
                batch(i * 2 + 2, 0)
            batch(B - 1, (B - 1) % 2, last=True)
            out = output(B - 1)
            for k in sorted(out):
                out[k]()

        m.start()
        with nc.Block() as block:
            @block.sync
            def _(sp):
                for out, src in loads:
                    sp.dma_start(out, src).then_inc(s_w, 16)

            @block.tensor
            def _(pe):
                until(pe, s_w, 16 * len(loads))
                nc.tensor.matmul(misc[0][0:NS, 0:1], WrT[:, :], h0[:, :], start=True, stop=True).then_inc(s_pre, 1)
                until(pe, s_prep, 2)
                nc.tensor.matmul(misc[1][0:1, 0:1], tsum[:, :], ones[:, :], start=True, stop=True).then_inc(s_pre, 1)
                until(pe, s_flag, 1)

                def prepare(b, par):
                    xs, base = xs2[par], prep_base(b)

                    def use(n, free):
                        until(pe, s_free, base + free)
                        return misc[n % 2]

                    def turn(jp):
                        bank = use(T0 + jp, max(jp - 1, 0))
                        for jj in range(2):
                            until(pe, s_xn, b * TB + 2 * jp + jj + 1)
                            for c in range(DC):
                                last = nc.tensor.transpose(bank[:, c * 256 + jj * P:c * 256 + jj * P + P],
                                                           xn[jj][:, c * P:c * P + P], g.ident[:, :])
                            last.then_inc(s_tp, 1)

                    def signal():
                        until(pe, s_gc, b + 1)
                        bank = use(UZ, UZ)
                        for c in range(DC):
                            last = nc.tensor.matmul(bank[0:NS, 0:1], WiT[:, c, :], gcs[:, c:c + 1], start=(c == 0), stop=(c == DC - 1))
                        last.then_inc(s_use, 1)

                    def select():
                        until(pe, s_nh, b + 1)
                        bank = use(US, US)
                        for c in range(DC):
                            last = nc.tensor.matmul(bank[:, c:c + 1], selWT[:, c * P:c * P + P], nh[4][:, :], start=True, stop=True)
                        last.then_inc(s_use, 1)

                    def steps(q):
                        until(pe, s_xs, b + 1)
                        c, h = q // 2, q % 2
                        bank = use(UD + q, UD + max(q - 1, 0))
                        for k in range(DC):
                            last = nc.tensor.matmul(bank[:, :], dWT[:, k, c * P:c * P + P], xs[:, k, h * HALF:(h + 1) * HALF],
                                                    start=(k == 0), stop=(k == DC - 1))
                        last.then_inc(s_use, 1)

                    def b_and_c(h):
                        bank = use(UB + h, UB + h - 1)
                        for k in range(DC):
                            last = nc.tensor.matmul(bank[0:96, :], bcT[:, k, :], xs[:, k, h * HALF:(h + 1) * HALF],
                                                    start=(k == 0), stop=(k == DC - 1))
                        last.then_inc(s_use, 1)

                    todo = [lambda jp=jp: turn(jp) for jp in range(4)] + [signal, select]
                    todo += [lambda k=k: steps(k) for k in range(4)] + [lambda h=h: b_and_c(h) for h in range(2)]
                    return dict(enumerate(todo))

                def states(b, par, after):
                    parts = parts2[par]

                    def reduce_states(n):
                        for c in range(DC):
                            until(pe, s_hc, b * 2 * NS + 2 * n + c + 1)
                            for h in range(2):
                                last = nc.tensor.matmul(yps[:, c, h, :], g.ident[:, :], hc[:, c, h * HALF:(h + 1) * HALF],
                                                        start=(n == 0), stop=(n == NS - 1))
                            last.then_inc(s_y, 1)

                    until(pe, s_pt, (b + 1) * 2)
                    for n in range(NS):
                        for q in range(4):
                            w, h = q // 2, q % 2
                            if n or q > 1:
                                until(pe, s_ev, b * 4 * NS + 4 * n + q - 1)
                            elif q == 0:
                                until(pe, s_ev, b * 4 * NS)
                            nc.tensor.matmul(ring[q % 2][:, :], rep[:, w * NS + n, :], parts[:, h * HALF:(h + 1) * HALF],
                                             start=True, stop=True).then_inc(s_bc, 1)
                        if n:
                            if n == 1:
                                until(pe, s_yev, b * 4)
                            reduce_states(n - 1)
                        after(n)
                    reduce_states(NS - 1)

                def output(b):
                    def turn(jp):
                        until(pe, s_yev, (b + 1) * 4)
                        until(pe, s_free, y_base(b) + max(jp - 1, 0))
                        for jj in range(2):
                            for c in range(DC):
                                t = (2 * jp + jj) * P
                                last = nc.tensor.transpose(misc[jp % 2][:, jj * D + c * P:jj * D + c * P + P], ysb[:, c, t:t + P], g.ident[:, :])
                        last.then_inc(s_yt, 1)

                    return {jp: lambda jp=jp: turn(jp) for jp in range(4)}

                run(pe, prepare, states, output,
                    {0: [("y", 0), ("y", 1)], 1: [("y", 2), ("y", 3)], 2: [("p", 0)], 3: [("p", 1)], 4: [("p", 2)], 5: [("p", 3)],
                     6: [("p", 4)], 7: [("p", 5)], 8: [("p", 6), ("p", 7)], 9: [("p", 8)], 10: [("p", 9)], 11: [("p", 10)], 12: [("p", 11)]})

            @block.scalar
            def _(a):
                a.preload_act_table_set("natural_log_exp_and_others")
                until(a, s_w, 16 * len(loads))
                a.activation(absA[:, :, :], alog[:, :, :], ACT.Exp).then_inc(s_prep, 1)

                def prepare(b, par):
                    delta, parts, base = delta2[par], parts2[par], prep_base(b)
                    c_act = Tally(s_act, b * 4)

                    def copy_turned(jp):
                        until(a, s_tp, b * TB + 2 * jp + 2)
                        if jp == 0 and not isinstance(b, int):
                            until(a, s_yt, b * 4 - 4)
                        for c in range(DC):
                            ins = a.activation(xnT[:, c, jp * 256:(jp + 1) * 256], misc[jp % 2][:, c * 256:(c + 1) * 256],
                                               ACT.Copy, accum_out=gp[:, c, jp:jp + 1])
                        ins.then_inc(s_free, 1)

                    def signal():
                        until(a, s_use, b * 8 + 1)
                        a.activation(nh[0][:, :], misc[UZ % 2][0:NS, 0:1], ACT.Exp, scale=2.0 / S, bias=bias2[:, :]).then_inc(s_z, 1)
                        until(a, s_z, b + 1)
                        a.sem_inc(s_free, 1)

                    def select():
                        until(a, s_use, b * 8 + 2)
                        for c in range(DC):
                            ins = a.activation(es[0][:, c:c + 1], misc[US % 2][:, c:c + 1], ACT.Exp, scale=-1.0, bias=nselb[:, c:c + 1])
                        ins.then_inc(s_es, 1)
                        until(a, s_es, b + 1)
                        a.sem_inc(s_free, 1)

                    def steps(q):
                        c, h = q // 2, q % 2
                        ps = misc[(UD + q) % 2]
                        until(a, s_use, b * 8 + 3 + q)
                        if q >= 2:
                            until(a, s_dl, b * 4 + q - 1)
                        elif q == 0:
                            until(a, s_dl, b * 4)
                        a.activation(delta[:, c, h * HALF:(h + 1) * HALF], ps[:, :], ACT.Relu, bias=db[:, c:c + 1])
                        a.activation(ab[:, q % 2, :], ps[:, :], ACT.Abs, bias=db[:, c:c + 1]).then_inc(s_free, 1)
                        until(a, s_free, base + UD + q + 1)
                        c_act.inc(a.activation(ee[:, q % 2, :], ab[:, q % 2, :], ACT.Exp, scale=-1.0))
                        until(a, s_act, c_act.here())
                        a.activation(ll[:, q % 2, :], ee[:, q % 2, :], ACT.Ln, bias=1.0).then_inc(s_ll, 1)

                    def b_and_c(h):
                        until(a, s_use, b * 8 + 7 + h)
                        until(a, s_pt, b * 2)
                        a.activation(bcv[:, h, :], misc[(UB + h) % 2][0:96, :], ACT.Identity, bias=bcb[:, :])
                        a.activation(parts[:, h * HALF:(h + 1) * HALF], misc[(UB + h) % 2][0:96, :], ACT.Identity, bias=bcb[:, :]).then_inc(s_bcv, 1)
                        until(a, s_bcv, b * 2 + h + 1)
                        a.sem_inc(s_free, 1)

                    def split():
                        for h in range(2):
                            until(a, s_rest, b * 2 + h + 1)
                            for rows in (slice(32, 64), slice(64, 96)):
                                ins = a.activation(parts[rows, h * HALF:(h + 1) * HALF], br[rows, h, :], ACT.Copy)
                            ins.then_inc(s_low, 1)

                    todo = [lambda jp=jp: copy_turned(jp) for jp in range(4)] + [signal, select]
                    todo += [lambda k=k: steps(k) for k in range(4)] + [lambda h=h: b_and_c(h) for h in range(2)] + [split]
                    return dict(enumerate(todo))

                def states(b, par, after):
                    until(a, s_dl, b * 4 + 4)
                    for n in range(NS):
                        for q in range(4):
                            w, h = q // 2, q % 2
                            until(a, s_bc, b * 4 * NS + 4 * n + q + 1)
                            if q == 0:
                                until(a, s_hc, b * 2 * NS + max(2 * (n - 1), 0))
                            a.activation(bcs[:, n % 2, w, h * HALF:(h + 1) * HALF], ring[q % 2][:, :], ACT.Copy).then_inc(s_ev, 1)
                        for c in range(DC):
                            until(a, s_h, b * 2 * NS + max(2 * (n - 1) + c + 1, 0))
                            a.activation(Ad[:, c, :], delta2[par][:, c, :], ACT.Exp, scale=negA[:, c, n:n + 1]).then_inc(s_ad, 1)
                        after(n)

                def output(b):
                    def copy_y():
                        until(a, s_y, (b + 1) * 2 * NS)
                        for c in range(DC):
                            for h in range(2):
                                a.activation(ysb[:, c, h * HALF:(h + 1) * HALF], yps[:, c, h, :], ACT.Copy).then_inc(s_yev, 1)

                    return {0: copy_y}

                run(a, prepare, states, output,
                    {0: [("y", 0)], 2: [("p", 0)], 3: [("p", 1)], 4: [("p", 2)], 5: [("p", 3)], 6: [("p", 4)], 7: [("p", 5)],
                     8: [("p", 6)], 9: [("p", 7)], 10: [("p", 8)], 11: [("p", 9)], 12: [("p", 10)], 13: [("p", 11)], 14: [("p", 12)]})

            @block.vector
            def _(v):
                until(v, s_w, 16 * len(loads))
                c = Tally(s_dv)
                v.memset(ones[:, :], 1.0)
                c.inc(v.tensor_tensor(db[:, :], db[:, :], db2[:, :], ALU.add))
                c.inc(v.tensor_scalar(nselb[:, :], selb[:, :], -1.0, None, ALU.mult))
                link(v, c, v.tensor_scalar(tau[:, :], tau[:, :], 0.1, 10.0, ALU.max, ALU.min))
                link(v, c, v.reciprocal(dtau[:, :], tau[:, :]))
                c.inc(v.tensor_scalar(dtau[:, :], dtau[:, :], DT, None, ALU.mult))
                until(v, s_pre, 1)
                link(v, c, v.tensor_tensor(bias2[:, :], misc[0][0:NS, 0:1], Wib[:, :], ALU.add))
                c.inc(v.tensor_scalar(bias2[:, :], bias2[:, :], 2.0, None, ALU.mult))
                until(v, s_prep, 1)
                c.inc(v.tensor_scalar(negA[:, :, :], absA[:, :, :], -1.0, None, ALU.mult))
                link(v, c, v.tensor_scalar(tiny[:, :, :], absA[:, :, :], 1e-6, None, ALU.is_lt))
                v.tensor_reduce(tsum[:, :], tiny[:, :, :], AX.XY, ALU.add).then_inc(s_prep, 1)
                link(v, c, v.tensor_scalar(rest[:, :, :], tiny[:, :, :], -1.0, 1.0, ALU.mult, ALU.add))
                link(v, c, v.tensor_tensor(invA[:, :, :], absA[:, :, :], rest[:, :, :], ALU.mult))
                link(v, c, v.tensor_tensor(invA[:, :, :], invA[:, :, :], tiny[:, :, :], ALU.add))
                link(v, c, v.reciprocal(invA[:, :, :], invA[:, :, :]))
                link(v, c, v.tensor_tensor(invA[:, :, :], invA[:, :, :], rest[:, :, :], ALU.mult))
                link(v, c, v.tensor_tensor(invA[:, :, :], tiny[:, :, :], invA[:, :, :], ALU.subtract))
                until(v, s_pre, 2)
                link(v, c, v.tensor_copy(flag[:, :], misc[1][0:1, 0:1]))
                v.sem_inc(s_flag, 1)
                some_tiny = v.value_load(flag[0:1, 0:1], min_val=0, max_val=D * NS)
                pre = c.n

                def prepare(b, par):
                    xs, delta, parts = xs2[par], delta2[par], parts2[par]
                    PER = 24
                    c = Tally(s_dv, pre + b * PER)

                    def norm(jp):
                        for j in (2 * jp, 2 * jp + 1):
                            if j >= 2:
                                until(v, s_tp, b * TB + j - 1)
                            norm_tile(v, g, xn[j % 2][:, :], b * TB + j).then_inc(s_xn, 1)

                    def mean():
                        until(v, s_free, prep_base(b) + 4)
                        v.tensor_reduce(gcs[:, :], gp[:, :, :], AX.X, ALU.add).then_inc(s_gc, 1)

                    def signal():
                        until(v, s_z, b + 1)
                        link(v, c, v.tensor_scalar(nh[1][:, :], nh[0][:, :], 1.0, None, ALU.add))
                        link(v, c, v.reciprocal(nh[2][:, :], nh[1][:, :]))
                        link(v, c, v.tensor_scalar(nh[2][:, :], nh[2][:, :], -2.0, 1.0, ALU.mult, ALU.add))
                        link(v, c, v.tensor_tensor(nh[3][:, :], nh[2][:, :], h0[:, :], ALU.subtract))
                        v.scalar_tensor_tensor(nh[4][:, :], nh[3][:, :], dtau[:, :], h0[:, :], ALU.mult, ALU.add).then_inc(s_nh, 1)

                    def select():
                        until(v, s_es, b + 1)
                        link(v, c, v.tensor_scalar(es[1][:, :], es[0][:, :], 1.0, None, ALU.add))
                        link(v, c, v.reciprocal(es[2][:, :], es[1][:, :]))
                        for ch in range(DC):
                            ins = v.tensor_scalar(xs[:, ch, :], xnT[:, ch, :], es[2][:, ch:ch + 1], None, ALU.mult)
                        ins.then_inc(s_xs, 1)

                    def softplus(q):
                        until(v, s_ll, b * 4 + q + 1)
                        e_, l_, d_ = ee[:, q % 2, :], ll[:, q % 2, :], dd[:, q % 2, :]
                        link(v, c, v.tensor_scalar(d_, e_, 1.0, 1.0, ALU.add, ALU.subtract))
                        link(v, c, v.tensor_tensor(d_, e_, d_, ALU.subtract))
                        link(v, c, v.tensor_tensor(d_, d_, l_, ALU.add))
                        link(v, c, v.tensor_tensor(d_, d_, e_, ALU.min))
                        dl = delta[:, q // 2, (q % 2) * HALF:(q % 2 + 1) * HALF]
                        v.tensor_tensor(dl, dl, d_, ALU.add).then_inc(s_dl, 1)
                        if q == 3:
                            assert c.n <= PER
                            v.sem_inc(s_dv, PER - c.n)

                    def split():
                        for h in range(2):
                            until(v, s_bcv, b * 2 + h + 1)
                            v.tensor_tensor(br[:, h, :], bcv[:, h, :], parts[:, h * HALF:(h + 1) * HALF], ALU.subtract).then_inc(s_rest, 1)

                    def split_last():
                        for h in range(2):
                            until(v, s_low, b * 2 + h + 1)
                            pt = parts[64:96, h * HALF:(h + 1) * HALF]
                            v.tensor_tensor(pt, br[64:96, h, :], pt, ALU.subtract).then_inc(s_pt, 1)

                    todo = [lambda jp=jp: norm(jp) for jp in range(4)] + [mean, signal, select]
                    todo += [lambda k=k: softplus(k) for k in range(4)] + [split, split_last]
                    return dict(enumerate(todo))

                def states(b, par, after):
                    xs, delta = xs2[par], delta2[par]
                    until(v, s_xs, b + 1)
                    for n in range(NS):
                        k = b * 2 * NS + 2 * n
                        Bn, Cn = bcs[:, n % 2, 0, :], bcs[:, n % 2, 1, :]
                        until(v, s_ev, b * 4 * NS + 4 * n + 2)
                        until(v, s_h, k)
                        for ch in range(DC):
                            v.tensor_tensor(u[:, ch, :], xs[:, ch, :], Bn, ALU.mult).then_inc(s_xb, 1)
                        for ch in range(DC):
                            until(v, s_ad, k + ch + 1)
                            until(v, s_xb, k + ch + 1)
                            v.scalar_tensor_tensor(u[:, ch, :], Ad[:, ch, :], -1.0, u[:, ch, :], ALU.add, ALU.mult).then_inc(s_u, 1)
                        with v.If(some_tiny > 0):
                            until(v, s_u, k + 2)
                            until(v, s_hc, k)
                            for ch in range(DC):
                                v.tensor_tensor(hh[:, ch, :], xs[:, ch, :], Bn, ALU.mult)
                                v.tensor_scalar(u[:, ch, :], u[:, ch, :], rest[:, ch, n:n + 1], None, ALU.mult)
                                v.drain()
                                v.scalar_tensor_tensor(hh[:, ch, :], hh[:, ch, :], tiny[:, ch, n:n + 1], delta[:, ch, :], ALU.mult, ALU.mult)
                                v.drain()
                                v.tensor_tensor(u[:, ch, :], u[:, ch, :], hh[:, ch, :], ALU.add)
                            v.drain()
                        for ch in range(DC):
                            until(v, s_u, k + ch + 1)
                            v.tensor_tensor_scan(hh[:, ch, :], Ad[:, ch, :], u[:, ch, :], 0.0, ALU.mult, ALU.add).then_inc(s_h, 1)
                        until(v, s_ev, b * 4 * NS + 4 * n + 4)
                        for ch in range(DC):
                            until(v, s_h, k + ch + 1)
                            until(v, s_y, b * 2 * NS + max(2 * (n - 1) + ch + 1, 0))
                            v.scalar_tensor_tensor(hc[:, ch, :], hh[:, ch, :], invA[:, ch, n:n + 1], Cn, ALU.mult, ALU.mult).then_inc(s_hc, 1)
                        after(n)

                def output(b):
                    def add(jp):
                        until(v, s_yt, b * 4 + jp + 1)
                        xr = g.xres[:, bass.ds(b * TB + 2 * jp, 2), :]
                        v.tensor_tensor(xr, xr, misc[jp % 2][:, :].rearrange("p (j d) -> p j d", j=2), ALU.add).then_inc(s_free, 1)

                    return {jp: lambda jp=jp: add(jp) for jp in range(4)}

                run(v, prepare, states, output,
                    {0: [("y", 0), ("y", 1)], 1: [("y", 2), ("y", 3), ("p", 0)], 2: [("p", 1)], 3: [("p", 2)], 4: [("p", 3)], 5: [("p", 4)],
                     6: [("p", 5)], 7: [("p", 6)], 9: [("p", 7)], 10: [("p", 8)], 11: [("p", 9)], 12: [("p", 10)], 13: [("p", 11)], 14: [("p", 12)]})


def route(nc, g, dram, tag, s_fill=None):
    U, SETS = GROUP, 4
    NG = NT // U
    with ExitStack() as stack:
        m = Mem(nc, stack, tag)
        Wr = m.sb("Wr", [P, DC, E])
        tri = m.sb("tri", [P, P], BF16)
        oneb = m.sb("oneb", [P, P], BF16)
        jrow = m.sb("jrow", [P, 1, E])
        reset = m.sb("reset", [P, E * U])
        trash = m.sb("trash", [P, 1])
        xn = [m.sb(f"xn{j}", [P, D]) for j in range(SETS * U)]
        at = [m.sb(f"at{j}", [P, 1], U32) for j in range(SETS * U)]
        xT = [m.sb(f"xT{j}", [P, HALF]) for j in range(U // 2)]
        d, ex, cnd, posm = (m.sb(n, [P, U, E]) for n in ("d", "ex", "cnd", "posm"))
        ohb = m.sb("ohb", [P, U, E], BF16)
        tot, pre = m.sb("tot", [P, E, U]), m.sb("pre", [P, E, U])
        carry = m.sb("carry", [P, E])
        mx, mn, idx, ssum, pos1, kept, slot, gf, tr = (
            m.sb(n, [P, U]) for n in ("mx", "mn", "idx", "ssum", "pos1", "kept", "slot", "gf", "tr"))
        sidx = m.sb("sidx", [P, U], U32)
        psT = [m.ps(f"psT{j}") for j in range(U // 2)]
        psL = [m.ps(f"psL{j}") for j in range(2)]
        psC = [m.ps(f"psC{j}") for j in range(2)]
        s_w, s_xn, s_tp, s_xT, s_lp, s_lg = (m.sem(n) for n in ("s_w", "s_xn", "s_tp", "s_xT", "s_lp", "s_lg"))
        s_dv, s_ex, s_oh, s_cum, s_row, s_tick = (m.sem(n) for n in ("s_dv", "s_ex", "s_oh", "s_cum", "s_row", "s_tick"))
        s_left = m.sem("s_left")
        s_sc = [m.sem(f"s_sc{j}", moved=True) for j in range(SETS)]
        loads = [(Wr[:, :, :], dram["Wr"].rearrange("(c p) e -> p c e", p=P)), (tri[:, :], dram["tri"].bitcast(BF16)),
                 (oneb[:, :], dram["oneb"].bitcast(BF16)), (jrow[:, 0, :], dram["jrow"]),
                 (reset[:, :], dram["reset"]), (trash[:, :], dram["trash"])]
        m.start()
        with nc.Block() as block:
            @block.sync
            def _(sp):
                for out, src in loads:
                    sp.dma_start(out, src).then_inc(s_w, 16)

            @block.tensor
            def _(pe):
                until(pe, s_w, 16 * len(loads))
                with pe.Fori(0, NG // SETS) as it:
                    for k in range(SETS):
                        n, par = it * SETS + k, k % 2
                        for jp in range(U // 2):
                            until(pe, s_xn, n * U + 2 * jp + 2)
                            until(pe, s_xT, n * (U // 2))
                            for jj in range(2):
                                for c in range(DC):
                                    last = nc.tensor.transpose(psT[jp][:, jj * D + c * P:jj * D + (c + 1) * P],
                                                               xn[k * U + 2 * jp + jj][:, c * P:(c + 1) * P], g.ident[:, :])
                            last.then_inc(s_tp, 1)
                        until(pe, s_lg, n)
                        for j in range(U):
                            until(pe, s_xT, n * (U // 2) + j // 2 + 1)
                            for c in range(DC):
                                last = nc.tensor.matmul(psL[par][:, j * E:(j + 1) * E], xT[j // 2][:, (j % 2) * D + c * P:(j % 2) * D + (c + 1) * P],
                                                        Wr[:, c, :], start=(c == 0), stop=(c == DC - 1))
                        last.then_inc(s_lp, 1)
                        until(pe, s_oh, n + 1)
                        flat = ohb[:, :, :].rearrange("p i e -> p (i e)")
                        nc.tensor.matmul(psC[par][:, 0:U * E], tri[:, :], flat, start=True, stop=True)
                        nc.tensor.matmul(psC[par][:, U * E:2 * U * E], oneb[:, :], flat, start=True, stop=True).then_inc(s_cum, 1)

            @block.scalar
            def _(a):
                with a.Fori(0, NG // SETS) as it:
                    for k in range(SETS):
                        n = it * SETS + k
                        until(a, s_lp, n)
                        for jp in range(U // 2):
                            until(a, s_tp, n * (U // 2) + jp + 1)
                            a.activation(xT[jp][:, :], psT[jp][:, :], ACT.Copy).then_inc(s_xT, 1)
                        until(a, s_lg, n + 1)
                        a.activation(ex[:, :, :], d[:, :, :], ACT.Exp).then_inc(s_ex, 1)

            @block.gpsimd
            def _(p_):
                w = Waits(p_, s_tick)
                if s_fill:
                    w.ge(s_fill, 16 * (SLOTS // P // FILL))
                def left(it, k):
                    p_.wait_ge(s_sc[k], it * (16 * U) + 16 * U)
                    p_.sem_inc(s_left, 1)

                with p_.Fori(0, NG // SETS) as it:
                    for k in range(SETS):
                        for j in range(k * U, (k + 1) * U):
                            w.ge(s_row, it * SETS * U + j + 1)
                            p_.indirect_dma_start(dram["slots"], bass.IndirectOffsetOnAxis(ap=at[j][:, :], axis=0),
                                                  xn[j][:, :], None).then_inc(s_sc[k], 16)
                        if k:
                            left(it, k - 1)
                    left(it, SETS - 1)

            @block.vector
            def _(v):
                PER = 21
                wide = lambda t: t[:, :].unsqueeze(2).broadcast_to([P, U, E])
                fl = lambda t: t[:, :, :].rearrange("p e i -> p (e i)")

                def norm(n, k):
                    for j in range(U):
                        norm_tile(v, g, xn[k * U + j][:, :], n * U + j).then_inc(s_xn, 1)

                def group(it, k):
                    n, par = it * SETS + k, k % 2
                    c = Tally(s_dv, 1 + n * PER)
                    cols = bass.ds(n * U, U)
                    until(v, s_lp, n + 1)
                    scores = psL[par][:, 0:U * E].rearrange("p (i e) -> p i e", e=E)
                    link(v, c, v.tensor_reduce(mx[:, :], scores, AX.X, ALU.max))
                    v.tensor_tensor(d[:, :, :], scores, wide(mx), ALU.subtract).then_inc(s_lg, 1)
                    until(v, s_lg, n + 1)
                    link(v, c, v.tensor_scalar(cnd[:, :, :], d[:, :, :], 0.0, -float(E), ALU.is_ge, ALU.mult))
                    link(v, c, v.tensor_tensor(cnd[:, :, :], cnd[:, :, :], jrow[:, :, :].broadcast_to([P, U, E]), ALU.add))
                    link(v, c, v.tensor_reduce(mn[:, :], cnd[:, :, :], AX.X, ALU.min))
                    v.tensor_tensor(ohb[:, :, :], cnd[:, :, :], wide(mn), ALU.is_equal).then_inc(s_oh, 1)
                    c.inc(v.tensor_scalar(idx[:, :], mn[:, :], float(E), None, ALU.add))
                    if k + 1 < SETS:
                        until(v, s_left, it * SETS + max(k - 2, 0))
                        norm(n + 1, k + 1)
                    until(v, s_ex, n + 1)
                    link(v, c, v.tensor_reduce(ssum[:, :], ex[:, :, :], AX.X, ALU.add))
                    link(v, c, v.reciprocal(ssum[:, :], ssum[:, :]))
                    until(v, s_cum, n + 1)
                    within = psC[par][:, 0:U * E].rearrange("p (i e) -> p i e", e=E)
                    whole = psC[par][:, U * E:2 * U * E].rearrange("p (i e) -> p e i", e=E)
                    link(v, c, v.tensor_copy(tot[:, :, :], whole))
                    link(v, c, v.tensor_tensor(tot[:, :, 0], tot[:, :, 0], carry[:, :], ALU.add))
                    link(v, c, v.tensor_tensor_scan(fl(pre), reset[:, :], fl(tot), 0.0, ALU.mult, ALU.add))
                    link(v, c, v.tensor_copy(carry[:, :], pre[:, :, U - 1]))
                    link(v, c, v.tensor_tensor(pre[:, :, :], pre[:, :, :], whole, ALU.subtract))
                    link(v, c, v.tensor_tensor(posm[:, :, :], within, pre[:, :, :].rearrange("p e i -> p i e"), ALU.add))
                    link(v, c, v.tensor_tensor(posm[:, :, :], posm[:, :, :], ohb[:, :, :], ALU.mult))
                    link(v, c, v.tensor_reduce(pos1[:, :], posm[:, :, :], AX.X, ALU.add))
                    c.inc(v.tensor_scalar(kept[:, :], pos1[:, :], float(CAP), None, ALU.is_le))
                    link(v, c, v.tensor_scalar(slot[:, :], pos1[:, :], float(CAP), -1.0, ALU.min, ALU.add))
                    v.tensor_scalar(g.nk[:, cols], kept[:, :], -1.0, 1.0, ALU.mult, ALU.add)
                    v.tensor_tensor(g.fe[:, cols], kept[:, :], ssum[:, :], ALU.mult)
                    link(v, c, v.scalar_tensor_tensor(gf[:, :], idx[:, :], float(CAP), slot[:, :], ALU.mult, ALU.add))
                    v.tensor_copy(g.gidx[:, cols], gf[:, :])
                    link(v, c, v.tensor_scalar(tr[:, :], gf[:, :], -1.0, trash[:, :], ALU.mult, ALU.add))
                    link(v, c, v.tensor_tensor(tr[:, :], tr[:, :], g.nk[:, cols], ALU.mult))
                    assert c.n == PER - 1
                    link(v, c, v.tensor_tensor(sidx[:, :], tr[:, :], gf[:, :], ALU.add))
                    for j in range(U):
                        v.tensor_copy(at[k * U + j][:, :], sidx[:, j:j + 1]).then_inc(s_row, 1)

                until(v, s_w, 16 * len(loads))
                v.memset(carry[:, :], 0.0).then_inc(s_dv, 1)
                assert NG // SETS <= SETS - 1
                with v.Fori(0, NG // SETS) as it:
                    until(v, s_left, it * (SETS - 1))
                    norm(it * SETS, 0)
                    for k in range(SETS):
                        group(it, k)


def experts(nc, g, dram, tag, w1, w2, s_w):
    BLK, PAIR = 256, 2
    NB = CAP // BLK
    NK = PAIR * NB
    BT = BLK // P
    ET = CAP // P
    with ExitStack() as stack:
        m = Mem(nc, stack, tag)
        rows = [m.sb(f"rows{q}", [P, ET, D]) for q in range(PAIR)]
        out = [m.sb(f"out{q}", [P, ET, D]) for q in range(PAIR)]
        xT = [m.sb(f"xT{q}", [P, DC, BLK]) for q in range(2)]
        h = [m.sb(f"h{q}", [P, FC, BLK]) for q in range(2)]
        psX = [m.ps(f"psX{q}") for q in range(2)]
        psH = [m.ps(f"psH{q}") for q in range(4)]
        psO = [m.ps(f"psO{q}") for q in range(2)]
        s_in = [m.sem(f"s_in{q}") for q in range(PAIR)]
        s_out = [m.sem(f"s_out{q}") for q in range(PAIR)]
        s_t, s_x, s_m1, s_h, s_m2, s_o = (m.sem(n) for n in ("s_t", "s_x", "s_m1", "s_h", "s_m2", "s_o"))
        m.start()
        with nc.Block() as block:
            @block.sync
            def _(sp):
                view = lambda t, e: dram[t][bass.ds(e * CAP, CAP), :].rearrange("(p j) d -> p j d", j=ET)

                def load_rows(e, q):
                    sp.dma_start(rows[q][:, :, :], view("slots", e)).then_inc(s_in[q], 16)

                def store(e, q):
                    until(sp, s_o, e * NB + NB)
                    sp.dma_start(view("eout", e), out[q][:, :, :]).then_inc(s_out[q], 16)

                load_rows(0, 0)
                load_rows(1, 1)
                with sp.Fori(0, E // PAIR - 1) as it:
                    for q in range(PAIR):
                        until(sp, s_m2, it * NK + (q + 1) * NB)
                        load_expert(sp, dram, w1[q], w2[q], s_w[q], it * PAIR + q + PAIR)
                        load_rows(it * PAIR + q + PAIR, q)
                        store(it * PAIR + q, q)
                for q in range(PAIR):
                    store(E - PAIR + q, q)
                for q in range(PAIR):
                    until(sp, s_out[q], 16 * E // PAIR)

            @block.tensor
            def _(pe):
                with pe.Fori(0, E // PAIR) as it:
                    def turn(k):
                        q = k // NB
                        until(pe, s_in[q], it * 16 + 16)
                        until(pe, s_x, it * NK + max(k - 1, 0))
                        for j in range(BT):
                            for c in range(DC):
                                last = nc.tensor.transpose(psX[k % 2][:, c * BLK + j * P:c * BLK + (j + 1) * P],
                                                           rows[q][:, (k % NB) * BT + j, c * P:(c + 1) * P], g.ident[:, :])
                        last.then_inc(s_t, 1)

                    def up(k):
                        q = k // NB
                        until(pe, s_x, it * NK + k + 1)
                        until(pe, s_w[q], it * 32 + 32)
                        for f in range(FC):
                            bank, half = psH[f // 2], f % 2
                            if half == 0:
                                until(pe, s_h, it * NK * 4 + max((k - 1) * 4 + f // 2 + 1, 0))
                            for c in range(DC):
                                last = nc.tensor.matmul(bank[:, half * BLK:(half + 1) * BLK], w1[q][:, c, f * P:(f + 1) * P],
                                                        xT[k % 2][:, c, :], start=(c == 0), stop=(c == DC - 1))
                            if half:
                                last.then_inc(s_m1, 1)

                    def down(k):
                        q = k // NB
                        until(pe, s_h, it * NK * 4 + 4 * k + 4)
                        until(pe, s_o, it * NK + max(k - 1, 0))
                        for j in range(BT):
                            for f in range(FC):
                                last = nc.tensor.matmul(psO[k % 2][:, j * D:(j + 1) * D], h[k % 2][:, f, j * P:(j + 1) * P],
                                                        w2[q][:, f, :], start=(f == 0), stop=(f == FC - 1))
                        last.then_inc(s_m2, 1)

                    for k in range(NK):
                        turn(k)
                        if k:
                            up(k - 1)
                        if k > 1:
                            down(k - 2)
                    up(NK - 1)
                    down(NK - 2)
                    down(NK - 1)

            @block.scalar
            def _(a):
                with a.Fori(0, E // PAIR) as it:
                    for k in range(NK):
                        for q in range(4):
                            until(a, s_m1, it * NK * 4 + 4 * k + q + 1)
                            until(a, s_m2, it * NK + max(k - 1, 0))
                            a.activation(h[k % 2][:, 2 * q:2 * q + 2, :], psH[q][:, :].rearrange("p (f t) -> p f t", f=2),
                                         ACT.Relu).then_inc(s_h, 1)

            @block.vector
            def _(v):
                with v.Fori(0, E // PAIR) as it:
                    def copy_turned(k):
                        until(v, s_t, it * NK + k + 1)
                        until(v, s_m1, it * NK * 4 + max(4 * (k - 1), 0))
                        v.tensor_copy(xT[k % 2][:, :, :], psX[k % 2][:, :].rearrange("p (c t) -> p c t", c=DC)).then_inc(s_x, 1)

                    def copy_out(k):
                        q = k // NB
                        until(v, s_m2, it * NK + k + 1)
                        until(v, s_out[q], it * 16)
                        v.tensor_copy(out[q][:, (k % NB) * BT:(k % NB + 1) * BT, :],
                                      psO[k % 2][:, :].rearrange("p (j d) -> p j d", j=BT)).then_inc(s_o, 1)

                    for k in range(NK):
                        copy_turned(k)
                        if k > 1:
                            copy_out(k - 2)
                    copy_out(NK - 2)
                    copy_out(NK - 1)


def combine(nc, g, dram, tag, out):
    U = 8
    NI = NT // (2 * U)
    with ExitStack() as stack:
        m = Mem(nc, stack, tag)
        at = [m.sb(f"at{j}", [P, 1], U32) for j in range(2 * U)]
        got = [m.sb(f"got{j}", [P, D]) for j in range(2 * U)]
        t = [m.sb(f"t{j}", [P, D]) for j in range(2 * U)]
        nmean, nkr = m.sb("nmean", [P, NT]), m.sb("nkr", [P, NT])
        s_at, s_use, s_t, s_a, s_nm, s_tick = (m.sem(n) for n in ("s_at", "s_use", "s_t", "s_a", "s_nm", "s_tick"))
        s_get = [m.sem(f"s_get{j}", moved=True) for j in range(2 * U)]
        s_out = m.sem("s_out")
        m.start()
        with nc.Block() as block:
            if out is not None:
                @block.sync
                def _(sp):
                    for b in range(B):
                        until(sp, s_use, (b + 1) * TB)
                        sp.dma_start(out[S * b:S * b + S, :].rearrange("(i p) d -> p i d", p=P),
                                     g.xres[:, TB * b:TB * b + TB, :]).then_inc(s_out, 16)
                    until(sp, s_out, 16 * B)

            @block.gpsimd
            def _(p_):
                w = Waits(p_, s_tick)
                with p_.Fori(0, NI) as it:
                    for j in range(2 * U):
                        w.ge(s_at, it * 2 * U + j + 1)
                        if j % U == 0:
                            w.ge(s_use, it * 2 * U + max(j - U, 0))
                        p_.indirect_dma_start(got[j][:, :], None, dram["eout"],
                                              bass.IndirectOffsetOnAxis(ap=at[j][:, :], axis=0)).then_inc(s_get[j], 16)

            @block.scalar
            def _(a):
                until(a, s_nm, 2)
                with a.Fori(0, NI) as it:
                    for j in range(2 * U):
                        i = it * 2 * U + j
                        if j % U == 0:
                            until(a, s_use, it * 2 * U + max(j - U, 0))
                        a.activation(t[j][:, :], g.xres[:, bass.ds(i, 1), :].rearrange("p o d -> p (o d)"), ACT.Identity,
                                     bias=nmean[:, bass.ds(i, 1)]).then_inc(s_t, 1)

            @block.vector
            def _(v):
                def slots(it, group):
                    for j in range(group * U, group * U + U):
                        v.tensor_copy(at[j][:, :], g.gidx[:, bass.ds(it * 2 * U + j, 1)]).then_inc(s_at, 1)

                def add(it, group):
                    js = range(group * U, group * U + U)
                    i = [it * 2 * U + j for j in range(2 * U)]
                    x = [g.xres[:, bass.ds(k, 1), :].rearrange("p o d -> p (o d)") for k in i]
                    for j in js:
                        until(v, s_t, i[j] + 1)
                        v.scalar_tensor_tensor(t[j][:, :], t[j][:, :], nkr[:, bass.ds(i[j], 1)], x[j], ALU.mult, ALU.add).then_inc(s_a, 1)
                    for j in js:
                        until(v, s_a, i[j] + 1)
                        until_moved(v, s_get[j], it * 16 + 16)
                        v.scalar_tensor_tensor(x[j], got[j][:, :], g.fe[:, bass.ds(i[j], 1)], t[j][:, :], ALU.mult, ALU.add).then_inc(s_use, 1)
                    if out is None:
                        for j in js:
                            until(v, s_use, i[j] + 1)
                            v.bn_stats(g.st[:, bass.ds(i[j], 1), :], g.xres[:, bass.ds(i[j], 1), :])

                slots(0, 0)
                slots(0, 1)
                v.tensor_scalar(nmean[:, :], g.mean[:, :], -1.0, None, ALU.mult).then_inc(s_nm, 1)
                v.tensor_tensor(nkr[:, :], g.nk[:, :], g.rstd[:, :], ALU.mult).then_inc(s_nm, 1)
                until(v, s_nm, 2)
                with v.Fori(0, NI - 1) as it:
                    for group in range(2):
                        add(it, group)
                        slots(it + 1, group)
                for group in range(2):
                    add(NI - 1, group)


def load_expert(sp, dram, w1, w2, sem, e):
    sp.dma_start(w1[:, :, :], dram["W1"][bass.ds(e * D, D), :].rearrange("(c p) f -> p c f", p=P)).then_inc(sem, 16)
    sp.dma_start(w2[:, :, :], dram["W2"][bass.ds(e * FF, FF), :].rearrange("(c p) f -> p c f", p=P)).then_inc(sem, 16)


def moe_layer(nc, g, dram, tag, s_fill=None, out=None, taken=False):
    with ExitStack() as stack:
        m = Mem(nc, stack, tag)
        w1 = [m.sb(f"w1{q}", [P, DC, FF]) for q in range(2)]
        w2 = [m.sb(f"w2{q}", [P, FC, D]) for q in range(2)]
        s_w = [m.sem(f"s_w{q}") for q in range(2)]
        m.start()
        for q in range(2):
            load_expert(nc.sync, dram, w1[q], w2[q], s_w[q], q)
        norm_stats(nc, g, tag + "n_", taken=taken)
        route(nc, g, dram, tag + "r_", s_fill)
        experts(nc, g, dram, tag + "e_", w1, w2, s_w)
    combine(nc, g, dram, tag + "c_", out)


class Event:

    def __init__(self, sem, per):
        self.sem, self.per = sem, per

    def wait(self, eng, it, i):
        until(eng, self.sem, it * self.per + i + 1)

    def wait_all_before(self, eng, it):
        until(eng, self.sem, it * self.per)


class Banks:

    LAST = "last"

    def __init__(self, m, first, body, end, turns):
        self.bank = [m.ps(f"bank{q}") for q in range(8)]
        self.full = [m.sem(f"s_full{q}") for q in range(8)]
        self.free = [m.sem(f"s_free{q}") for q in range(8)]
        self.turns, self.key = turns, {}
        self.first, self.used_first = self.deal(first)
        self.body, self.used_body = self.deal(body)
        self.end, _ = self.deal(end)

    def deal(self, plan):
        where, uses = {}, [0] * 8
        for n, name in enumerate(plan):
            where[name] = (n % 8, uses[n % 8])
            uses[n % 8] += 1
        return where, uses

    def use(self, it, name):
        if it is None:
            return self.first[name]
        if isinstance(it, str):
            q, k = self.end[name]
            return q, self.used_first[q] + self.turns * self.used_body[q] + k
        q, k = self.body[name]
        return q, it * self.used_body[q] + (self.used_first[q] + k)

    def fill(self, pe, it, name):
        q, before = self.use(it, name)
        until(pe, self.free[q], before)
        return self.bank[q]

    def filled(self, ins, it, name):
        ins.then_inc(self.full[self.use(it, name)[0]], 1)

    def read(self, eng, it, name):
        q, before = self.use(it, name)
        until(eng, self.full[q], before + 1)
        return self.bank[q]

    def released(self, eng, it, name):
        eng.sem_inc(self.free[self.use(it, name)[0]], 1)


def gla_layer(nc, g, dram):
    C, G, HP = TB, 4, 32
    HG = H // G
    with ExitStack() as stack:
        m = Mem(nc, stack, "gla_")
        Wqkv = m.sb("Wqkv", [P, DC, 3 * D])
        Wgf = m.sb("Wgf", [P, DC, 48])
        Wg2T = m.sb("Wg2T", [HD, D])
        WoT = m.sb("WoT", [P, DC, D])
        lnw = m.sb("lnw", [P, DC])
        trif = m.sb("trif", [P, P])
        onef = m.sb("onef", [P, P])
        identb = m.sb("identb", [P, P], BF16)
        later = m.sb("later", [P, HALF], BF16)
        heads = m.sb("heads", [96, H * P], BF16)
        bmask = m.sb("bmask", [P, D])
        hmask = m.sb("hmask", [P, HG])
        xn2 = [m.sb(f"xn{j}", [P, 2, D]) for j in range(2)]
        xn = [xn2[j // 2][:, j % 2, :] for j in range(4)]
        xnT = m.sb("xnT", [P, DC, S])
        gz = m.sb("gz", [48, S])
        th = [m.sb(f"th{j}", [P, HALF]) for j in range(2)]
        tv = m.sb("tv", [P, 2, D])
        qpad = m.sb("qpad", [P, C * H, HP])
        kpad = m.sb("kpad", [P, C * H, HP])
        ktil = [m.sb(f"ktil{j}", [P, H, HP]) for j in range(2)]
        v2 = m.sb("v2", [P, C * D + HD])
        gt = m.sb("gt", [P, C, D])
        og = gt
        small = lambda n: m.sb(n, [P, C * H])
        zc, za, ze, zl, zr, f = (small(n) for n in ("zc", "za", "ze", "zl", "zr", "f"))
        f3 = m.sb("f3", [P, C, 3, HP])
        n2, nl, ny, nt, rn = (small(n) for n in ("n2", "nl", "ny", "nt", "rn"))
        Ft, dF, eF, dec, wk = (small(n) for n in ("Ft", "dF", "eF", "dec", "wk"))
        ftv = m.sb("ftv", [96, HALF])
        ftr = m.sb("ftr", [96, HALF])
        FP = m.sb("FP", [96, S], BF16)
        FN = m.sb("FN", [96, S], BF16)
        qT = [m.sb(f"qT{j}", [P, G, P]) for j in range(3)]
        kT = [m.sb(f"kT{j}", [P, G, P]) for j in range(3)]
        Dg = [m.sb(f"Dg{j}", [P, HG, P]) for j in range(2)]
        odd = m.sb("odd", [P, G, HALF])
        sq = odd[:, :, :].rearrange("p g t -> p (g t)").rearrange("p (h k) -> p h k", k=HD)
        Ag = [t.rearrange("p (h t) -> p h t", h=HG) for t in
              [xnT[:, q // 2, (q % 2) * HALF:(q % 2 + 1) * HALF] for q in range(G)] + [odd[:, q, :] for q in range(G)]]
        St = [m.sb(f"St{j}", [P, H, HD]) for j in range(2)]
        Um = m.sb("Um", [P, H, HD])
        Sd = m.sb("Sd", [P, H, HD])
        o1 = [m.sb(f"o1{j}", [P, H, HD]) for j in range(2)]
        bst = m.sb("bst", [P, C, 6])
        bdm, bq, bve, bl, by, bt, bmean, brs = (m.sb(n, [P, C]) for n in ("bdm", "bq", "bve", "bl", "by", "bt", "bmean", "brs"))
        onT = th
        Qd = [t[:, :].rearrange("p (h t) -> p h t", h=HG) for t in th] + \
             [t[:, :, :].rearrange("p a b -> p (a b)").rearrange("p (h t) -> p h t", h=HG) for t in xn2]
        oT = tv[:, :, :].rearrange("p a b -> p (a b)")

        start = [f"x{j}" for j in range(4)] + ["g0", "g1", "zf"]
        plan = ["Fn", "FT0", "FT1"]
        for c in range(C):
            plan += [f"qk{c}", f"vg{c}"]
        plan += ["qT0", "kT0"]
        for c in range(C):
            if c + 1 < C:
                plan += [f"qT{c + 1}", f"kT{c + 1}"]
            for q in range(G):
                plan += [f"S{c}{q}", f"G{c}{q}"]
                if c and q == 1:
                    plan += [f"t{c - 1}", f"i{c - 1}"]
                if c and q == 2:
                    plan += [f"o{c - 1}"]
            if c + 1 < C:
                plan += [f"U{c}"]
        plan += [f"t{C - 1}", f"i{C - 1}", f"o{C - 1}"]
        end = [f"n{j}" for j in range(4)] + [f"W{j}" for j in range(4)]
        banks = Banks(m, start, plan + start + end, plan + end, B - 1)

        def run(eng, prepare, batch):
            prepare(0, None)
            with eng.Fori(0, B - 1) as b:
                batch(b, b)
            batch(B - 1, Banks.LAST)

        ev = lambda name, per: Event(m.sem("s_" + name), per)
        e_xn, e_xp, e_xT, e_g1, e_th, e_tv, e_gt = ev("xn", C), ev("xp", C), ev("xT", 4), ev("g1", 2), ev("th", C), ev("tv", C), ev("gt", C)
        e_q, e_k, e_v = ev("q", C), ev("k", C), ev("v", C)
        e_zc, e_za, e_ze, e_zl, e_zr, e_f3, e_n2, e_nl, e_ny, e_f = (ev(n, 1) for n in ("zc", "za", "ze", "zl", "zr", "f3", "n2", "nl", "ny", "f"))
        e_kp = ev("kp", C)
        e_Ft, e_dF, e_wk, e_ftv, e_FP, e_FN = ev("Ft", 3), ev("dF", 1), ev("wk", 1), ev("ftv", 2), ev("FP", 2), ev("FN", 2)
        e_qT, e_kT, e_kt, e_D, e_A, e_au = ev("qT", C), ev("kT", C), ev("kt", C - 1), ev("D", C * G), ev("A", C * G), ev("au", C)
        e_st, e_og, e_tp, e_bv, e_bl, e_by, e_on, e_onp, e_onT, e_x, e_U = (
            ev("st", C), ev("og", C), ev("tp", C), ev("bv", 1), ev("bl", 1), ev("by", 1), ev("on", C), ev("onp", 4), ev("onT", 4),
            ev("x", 4), ev("U", C - 1))
        e_Qd, e_oT = ev("Qd", C * G), ev("oT", C)
        s_w, s_pre, s_dv, s_split, s_tick, s_pre8, s_ln = (m.sem(n) for n in ("s_w", "s_pre", "s_dv", "s_split", "s_tick", "s_chunk", "s_ln"))
        loads = [(Wqkv[:, :, :], dram["Wqkv"].rearrange("(c p) n -> p c n", p=P)), (Wgf[:, :, :], dram["Wgf"].rearrange("(c p) n -> p c n", p=P)),
                 (Wg2T[:, :], dram["Wg2T"]),
                 (WoT[:, :, :], dram["WoT"].rearrange("(c p) n -> p c n", p=P)), (lnw[:, :], dram["ln_w"]),
                 (trif[:, :], dram["trif"]), (onef[:, :], dram["onef"]), (identb[:, :], dram["identb"].bitcast(BF16)),
                 (later[:, :], dram["later"].bitcast(BF16)), (heads[:, :], dram["heads"].bitcast(BF16)), (bmask[:, :], dram["bmask"]),
                 (hmask[:, :], dram["hmask"])]
        flat = lambda t: t[:, :, :].rearrange("p a b -> p (a b)")

        m.start()
        with nc.Block() as block:
            @block.sync
            def _(sp):
                for out, src in loads:
                    sp.dma_start(out, src).then_inc(s_w, 16)

            @block.tensor
            def _(pe):
                until(pe, s_w, 16 * len(loads))
                until(pe, s_pre, 1)
                def prepare(b, key):
                    fill = lambda name: banks.fill(pe, key, name)
                    for jp in range(4):
                        bank = fill(f"x{jp}")
                        for jj in range(2):
                            e_xn.wait(pe, b, 2 * jp + jj)
                            for c in range(DC):
                                last = nc.tensor.transpose(bank[:, c * 256 + jj * P:c * 256 + jj * P + P],
                                                           xn[(2 * jp + jj) % 4][:, c * P:c * P + P], g.ident[:, :])
                        banks.filled(last, key, f"x{jp}")
                    e_xT.wait(pe, b, 3)
                    for h in range(2):
                        bank = fill(f"g{h}")
                        for k in range(DC):
                            last = nc.tensor.matmul(bank[0:48, :], Wgf[:, k, :], xnT[:, k, h * HALF:(h + 1) * HALF],
                                                    start=(k == 0), stop=(k == DC - 1))
                        banks.filled(last, key, f"g{h}")
                    bank = fill("zf")
                    for c in range(C):
                        e_g1.wait(pe, b, c // 4)
                        last = nc.tensor.matmul(bank[:, c * H:(c + 1) * H], gz[32:48, c * P:(c + 1) * P], g.ident[32:48, 32:48], start=True, stop=True)
                    banks.filled(last, key, "zf")

                def batch(b, key):
                    fill = lambda name: banks.fill(pe, key, name)
                    e_f3.wait(pe, b, 0)
                    bank = fill("Fn")
                    nc.tensor.matmul(bank[:, 0:C * H], trif[:, :], f[:, :], start=True, stop=True)
                    last = nc.tensor.matmul(bank[:, C * H:2 * C * H], onef[:, :], f[:, :], start=True, stop=True)
                    banks.filled(last, key, "Fn")
                    for h in range(2):
                        bank = fill(f"FT{h}")
                        for q in range(4):
                            last = nc.tensor.matmul(bank[0:96, q * P:(q + 1) * P], f3[:, 4 * h + q, :, :].rearrange("p a b -> p (a b)"),
                                                    trif[:, :], start=True, stop=True)
                        banks.filled(last, key, f"FT{h}")
                    for c in range(C):
                        bank = fill(f"qk{c}")
                        for k in range(DC):
                            last = nc.tensor.matmul(bank[:, :], xnT[:, k, c * P:(c + 1) * P], Wqkv[:, k, 0:2 * D],
                                                    start=(k == 0), stop=(k == DC - 1))
                        banks.filled(last, key, f"qk{c}")
                        bank = fill(f"vg{c}")
                        for k in range(DC):
                            nc.tensor.matmul(bank[:, 0:D], xnT[:, k, c * P:(c + 1) * P], Wqkv[:, k, 2 * D:3 * D],
                                             start=(k == 0), stop=(k == DC - 1))
                        e_g1.wait(pe, b, c // 4)
                        last = nc.tensor.matmul(bank[:, D:2 * D], gz[0:HD, c * P:(c + 1) * P], Wg2T[:, :], start=True, stop=True)
                        banks.filled(last, key, f"vg{c}")
                    def turn(c):
                        e_q.wait(pe, b, c)
                        for name, pad in (("qT", qpad), ("kT", kpad)):
                            if name == "kT":
                                e_kp.wait(pe, b, c)
                            bank = fill(f"{name}{c}")
                            for q in range(G):
                                src = pad[:, c * H + HG * q:c * H + HG * (q + 1), :].rearrange("p a b -> p (a b)")
                                last = nc.tensor.transpose(bank[:, q * P:(q + 1) * P], src, g.ident[:, :])
                            banks.filled(last, key, f"{name}{c}")

                    def intra(c):
                        bank = fill(f"t{c}")
                        e_v.wait(pe, b, c)
                        for q in range(G):
                            e_A.wait(pe, b, c * G + q)
                            for j in range(HG):
                                w = c * D + (HG * q + j) * HD
                                last = nc.tensor.matmul(bank[HP * j:HP * (j + 1), q * P:(q + 1) * P], v2[:, w:w + HP],
                                                        Ag[(c % 2) * G + q][:, j, :], start=True, stop=True)
                        banks.filled(last, key, f"t{c}")

                    def inter(c):
                        bank = fill(f"i{c}")
                        e_st.wait(pe, b, c)
                        for q in range(G):
                            last = nc.tensor.matmul(bank[:, q * HG * HD:(q + 1) * HG * HD], qT[c % 3][:, q, :],
                                                    St[c % 2][:, HG * q:HG * (q + 1), :].rearrange("p a b -> p (a b)"), start=True, stop=True)
                        banks.filled(last, key, f"i{c}")

                    def turn_back(c):
                        bank = fill(f"o{c}")
                        e_oT.wait(pe, b, c)
                        for q in range(G):
                            last = nc.tensor.transpose(bank[:, q * P:(q + 1) * P], oT[:, q * P:(q + 1) * P], g.ident[:, :])
                        banks.filled(last, key, f"o{c}")

                    turn(0)
                    for c in range(C):
                        if c + 1 < C:
                            turn(c + 1)
                        e_qT.wait(pe, b, c)
                        e_kT.wait(pe, b, c)
                        e_FN.wait(pe, b, c // 4)
                        for q in range(G):
                            bank = fill(f"S{c}{q}")
                            e_Qd.wait(pe, b, c * G + q)
                            last = nc.tensor.matmul(bank[:, :], kT[c % 3][:, q, :], Qd[q].rearrange("p h t -> p (h t)"), start=True, stop=True)
                            banks.filled(last, key, f"S{c}{q}")
                            bank = fill(f"G{c}{q}")
                            nc.tensor.matmul(bank[:, :], identb[:, :], later[:, :], start=True, stop=False)
                            for j in range(HG):
                                h = HG * q + j
                                nc.tensor.matmul(bank[:, j * P:(j + 1) * P], heads[:, h * P:(h + 1) * P], FP[:, c * P:(c + 1) * P],
                                                 start=False, stop=False, skip_group_check=True)
                            last = nc.tensor.matmul(bank[:, :], FN[:, c * P:(c + 1) * P], heads[:, q * HALF:(q + 1) * HALF],
                                                    start=False, stop=True)
                            banks.filled(last, key, f"G{c}{q}")
                            if c and q == 1:
                                intra(c - 1)
                                inter(c - 1)
                            if c and q == 2:
                                turn_back(c - 1)
                        if c + 1 == C:
                            break
                        bank = fill(f"U{c}")
                        e_kt.wait(pe, b, c)
                        e_v.wait(pe, b, c)
                        for q in range(G):
                            w = slice(q * HG * HD, (q + 1) * HG * HD)
                            last = nc.tensor.matmul(bank[:, w], ktil[c % 2][:, HG * q:HG * (q + 1), :].rearrange("p a b -> p (a b)"),
                                                    v2[:, c * D + q * HG * HD:c * D + (q + 1) * HG * HD], start=True, stop=True)
                        banks.filled(last, key, f"U{c}")
                    intra(C - 1)
                    inter(C - 1)
                    turn_back(C - 1)
                    if key is not Banks.LAST:
                        prepare(b + 1, key)
                    for jp in range(4):
                        bank = fill(f"n{jp}")
                        for jj in range(2):
                            e_on.wait(pe, b, 2 * jp + jj)
                            for c in range(DC):
                                last = nc.tensor.transpose(bank[:, c * 256 + jj * P:c * 256 + jj * P + P],
                                                           og[:, 2 * jp + jj, c * P:(c + 1) * P], g.ident[:, :])
                        banks.filled(last, key, f"n{jp}")
                    for jp in range(4):
                        e_onT.wait(pe, b, jp)
                        bank = fill(f"W{jp}")
                        for jj in range(2):
                            for k in range(DC):
                                last = nc.tensor.matmul(bank[:, jj * D:(jj + 1) * D], onT[jp % 2][:, k * 256 + jj * P:k * 256 + jj * P + P],
                                                        WoT[:, k, :], start=(k == 0), stop=(k == DC - 1))
                        banks.filled(last, key, f"W{jp}")

                run(pe, prepare, batch)

            @block.scalar
            def _(a):
                a.preload_act_table_set("natural_log_exp_and_others")

                def prepare(b, key):
                    read = lambda name: banks.read(a, key, name)
                    for jp in range(4):
                        bank = read(f"x{jp}")
                        if jp == 0:
                            e_oT.wait_all_before(a, b)
                        a.activation(xnT[:, :, jp * 256:(jp + 1) * 256], bank[:, :].rearrange("p (c t) -> p c t", c=DC),
                                     ACT.Copy).then_inc(e_xT.sem, 1)
                        e_xT.wait(a, b, jp)
                        banks.released(a, key, f"x{jp}")
                    for h in range(2):
                        bank = read(f"g{h}")
                        a.activation(gz[:, h * HALF:(h + 1) * HALF], bank[0:48, :], ACT.Copy).then_inc(e_g1.sem, 1)
                        e_g1.wait(a, b, h)
                        banks.released(a, key, f"g{h}")
                    bank = read("zf")
                    e_f3.wait_all_before(a, b)
                    a.activation(zc[:, :], bank[:, 0:C * H], ACT.Copy).then_inc(e_zc.sem, 1)
                    e_zc.wait(a, b, 0)
                    banks.released(a, key, "zf")
                    a.activation(za[:, :], zc[:, :], ACT.Abs).then_inc(e_za.sem, 1)
                    e_za.wait(a, b, 0)
                    a.activation(ze[:, :], za[:, :], ACT.Exp, scale=-1.0).then_inc(e_ze.sem, 1)
                    e_ze.wait(a, b, 0)
                    a.activation(zl[:, :], ze[:, :], ACT.Ln, bias=1.0).then_inc(e_zl.sem, 1)

                def batch(b, key):
                    read = lambda name: banks.read(a, key, name)
                    bank = read("Fn")
                    e_kt.wait_all_before(a, b)
                    a.activation(Ft[:, :], bank[:, C * H:2 * C * H], ACT.Copy).then_inc(e_Ft.sem, 1)
                    a.activation(eF[:, :], bank[:, 0:C * H], ACT.Exp).then_inc(e_Ft.sem, 1)
                    a.activation(dec[:, :], bank[:, C * H:2 * C * H], ACT.Exp).then_inc(e_Ft.sem, 1)
                    for h in range(2):
                        bank = read(f"FT{h}")
                        if h:
                            e_FP.wait(a, b, 0)
                        a.activation(ftv[:, :], bank[0:96, :], ACT.Copy).then_inc(e_ftv.sem, 1)
                        e_ftv.wait(a, b, h)
                        banks.released(a, key, f"FT{h}")
                        if h == 0:
                            e_dF.wait(a, b, 0)
                            a.activation(wk[:, :], dF[:, :], ACT.Exp).then_inc(e_wk.sem, 1)

                    def negate(h):
                        e_FP.wait(a, b, h)
                        a.activation(FN[:, h * HALF:(h + 1) * HALF], FP[:, h * HALF:(h + 1) * HALF], ACT.Copy, scale=-1.0).then_inc(e_FN.sem, 1)

                    negate(0)
                    for c in range(C):
                        bank = read(f"qk{c}")
                        if c >= 2:
                            e_k.wait(a, b, c - 2)
                        elif c == 0:
                            e_x.wait_all_before(a, b)
                        a.activation(th[c % 2][:, :], bank[:, :], ACT.Tanh, scale=0.5).then_inc(e_th.sem, 1)
                        bank = read(f"vg{c}")
                        if c >= 2:
                            e_v.wait(a, b, c - 2)
                        a.activation(tv[:, c % 2, :], bank[:, 0:D], ACT.Tanh, scale=0.5)
                        a.activation(gt[:, c, :], bank[:, D:2 * D], ACT.Tanh, scale=0.5).then_inc(e_tv.sem, 1)
                    a.preload_act_table_set("natural_log_exp_and_others")
                    e_n2.wait(a, b, 0)
                    a.activation(nl[:, :], n2[:, :], ACT.Ln, scale=float(2 ** 20)).then_inc(e_nl.sem, 1)
                    e_nl.wait(a, b, 0)
                    a.activation(ny[:, :], nl[:, :], ACT.Exp, scale=-0.5).then_inc(e_ny.sem, 1)
                    def copies(c):
                        for name, out, e in (("qT", qT, e_qT), ("kT", kT, e_kT)):
                            bank = read(f"{name}{c}")
                            if c >= 3:
                                e_og.wait(a, b, c - 3)
                            a.activation(out[c % 3][:, :, :], bank[:, :].rearrange("p (g t) -> p g t", g=G), ACT.Copy).then_inc(e.sem, 1)
                            e.wait(a, b, c)
                            banks.released(a, key, f"{name}{c}")

                    def copy_intra(c):
                        bank = read(f"t{c}")
                        if c:
                            e_og.wait(a, b, c - 1)
                        a.activation(oT[:, :], bank[:, :], ACT.Copy).then_inc(e_oT.sem, 1)
                        e_oT.wait(a, b, c)
                        banks.released(a, key, f"t{c}")

                    copies(0)
                    for c in range(C):
                        if c + 1 < C:
                            copies(c + 1)
                        for q in range(G):
                            n = c * G + q
                            bank = read(f"G{c}{q}")
                            if n >= 2:
                                e_A.wait(a, b, n - 2)
                            else:
                                e_A.wait_all_before(a, b)
                            a.activation(Dg[q % 2][:, :, :], bank[:, :].rearrange("p (h t) -> p h t", h=HG), ACT.Exp).then_inc(e_D.sem, 1)
                            e_D.wait(a, b, n)
                            banks.released(a, key, f"G{c}{q}")
                            if c and q == 1:
                                copy_intra(c - 1)
                        if c == 0:
                            negate(1)
                    copy_intra(C - 1)
                    e_bv.wait(a, b, 0)
                    a.activation(bl[:, :], bve[:, :], ACT.Ln).then_inc(e_bl.sem, 1)
                    e_bl.wait(a, b, 0)
                    a.activation(by[:, :], bl[:, :], ACT.Exp, scale=-0.5).then_inc(e_by.sem, 1)
                    if key is not Banks.LAST:
                        prepare(b + 1, key)
                    for jp in range(4):
                        bank = read(f"n{jp}")
                        if jp >= 2:
                            read(f"W{jp - 2}")
                        a.activation(onT[jp % 2][:, :], bank[:, :], ACT.Copy).then_inc(e_onT.sem, 1)
                        e_onT.wait(a, b, jp)
                        banks.released(a, key, f"n{jp}")

                run(a, prepare, batch)

            @block.gpsimd
            def _(p_):
                w = Waits(p_, s_tick)
                def batch(b, key):
                    w.ge(e_wk.sem, b + 1)
                    w.ge(e_kp.sem, b * C + 1)

                    def spread(c):
                        w.ge(e_qT.sem, b * C + c + 1)
                        for q in range(G):
                            if c:
                                bank, before = banks.use(key, f"S{c - 1}{q}")
                                w.ge(banks.full[bank], before + 1)
                            p_.tensor_tensor(Qd[q], qT[c % 3][:, q, :].unsqueeze(1).broadcast_to([P, HG, P]),
                                             hmask[:, :].unsqueeze(2).broadcast_to([P, HG, P]), ALU.mult).then_inc(e_Qd.sem, 1)

                    spread(0)
                    for c in range(C - 1):
                        if c >= 2:
                            w.ge(e_U.sem, b * e_U.per + c - 1)
                        w.ge(e_kp.sem, b * C + c + 1)
                        wide = wk[:, c * H:(c + 1) * H].unsqueeze(2).broadcast_to([P, H, HD])
                        p_.tensor_tensor(ktil[c % 2][:, :, 0:HD], kpad[:, c * H:(c + 1) * H, 0:HD], wide, ALU.mult).then_inc(e_kt.sem, 1)
                        spread(c + 1)

                run(p_, lambda b, key: None, batch)

            @block.vector
            def _(v):
                c0 = Tally(s_dv)
                until(v, s_w, 16 * len(loads))
                for t in (qpad, kpad):
                    c0.inc(v.memset(t[:, :, :], 0.0))
                for t in ktil:
                    c0.inc(v.memset(t[:, :, :], 0.0))
                c0.inc(v.memset(f3[:, :, :, :], 0.0))
                c0.inc(v.memset(v2[:, C * D:], 0.0))
                for c in range(DC):
                    c0.inc(v.tensor_scalar(WoT[:, c, :], WoT[:, c, :], lnw[:, c:c + 1], None, ALU.mult))
                until(v, s_dv, c0.n)
                v.sem_inc(s_pre, 1)
                pre = c0.n
                PER = 2 * C + 5

                def prepare(b, key):
                    for j in range(C):
                        if j >= 4:
                            banks.read(v, key, f"x{(j - 4) // 2}")
                        norm_tile(v, g, xn[j % 4], b * TB + j).then_inc(e_xn.sem, 1)
                    e_zc.wait(v, b, 0)
                    v.tensor_scalar(zr[:, :], zc[:, :], -1.0, 0.0, ALU.mult, ALU.max).then_inc(e_zr.sem, 1)
                    e_zr.wait(v, b, 0)
                    e_zl.wait(v, b, 0)
                    v.scalar_tensor_tensor(f[:, :], zr[:, :], -1.0, zl[:, :], ALU.mult, ALU.subtract).then_inc(e_f.sem, 1)
                    e_f.wait(v, b, 0)
                    wide = f[:, :].rearrange("p (c h) -> p c h", c=C).unsqueeze(2).broadcast_to([P, C, 3, H])
                    v.tensor_copy(f3[:, :, :, 0:H], wide).then_inc(e_f3.sem, 1)

                def batch(b, key):
                    t_ = Tally(s_dv, pre + b * PER)
                    read = lambda name: banks.read(v, key, name)
                    v.memset(St[0][:, :, :], 0.0).then_inc(e_st.sem, 1)
                    bank = read("Fn")
                    e_Ft.wait(v, b, 2)
                    v.tensor_tensor(dF[:, :], Ft[:, :], bank[:, 0:C * H], ALU.subtract).then_inc(e_dF.sem, 1)
                    e_dF.wait(v, b, 0)
                    banks.released(v, key, "Fn")
                    c_ = Tally(s_split, b * 8)
                    for h in range(2):
                        e_ftv.wait(v, b, h)
                        fp, fv, r = FP[:, h * HALF:(h + 1) * HALF], ftv[:, :], ftr[:, :]
                        link(v, c_, v.tensor_copy(fp, fv))
                        link(v, c_, v.tensor_tensor(r, fv, fp, ALU.subtract))
                        c_.inc(v.tensor_copy(fp[32:64, :], r[32:64, :]))
                        link(v, c_, v.tensor_copy(fp[64:96, :], r[64:96, :]))
                        v.tensor_tensor(fp[64:96, :], r[64:96, :], fp[64:96, :], ALU.subtract).then_inc(e_FP.sem, 1)
                        e_FP.wait(v, b, h)
                    for c in range(C):
                        e_th.wait(v, b, c)
                        bank = read(f"qk{c}")
                        hv = lambda ap: ap.rearrange("p (h k) -> p h k", h=H)
                        v.scalar_tensor_tensor(qpad[:, c * H:(c + 1) * H, 0:HD], hv(th[c % 2][:, 0:D]), 1.0, hv(bank[:, 0:D]),
                                               ALU.add, ALU.mult).then_inc(e_q.sem, 1)
                        v.scalar_tensor_tensor(kpad[:, c * H:(c + 1) * H, 0:HD], hv(th[c % 2][:, D:2 * D]), 1.0, hv(bank[:, D:2 * D]),
                                               ALU.add, ALU.mult).then_inc(e_k.sem, 1)
                        e_k.wait(v, b, c)
                        e_q.wait(v, b, c)
                        banks.released(v, key, f"qk{c}")
                        heads_of = slice(c * H, (c + 1) * H)
                        t_.inc(v.tensor_tensor(sq[:, heads_of, :], kpad[:, heads_of, 0:HD], kpad[:, heads_of, 0:HD], ALU.mult))
                        e_tv.wait(v, b, c)
                        bank = read(f"vg{c}")
                        v.scalar_tensor_tensor(v2[:, c * D:(c + 1) * D], tv[:, c % 2, :], 1.0, bank[:, 0:D], ALU.add, ALU.mult).then_inc(e_v.sem, 1)
                        e_v.wait(v, b, c)
                        banks.released(v, key, f"vg{c}")
                        until(v, t_.sem, t_.here())
                        t_.inc(v.tensor_reduce(n2[:, heads_of], sq[:, heads_of, :], AX.X, ALU.add))
                    until(v, t_.sem, t_.here())
                    v.tensor_scalar(n2[:, :], n2[:, :], 4e-24, None, ALU.max).then_inc(e_n2.sem, 1)
                    e_ny.wait(v, b, 0)
                    link(v, t_, v.tensor_scalar(ny[:, :], ny[:, :], 1024.0, None, ALU.mult))
                    link(v, t_, v.tensor_tensor(nt[:, :], ny[:, :], ny[:, :], ALU.mult))
                    link(v, t_, v.tensor_tensor(nt[:, :], nt[:, :], n2[:, :], ALU.mult))
                    link(v, t_, v.tensor_scalar(nt[:, :], nt[:, :], -0.5, 1.5, ALU.mult, ALU.add))
                    link(v, t_, v.tensor_tensor(rn[:, :], nt[:, :], ny[:, :], ALU.mult))
                    assert t_.n == PER

                    def unit(c):
                        heads_of = slice(c * H, (c + 1) * H)
                        v.tensor_tensor(kpad[:, heads_of, 0:HD], kpad[:, heads_of, 0:HD], rn[:, heads_of].unsqueeze(2).broadcast_to([P, H, HD]),
                                        ALU.mult).then_inc(e_kp.sem, 1)

                    unit(0)
                    unit(1)
                    def out_of_state(c):
                        held = read(f"i{c}")
                        hv = lambda ap: ap.rearrange("p (h k) -> p h k", h=H)
                        link(v, t8, v.tensor_tensor(o1[c % 2][:, :, :], hv(held[:, 0:D]), eF[:, c * H:(c + 1) * H].unsqueeze(2).broadcast_to([P, H, HD]), ALU.mult))
                        banks.released(v, key, f"i{c}")

                    def out_of(c):
                        turned, t1 = read(f"o{c}"), o1[c % 2]
                        link(v, t8, v.tensor_tensor(t1[:, :, :], t1[:, :, :], turned[:, :].rearrange("p (h k) -> p h k", k=HP)[:, :, 0:HD], ALU.add))
                        banks.released(v, key, f"o{c}")
                        v.scalar_tensor_tensor(og[:, c, :], gt[:, c, :], 1.0, flat(t1), ALU.add, ALU.mult).then_inc(e_og.sem, 1)
                        e_og.wait(v, b, c)
                        v.bn_stats(bst[:, c, :], og[:, c, :]).then_inc(e_tp.sem, 1)

                    t8 = Tally(s_pre8, b * (C * 4 - 2))
                    for c in range(C):
                        for q in range(G):
                            n = c * G + q
                            e_D.wait(v, b, n)
                            bank = read(f"S{c}{q}")
                            if c >= 2:
                                e_oT.wait(v, b, c - 2)
                            v.tensor_tensor(Ag[(c % 2) * G + q], bank[:, :].rearrange("p (h t) -> p h t", h=HG), Dg[q % 2][:, :, :],
                                            ALU.mult).then_inc(e_A.sem, 1)
                            e_A.wait(v, b, n)
                            banks.released(v, key, f"S{c}{q}")
                            if q == 1 and c + 2 < C:
                                unit(c + 2)
                            if c and q == 2:
                                out_of_state(c - 1)
                        if c:
                            out_of(c - 1)
                        if c + 1 == C:
                            break
                        bank = read(f"U{c}")
                        e_st.wait(v, b, c)
                        t8.inc(v.tensor_tensor(Um[:, :, :], bank[:, 0:D].rearrange("p (h k) -> p h k", h=H),
                                               bmask[:, :].rearrange("p (h k) -> p h k", h=H), ALU.mult))
                        link(v, t8, v.tensor_tensor(Sd[:, :, :], St[c % 2][:, :, :],
                                                    dec[:, c * H:(c + 1) * H].unsqueeze(2).broadcast_to([P, H, HD]), ALU.mult))
                        banks.released(v, key, f"U{c}")
                        v.sem_inc(e_U.sem, 1)
                        if c:
                            read(f"i{c - 1}")
                        v.tensor_tensor(St[(c + 1) % 2][:, :, :], Sd[:, :, :], Um[:, :, :], ALU.add).then_inc(e_st.sem, 1)
                    out_of_state(C - 1)
                    out_of(C - 1)
                    e_tp.wait(v, b, C - 1)
                    u = Tally(s_ln, b * 10)
                    u.inc(v.tensor_tensor(bdm[:, :], bst[:, :, 1], bst[:, :, 4], ALU.subtract))
                    u.inc(v.tensor_tensor(bq[:, :], bst[:, :, 1], bst[:, :, 4], ALU.add))
                    link(v, u, v.tensor_tensor(bve[:, :], bst[:, :, 2], bst[:, :, 5], ALU.add))
                    u.inc(v.tensor_scalar(bmean[:, :], bq[:, :], 0.5, None, ALU.mult))
                    link(v, u, v.tensor_tensor(bdm[:, :], bdm[:, :], bdm[:, :], ALU.mult))
                    link(v, u, v.tensor_scalar(bdm[:, :], bdm[:, :], 0.25, 64 * EPS, ALU.mult, ALU.add))
                    v.scalar_tensor_tensor(bve[:, :], bve[:, :], 1.0 / D, bdm[:, :], ALU.mult, ALU.add).then_inc(e_bv.sem, 1)
                    if key is not Banks.LAST:
                        prepare(b + 1, key)
                    e_by.wait(v, b, 0)
                    link(v, u, v.tensor_tensor(bt[:, :], by[:, :], by[:, :], ALU.mult))
                    link(v, u, v.tensor_tensor(bt[:, :], bt[:, :], bve[:, :], ALU.mult))
                    link(v, u, v.tensor_scalar(bt[:, :], bt[:, :], -0.5, 1.5, ALU.mult, ALU.add))
                    link(v, u, v.tensor_tensor(brs[:, :], bt[:, :], by[:, :], ALU.mult))
                    for c in range(C):
                        v.tensor_scalar(og[:, c, :], og[:, c, :], bmean[:, c:c + 1], brs[:, c:c + 1], ALU.subtract, ALU.mult).then_inc(e_on.sem, 1)
                    for jp in range(4):
                        bank = read(f"W{jp}")
                        xr = g.xres[:, bass.ds(b * TB + 2 * jp, 2), :]
                        v.tensor_tensor(xr, xr, bank[:, :].rearrange("p (j d) -> p j d", j=2), ALU.add).then_inc(e_x.sem, 1)
                        e_x.wait(v, b, jp)
                        banks.released(v, key, f"W{jp}")
                        for j in range(2):
                            v.bn_stats(g.st[:, bass.ds(b * TB + 2 * jp + j, 1), :], g.xres[:, bass.ds(b * TB + 2 * jp + j, 1), :])

                run(v, prepare, batch)


class Globals:
    pass


def hybrid_program(nc, dram, phases=("ssm", "ffn", "gla", "ffn2")):
    with ExitStack() as stack:
        m = Mem(nc, stack, "g_")
        g = Globals()
        g.xres = m.sb("xres", [P, NT, D])
        g.st = m.sb("st", [P, NT, 6])
        g.mean = m.sb("mean", [P, NT])
        g.rstd = m.sb("rstd", [P, NT])
        g.ident = m.sb("ident", [P, P])
        g.gidx = m.sb("gidx", [P, NT], U32)
        g.fe = m.sb("fe", [P, NT])
        g.nk = m.sb("nk", [P, NT])
        dram["slots"] = nc.dram_tensor("slots", (SLOTS, D), F32).ap()
        dram["eout"] = nc.dram_tensor("eout", (E * CAP, D), F32).ap()
        s_x = [m.sem(f"s_x{b}") for b in range(B)]
        s_ident, s_z, s_fill = m.sem("s_ident"), m.sem("s_z"), m.sem("s_fill")
        m.start()
        last = phases[-1]

        def is_last(phase):
            return dram["out"] if phase == last else None

        start_loads(nc, g, dram, s_x, s_ident)
        with nc.sbuf_tensor("zero", [P, FILL * D], F32) as zero:
            start_fill(nc, dram, zero, s_z, s_fill)
            norm_stats(nc, g, "n1_", s_x, s_ident)
            if "ffn" not in phases:
                until(nc.sync, s_fill, 16 * (SLOTS // P // FILL))
                nc.all_engine_barrier()
            if "ssm" in phases:
                ssm_layer(nc, g, dram)
            if "ffn" in phases:
                moe_layer(nc, g, dram, "f1", s_fill, is_last("ffn"))
        if "gla" in phases:
            norm_stats(nc, g, "n3_", taken="ffn" in phases)
            gla_layer(nc, g, dram)
        if "ffn2" in phases:
            moe_layer(nc, g, dram, "f2", None, is_last("ffn2"), taken="gla" in phases)
        if last in ("ssm", "gla"):
            store(nc, g, dram["out"])


def store(nc, g, out):
    with ExitStack() as stack:
        m = Mem(nc, stack, "st_")
        s_out = m.sem("s_out")
        m.start()
        with nc.Block() as block:
            @block.sync
            def _(sp):
                sp.dma_start(out.rearrange("(i p) d -> p i d", p=P), g.xres[:, :, :]).then_inc(s_out, 16)
                until(sp, s_out, 16)


def constants():
    rep = np.zeros((96, 2 * NS, P), np.float32)
    for n in range(2 * NS):
        for part in range(3):
            rep[32 * part + n, n, :] = 1
    reset = np.ones((P, E, GROUP), np.float32)
    reset[:, :, 0] = 0
    tri = np.triu(np.ones((P, P), np.float32))
    heads = np.zeros((96, H, P), np.float32)
    for h in range(H):
        heads[[h, 32 + h, 64 + h], h, :] = 1
    later = np.where(np.arange(P)[:, None] > np.arange(P)[None, :], np.float32(NEG), np.float32(0))
    bmask = np.zeros((4, 32, 4, 4, HD), np.float32)
    for h in range(4):
        bmask[h, :, :, h, :] = 1
    hmask = (np.arange(P)[:, None] // 32 == np.arange(4)[None, :]).astype(np.float32)
    bits = lambda w: (np.ascontiguousarray(w, np.float32).view(np.uint32) >> 16).astype(np.uint16)
    return {"trif": tri, "onef": np.ones((P, P), np.float32), "identb": bits(np.eye(P)),
            "later": bits(np.tile(later, (1, 4))), "heads": bits(heads.reshape(96, -1)), "bmask": bmask.reshape(P, D), "hmask": hmask,
            "tri": bits(tri), "oneb": bits(np.ones((P, P))), "reset": reset.reshape(P, E * GROUP),
            "jrow": np.tile(np.arange(E, dtype=np.float32), (P, 1)),
            "trash": (E * CAP + np.arange(P, dtype=np.float32))[:, None],
            "ident": np.eye(P, dtype=np.float32), "rep": bits(rep.reshape(96, -1))}


def layout(i):
    a = {k: np.asarray(v) for k, v in i.items()}
    A, L = "L0_attn_a_", "L0_attn_b_"
    tr = lambda w: np.ascontiguousarray(w.T)
    by_chunk = lambda w: np.ascontiguousarray(w.reshape(DC, P).T)
    d = {"x": a[A + "x"].reshape(T, D), "dWT": tr(a[A + "delta_W"]),
         "bcT": np.ascontiguousarray(np.tile(np.concatenate([a[A + "B_W"], a[A + "C_W"]], 0).T, (1, 3))),
         "bcb": np.ascontiguousarray(np.tile(np.concatenate([a[A + "B_b"], a[A + "C_b"]]), 3)[:, None]),
         "delta_b": by_chunk(a[A + "delta_b"]), "dt_bias": by_chunk(a[A + "dt_bias"]), "A_log": a[A + "A_log"],
         "WiT": tr(a[A + "Wi_W"]), "Wi_b": a[A + "Wi_b"][:, None], "WrT": tr(a[A + "Wr_W"]), "h0": tr(a[A + "h0"]),
         "tau": a[A + "tau"][:, None], "selWT": tr(a[A + "sel_W"]), "sel_b": by_chunk(a[A + "sel_b"])}
    F = "L0_ffn_"
    d.update({"Wr": a[F + "Wr"], "W1": a[F + "W1"].reshape(E * D, FF), "W2": a[F + "W2"].reshape(E * FF, D)})
    d.update({"Wqkv": np.concatenate([a[L + "Wq"], a[L + "Wk"], a[L + "Wv"]], 0).T.copy(),
              "Wgf": tr(np.concatenate([a[L + "Wg1"], np.zeros((16, D), np.float32), a[L + "Wf"]], 0)), "Wg2T": tr(a[L + "Wg2"]), "WoT": tr(a[L + "Wo"]), "ln_w": by_chunk(a[L + "ln_w"])})
    d.update(constants())
    return d


PHASES = ("ssm", "ffn", "gla", "ffn2")


def kernel(**inputs):
    import concourse.bacc as bacc
    from concourse.bass_utils import run_bass_kernel_spmd

    nc = bacc.Bacc("TRN2", target_bir_lowering=False, num_devices=1)
    arrays, dram = {}, {}
    for name, a in layout(inputs).items():
        arrays[f"in_{name}"] = a
        dram[name] = nc.dram_tensor(f"in_{name}", a.shape, mybir.dt.from_np(a.dtype), kind="ExternalInput").ap()
    dram["out"] = nc.dram_tensor("out_x", (T, D), F32, kind="ExternalOutput").ap()
    hybrid_program(nc, dram, PHASES)
    r = run_bass_kernel_spmd(nc, [arrays], core_ids=[0])
    return r.results[0]["out_x"].reshape(B, S, D)
```
